# Optimizing a Trainium2 kernel written in Bass

```python
import numpy as np
import jax
import jax.numpy as jnp

def _softmax(x, axis=-1):
    return jax.nn.softmax(x, axis=axis)

def _gelu(x):
    return jax.nn.gelu(x, approximate=True)

def _silu(x):
    return jax.nn.silu(x)

def _sigmoid(x):
    return jax.nn.sigmoid(x)

def _layernorm(x, axis=-1, eps=1e-05):
    m = jnp.mean(x, axis=axis, keepdims=True)
    v = jnp.var(x, axis=axis, keepdims=True)
    return (x - m) / jnp.sqrt(v + eps)

def _scatter_add(tgt, idx, src, axis=0):
    return tgt.at[idx].add(src)

def _segment_sum(src, seg, n):
    return jax.ops.segment_sum(src, seg, n)
kernel_name = 'mk_flamingo_gated_d2_seqx_r8_f2ac7b'

def setup_inputs(seed: int=0):
    np.random.seed(seed)
    _w = jnp.asarray

    def _rec_inputs():
        import jax
        import jax.numpy as jnp
        _rk = jax.random.key(seed)
        x = 0.0002417 + 0.9998 * jax.random.normal(jax.random.fold_in(_rk, 1), (64, 128, 128), jnp.float32)
        _lenS = 128 - jax.random.randint(jax.random.fold_in(_rk, 7), (64,), 0, max(1, 128 // 4) + 1, jnp.int32)
        _lenS2 = 77 - jax.random.randint(jax.random.fold_in(_rk, 8), (64,), 0, max(1, 77 // 4) + 1, jnp.int32)
        _ctx_1024P = jax.random.normal(jax.random.fold_in(_rk, 11), (64, 16, 128), jnp.float32)
        _ctx_1024c = jax.random.dirichlet(jax.random.fold_in(_rk, 511), 0.3 * jnp.ones((16,), jnp.float32), (64, 77))
        _ctx_1024t = jnp.einsum('bsk,bkd->bsd', _ctx_1024c, _ctx_1024P)
        _ctx_1024t = _ctx_1024t * jax.lax.rsqrt(jnp.mean(jnp.square(_ctx_1024t)) + 1e-12) * 0.953939
        ctx_1024 = 7.22013e-05 + 1.00017 * (_ctx_1024t + 0.3 * jax.random.normal(jax.random.fold_in(_rk, 611), (64, 77, 128), jnp.float32))
        _g = jax.random.normal(jax.random.fold_in(_rk, 9001), (2, 2), jnp.float32)
        _g = jnp.sign(_g) * jnp.maximum(jnp.abs(_g), 1.0) + (_g == 0) * 1.0
        g_xattn = _g[0]
        g_ffn = _g[1]
        return (x, ctx_1024, g_xattn, g_ffn)
    x, ctx_1024, g_xattn, g_ffn = _rec_inputs()

    def _L0_xattn_setup():
        import jax, jax.numpy as jnp
        import numpy as np
        EMBED = 128
        HEADS = 16
        HEAD_DIM = EMBED // HEADS
        EXP_DIM = 2 * HEAD_DIM

        def _feature_map(x, fm_w, fm_b):
            z = jnp.einsum('nshd,ed->nshe', x, fm_w) + fm_b
            return jnp.concatenate([jnp.exp(z), jnp.exp(-z)], axis=-1)
        key = jax.random.key(seed)
        ks = jax.random.split(key, 7)
        N, S = (4, 256)
        values = jax.random.normal(ks[0], (N, S, EMBED), dtype=jnp.float32)
        keys_ = jax.random.normal(ks[1], (N, S, EMBED), dtype=jnp.float32)
        query = jax.random.normal(ks[2], (N, S, EMBED), dtype=jnp.float32)
        fm_w = jnp.eye(HEAD_DIM, dtype=jnp.float32) + 0.02 * jax.random.normal(ks[3], (HEAD_DIM, HEAD_DIM), dtype=jnp.float32)
        fm_b = 0.02 * jax.random.normal(ks[4], (HEAD_DIM,), dtype=jnp.float32)
        fc_w = jax.random.normal(ks[5], (EMBED, HEADS * EXP_DIM), dtype=jnp.float32) * (1.0 / np.sqrt(HEADS * EXP_DIM))
        fc_b = jnp.zeros((EMBED,), dtype=jnp.float32)
        return {'values': values, 'keys': keys_, 'query': query, 'fm_w': fm_w, 'fm_b': fm_b, 'fc_w': fc_w, 'fc_b': fc_b}
    _L0_xattn_all = _L0_xattn_setup()
    _L0_xattn_in = {k: v for k, v in _L0_xattn_all.items() if k in ('fm_w', 'fm_b', 'fc_w', 'fc_b')}
    del _L0_xattn_all

    def _L0_ffn_setup():
        import jax, jax.numpy as jnp
        import numpy as np
        B, S, H, E, I, MAX_K, A_HID = (2, 256, 128, 8, 336, 6, 50)
        key = jax.random.key(seed)
        ks = jax.random.split(key, 10)
        sc = 0.02
        return {'hidden_states': jax.random.normal(ks[0], (B, S, H), dtype=jnp.float32), 'router_w': jax.random.normal(ks[1], (E, H), dtype=jnp.float32) * sc, 'actor_w1': jax.random.normal(ks[2], (A_HID, H), dtype=jnp.float32) * sc, 'actor_b1': jnp.zeros((A_HID,), dtype=jnp.float32), 'actor_w2': jax.random.normal(ks[3], (MAX_K, A_HID), dtype=jnp.float32) * sc, 'actor_b2': jnp.zeros((MAX_K,), dtype=jnp.float32), 'gate_w': jax.random.normal(ks[4], (E, I, H), dtype=jnp.float32) * sc, 'up_w': jax.random.normal(ks[5], (E, I, H), dtype=jnp.float32) * sc, 'down_w': jax.random.normal(ks[6], (E, H, I), dtype=jnp.float32) * sc}
    _L0_ffn_all = _L0_ffn_setup()
    _L0_ffn_in = {k: v for k, v in _L0_ffn_all.items() if k in ('router_w', 'actor_w1', 'actor_b1', 'actor_w2', 'actor_b2', 'gate_w', 'up_w', 'down_w')}
    del _L0_ffn_all

    def _L1_xattn_setup():
        import jax, jax.numpy as jnp
        import numpy as np
        NUM_HEADS = 16
        MAX_REL = 128

        def _relative_ids(q_len, k_len, max_rel):
            rel = jnp.arange(q_len)[:, None] - jnp.arange(k_len)[None, :]
            return jnp.clip(rel, -max_rel, max_rel) + max_rel
        key = jax.random.key(seed)
        ks = jax.random.split(key, 13)
        B, S, H = (2, 256, 128)
        hd = H // NUM_HEADS
        s = 1.0 / np.sqrt(H)
        inp = {'query': jax.random.normal(ks[0], (B, S, H), jnp.float32), 'key': jax.random.normal(ks[1], (B, S, H), jnp.float32), 'value': jax.random.normal(ks[2], (B, S, H), jnp.float32), 'Wq': jax.random.normal(ks[3], (H, H), jnp.float32) * s, 'bq': jnp.zeros((H,), jnp.float32), 'Wk': jax.random.normal(ks[4], (H, H), jnp.float32) * s, 'bk': jnp.zeros((H,), jnp.float32), 'Wv': jax.random.normal(ks[5], (H, H), jnp.float32) * s, 'bv': jnp.zeros((H,), jnp.float32), 'Wo': jax.random.normal(ks[6], (H, H), jnp.float32) * s, 'bo': jnp.zeros((H,), jnp.float32), 'rel_key_table': jax.random.normal(ks[7], (2 * MAX_REL + 1, hd), jnp.float32), 'rel_value_table': jax.random.normal(ks[8], (2 * MAX_REL + 1, hd), jnp.float32)}
        return inp
    _L1_xattn_all = _L1_xattn_setup()
    _L1_xattn_in = {k: v for k, v in _L1_xattn_all.items() if k in ('Wq', 'bq', 'Wk', 'bk', 'Wv', 'bv', 'Wo', 'bo', 'rel_key_table', 'rel_value_table')}
    del _L1_xattn_all

    def _L1_ffn_setup():
        import jax, jax.numpy as jnp
        import numpy as np
        TOP_K = 2
        key = jax.random.key(seed)
        kx, kg, k1, k2 = jax.random.split(key, 4)
        B, T, D, E, H = (4, 128, 128, 8, 256)
        x = jax.random.normal(kx, (B, T, D), dtype=jnp.float32)
        Wg = jax.random.normal(kg, (D, E), dtype=jnp.float32) * 0.02
        W1 = jax.random.normal(k1, (E, D, H), dtype=jnp.float32) * 0.02
        W2 = jax.random.normal(k2, (E, H, D), dtype=jnp.float32) * 0.02
        return {'x': x, 'Wg': Wg, 'W1': W1, 'W2': W2}
    _L1_ffn_all = _L1_ffn_setup()
    _L1_ffn_in = {k: v for k, v in _L1_ffn_all.items() if k in ('Wg', 'W1', 'W2')}
    del _L1_ffn_all
    return {'x': x, 'ctx_1024': ctx_1024, 'g_xattn': g_xattn, 'g_ffn': g_ffn, 'L0_xattn_fm_w': _L0_xattn_in['fm_w'], 'L0_xattn_fm_b': _L0_xattn_in['fm_b'], 'L0_xattn_fc_w': _L0_xattn_in['fc_w'], 'L0_xattn_fc_b': _L0_xattn_in['fc_b'], 'L0_ffn_router_w': _L0_ffn_in['router_w'], 'L0_ffn_actor_w1': _L0_ffn_in['actor_w1'], 'L0_ffn_actor_b1': _L0_ffn_in['actor_b1'], 'L0_ffn_actor_w2': _L0_ffn_in['actor_w2'], 'L0_ffn_actor_b2': _L0_ffn_in['actor_b2'], 'L0_ffn_gate_w': _L0_ffn_in['gate_w'], 'L0_ffn_up_w': _L0_ffn_in['up_w'], 'L0_ffn_down_w': _L0_ffn_in['down_w'], 'L1_xattn_Wq': _L1_xattn_in['Wq'], 'L1_xattn_bq': _L1_xattn_in['bq'], 'L1_xattn_Wk': _L1_xattn_in['Wk'], 'L1_xattn_bk': _L1_xattn_in['bk'], 'L1_xattn_Wv': _L1_xattn_in['Wv'], 'L1_xattn_bv': _L1_xattn_in['bv'], 'L1_xattn_Wo': _L1_xattn_in['Wo'], 'L1_xattn_bo': _L1_xattn_in['bo'], 'L1_xattn_rel_key_table': _L1_xattn_in['rel_key_table'], 'L1_xattn_rel_value_table': _L1_xattn_in['rel_value_table'], 'L1_ffn_Wg': _L1_ffn_in['Wg'], 'L1_ffn_W1': _L1_ffn_in['W1'], 'L1_ffn_W2': _L1_ffn_in['W2']}

def reference(x, ctx_1024, g_xattn, g_ffn, L0_xattn_fm_w, L0_xattn_fm_b, L0_xattn_fc_w, L0_xattn_fc_b, L0_ffn_router_w, L0_ffn_actor_w1, L0_ffn_actor_b1, L0_ffn_actor_w2, L0_ffn_actor_b2, L0_ffn_gate_w, L0_ffn_up_w, L0_ffn_down_w, L1_xattn_Wq, L1_xattn_bq, L1_xattn_Wk, L1_xattn_bk, L1_xattn_Wv, L1_xattn_bv, L1_xattn_Wo, L1_xattn_bo, L1_xattn_rel_key_table, L1_xattn_rel_value_table, L1_ffn_Wg, L1_ffn_W1, L1_ffn_W2):
    import jax
    import jax.numpy as jnp

    def _L0_xattn_ref(values, keys, query, fm_w, fm_b, fc_w, fc_b):
        import jax, jax.numpy as jnp
        import numpy as np
        EMBED = 128
        HEADS = 16
        HEAD_DIM = EMBED // HEADS
        EXP_DIM = 2 * HEAD_DIM

        def _feature_map(x, fm_w, fm_b):
            z = jnp.einsum('nshd,ed->nshe', x, fm_w) + fm_b
            return jnp.concatenate([jnp.exp(z), jnp.exp(-z)], axis=-1)
        N, S, _ = query.shape
        v = values.reshape(N, -1, HEADS, HEAD_DIM)
        k = keys.reshape(N, -1, HEADS, HEAD_DIM)
        q = query.reshape(N, -1, HEADS, HEAD_DIM)
        v, k, q = (_feature_map(x, fm_w, fm_b) for x in (v, k, q))
        scores = jnp.einsum('nqhd,nkhd->nhqk', q, k) / jnp.sqrt(jnp.float32(EMBED))
        attn = jax.nn.softmax(scores, axis=-1)
        out = jnp.einsum('nhql,nlhd->nqhd', attn, v)
        out = out.reshape(N, S, HEADS * EXP_DIM)
        return out @ fc_w.T + fc_b

    def _L0_ffn_ref(hidden_states, router_w, actor_w1, actor_b1, actor_w2, actor_b2, gate_w, up_w, down_w):
        import jax, jax.numpy as jnp
        import numpy as np
        B, S, H, E, I, MAX_K, A_HID = (2, 256, 128, 8, 336, 6, 50)
        probs = jax.nn.softmax(jnp.einsum('bsh,eh->bse', hidden_states, router_w).astype(jnp.float32), axis=-1)
        a_h = jax.nn.gelu(jnp.einsum('bsh,ah->bsa', hidden_states, actor_w1) + actor_b1)
        actor_logits = jnp.clip(jnp.einsum('bsa,ka->bsk', a_h, actor_w2) + actor_b2, -30.0, 30.0)
        sampled_k = jnp.argmax(actor_logits, axis=-1) + 1
        order = jnp.argsort(-probs, axis=-1)
        rank = jnp.argsort(order, axis=-1)
        mask = rank < sampled_k[..., None]
        scores = jnp.where(mask, probs, 0.0).astype(hidden_states.dtype)
        out = jnp.zeros_like(hidden_states)
        for e in range(E):
            g = jnp.einsum('bsh,ih->bsi', hidden_states, gate_w[e])
            u = jnp.einsum('bsh,ih->bsi', hidden_states, up_w[e])
            y = jnp.einsum('bsi,hi->bsh', jax.nn.silu(g) * u, down_w[e])
            out = out + scores[..., e:e + 1] * y
        return out

    def _L1_xattn_ref(query, key, value, Wq, bq, Wk, bk, Wv, bv, Wo, bo, rel_key_table, rel_value_table):
        import jax, jax.numpy as jnp
        import numpy as np
        NUM_HEADS = 16
        MAX_REL = 128

        def _relative_ids(q_len, k_len, max_rel):
            rel = jnp.arange(q_len)[:, None] - jnp.arange(k_len)[None, :]
            return jnp.clip(rel, -max_rel, max_rel) + max_rel
        B, Sq, H = query.shape
        Sk = key.shape[1]
        nh = NUM_HEADS
        hd = H // nh
        q = (query @ Wq + bq).reshape(B, Sq, nh, hd).transpose(0, 2, 1, 3)
        k = (key @ Wk + bk).reshape(B, Sk, nh, hd).transpose(0, 2, 1, 3)
        v = (value @ Wv + bv).reshape(B, Sk, nh, hd).transpose(0, 2, 1, 3)
        scores = jnp.einsum('bhqd,bhkd->bhqk', q, k)
        ids = _relative_ids(Sq, Sk, MAX_REL)
        rel_k = rel_key_table[ids]
        scores = scores + jnp.einsum('bhqd,qkd->bhqk', q, rel_k)
        scores = scores / jnp.sqrt(jnp.asarray(hd, scores.dtype))
        attn = jax.nn.softmax(scores, axis=-1)
        out = jnp.einsum('bhqk,bhkd->bhqd', attn, v)
        rel_v = rel_value_table[ids]
        out = out + jnp.einsum('bhqk,qkd->bhqd', attn, rel_v)
        out = out.transpose(0, 2, 1, 3).reshape(B, Sq, H)
        return out @ Wo + bo

    def _L1_ffn_ref(x, Wg, W1, W2):
        import jax, jax.numpy as jnp
        import numpy as np
        TOP_K = 2
        B, T, D = x.shape
        E = W1.shape[0]
        logits = jnp.einsum('btd,de->bte', x, Wg)
        probs = jax.nn.softmax(logits, axis=-1)
        top_w, top_i = jax.lax.top_k(probs, TOP_K)
        top_w = top_w / (jnp.sum(top_w, axis=-1, keepdims=True) + 1e-08)
        N = B * T
        oh = jax.nn.one_hot(top_i.reshape(N, TOP_K), E, dtype=x.dtype)
        combine = jnp.sum(oh * top_w.reshape(N, TOP_K)[..., None], axis=1)
        xt = x.reshape(N, D)
        h = jnp.einsum('td,edh->teh', xt, W1)
        h = jnp.square(jax.nn.relu(h))
        y = jnp.einsum('teh,ehd->ted', h, W2)
        out = jnp.einsum('te,ted->td', combine, y)
        return out.reshape(B, T, D)
    x = x + jnp.tanh(g_xattn[0]) * _L0_xattn_ref(ctx_1024, ctx_1024, _layernorm(x, axis=-1), L0_xattn_fm_w, L0_xattn_fm_b, L0_xattn_fc_w, L0_xattn_fc_b)
    x = x + jnp.tanh(g_ffn[0]) * _L0_ffn_ref(_layernorm(x, axis=-1), L0_ffn_router_w, L0_ffn_actor_w1, L0_ffn_actor_b1, L0_ffn_actor_w2, L0_ffn_actor_b2, L0_ffn_gate_w, L0_ffn_up_w, L0_ffn_down_w)
    x = x + jnp.tanh(g_xattn[1]) * _L1_xattn_ref(_layernorm(x, axis=-1), ctx_1024, ctx_1024, L1_xattn_Wq, L1_xattn_bq, L1_xattn_Wk, L1_xattn_bk, L1_xattn_Wv, L1_xattn_bv, L1_xattn_Wo, L1_xattn_bo, L1_xattn_rel_key_table, L1_xattn_rel_value_table)
    x = x + jnp.tanh(g_ffn[1]) * _L1_ffn_ref(_layernorm(x, axis=-1), L1_ffn_Wg, L1_ffn_W1, L1_ffn_W2)
    return x

_drawn_inputs = setup_inputs


def setup_inputs(seed=0):
    import zlib

    import numpy as np

    out = dict(_drawn_inputs(seed))
    spreads = {'g_ffn': (-1.0, 0.6),
     'L0_xattn_fc_b': (0.0, 0.8),
     'L0_ffn_actor_b1': (0.0, 0.8),
     'L0_ffn_actor_b2': (0.0, 0.8),
     'L1_xattn_bq': (0.0, 0.8),
     'L1_xattn_bk': (0.0, 0.8),
     'L1_xattn_bv': (0.0, 0.714),
     'L1_xattn_bo': (0.0, 0.691)}
    factors = {'L0_ffn_router_w': 8.0,
     'L0_ffn_actor_w1': 8.0,
     'L0_ffn_actor_w2': 8.0,
     'L0_ffn_gate_w': 8.0,
     'L0_ffn_up_w': 8.0,
     'L0_ffn_down_w': 8.0,
     'L1_ffn_Wg': 8.0,
     'L1_ffn_W1': 8.0,
     'L1_ffn_W2': 8.0}
    for name, (base, spread) in spreads.items():
        noise = np.random.default_rng([zlib.crc32(name.encode()), seed]).standard_normal(out[name].shape)
        drawn = base * np.exp(spread * noise) if base else spread * noise
        out[name] = jnp.asarray(drawn.astype(out[name].dtype))
    for name, factor in factors.items():
        out[name] = (out[name] * factor).astype(out[name].dtype)
    return out
```

```python
from contextlib import ExitStack

import concourse.bass as bass
from concourse import mybir

F32 = mybir.dt.float32
F16 = mybir.dt.float16
ALU = mybir.AluOpType
ACT = mybir.ActivationFunctionType
AX_X = mybir.AxisListType.X

P = 128
D = 128
KC = 77
NH = 16
HD = D // NH
FD = 2 * HD
HQ = 4
QW = HQ * KC
EPS = 1e-5

QC = 8
QG = P // QC
KT = KC + P - QC

NE = 8
GB = 4
GT = GB * P
AH = 50
MAX_K = 6
TOP_K = 2
I0, R0, C0 = 336, 112, 3
I1, R1, C1 = 256, 128, 2
WSCALE = 256.0
RING = 4
LAG = 2


def wait(eng, sem, value):
    if isinstance(value, int) and value <= 0:
        return
    eng.wait_ge(sem, value)


def inside(n, lo, hi):
    return lo <= n < hi if isinstance(n, int) else True


def slots(eng, first, lo, hi, last, body):
    for n in range(first, lo):
        body(n, n % 2)
    with eng.Fori(0, (hi - lo) // 2) as i:
        for r in range(2):
            body(2 * i + (lo + r), (lo + r) % 2)
    for n in range(hi, last):
        body(n, n % 2)


class Program:
    pass


def layernorm_constants(nc, name, stats, mean, rstd, B):
    with ExitStack() as ctx:
        def sb(n, w):
            return ctx.enter_context(nc.sbuf_tensor(f"{name}_{n}", [P, w], F32))

        diff, var, sd, newton = sb("diff", B), sb("var", B), sb("sd", B), sb("newton", B)
        step = ctx.enter_context(nc.semaphore(f"{name}_step"))
        root = ctx.enter_context(nc.semaphore(f"{name}_root"))
        with nc.Block(name=name) as block:
            @block.scalar
            def _(act):
                act.wait_ge(step, 6)
                nc.scalar.activation(sd[:, :], var[:, :], ACT.Sqrt).then_inc(root, 1)

            @block.vector
            def _(dve):
                done = 0

                def link(ins):
                    nonlocal done
                    done += 1
                    ins.then_inc(step, 1)
                    dve.wait_ge(step, done)

                half = [stats[:, :, k] for k in range(6)]
                link(nc.vector.tensor_tensor(mean[:, :], half[1], half[4], ALU.add))
                link(nc.vector.tensor_tensor(diff[:, :], half[1], half[4], ALU.subtract))
                link(nc.vector.tensor_tensor(var[:, :], half[2], half[5], ALU.add))
                link(nc.vector.scalar_tensor_tensor(out=diff[:, :], in0=diff[:, :], scalar=0.25, in1=diff[:, :],
                                                    op0=ALU.mult, op1=ALU.mult))
                link(nc.vector.scalar_tensor_tensor(out=var[:, :], in0=var[:, :], scalar=1.0 / D, in1=diff[:, :],
                                                    op0=ALU.mult, op1=ALU.add))
                link(nc.vector.tensor_scalar(var[:, :], var[:, :], EPS, None, ALU.add))
                link(nc.vector.tensor_scalar(mean[:, :], mean[:, :], 0.5, None, ALU.mult))
                dve.wait_ge(root, 1)
                link(nc.vector.reciprocal(rstd[:, :], sd[:, :]))
                link(nc.vector.tensor_tensor(newton[:, :], rstd[:, :], rstd[:, :], ALU.mult))
                link(nc.vector.tensor_tensor(newton[:, :], newton[:, :], var[:, :], ALU.mult))
                link(nc.vector.tensor_scalar(newton[:, :], newton[:, :], -0.5, 1.5, ALU.mult, ALU.add))
                link(nc.vector.tensor_tensor(rstd[:, :], rstd[:, :], newton[:, :], ALU.mult))


def load_x(nc, B, x, x_all, stats):
    G = 4
    with ExitStack() as ctx:
        loaded = [ctx.enter_context(nc.semaphore(f"x_loaded{g}")) for g in range(G)]
        with nc.Block(name="load") as block:
            @block.sync
            def _(sp):
                for g in range(G):
                    own = slice(g * B // G, (g + 1) * B // G)
                    sp.dma_start(x_all[:, own, :], x[own].rearrange("b q d -> q b d")).then_inc(loaded[g], 16)

            @block.vector
            def _(dve):
                for g in range(G):
                    dve.wait_ge(loaded[g], 16)
                    with dve.Fori(g * B // G, (g + 1) * B // G) as n:
                        nc.vector.bn_stats(stats[:, n, :], x_all[:, n, :])


def feature_attention(nc, B, io, x_all, stats, mean, rstd, ident, gates):
    with ExitStack() as ctx:
        def sb(n, s):
            return ctx.enter_context(nc.sbuf_tensor("a0_" + n, s, F32))

        def ps(n):
            return ctx.enter_context(nc.psum_tensor("a0_" + n, [P, 512], F32))

        def sem(n):
            return ctx.enter_context(nc.semaphore("a0_" + n))

        w_rep, w_sign = sb("w_rep", [P, HD]), sb("w_sign", [P, 2 * 8 * 2])
        fm_w = sb("fm_w", [P, 2, P])
        b_rep, b_sign, fm_b = sb("b_rep", [P, 1]), sb("b_sign", [P, 1]), sb("fm_b", [P, 1])
        head_mask = sb("head_mask", [P, 8])
        fc_w, fc_b = sb("fc_w", [P, 2, D]), sb("fc_b", [P, D])
        xn = [sb(f"xn{p}", [P, D]) for p in range(2)]
        xc = [sb(f"xc{p}", [P, P + KC]) for p in range(2)]
        feat = [sb(f"feat{p}", [P, 2, P + KC]) for p in range(2)]
        kfeat = [sb(f"kfeat{p}", [P, 2, 8, KC]) for p in range(2)]
        vfeat = [sb(f"vfeat{p}", [KC, NH, FD + 1]) for p in range(2)]
        mixed = [sb(f"mixed{p}", [P, NH, FD]) for p in range(2)]
        mixed_t = [sb(f"mixed_t{p}", [P, 2, P]) for p in range(2)]
        top = [sb(f"top{k}", [P, HQ]) for k in range(4)]
        prob = [sb(f"prob{k}", [P, HQ, KC]) for k in range(4)]
        prob_t = [sb(f"prob_t{k}", [KC, HQ, P]) for k in range(4)]
        rden = [sb(f"rden{p}", [P, NH]) for p in range(2)]

        score_ps = [ps(f"score{k}") for k in range(2)]
        trans_ps = [ps(f"trans{k}") for k in range(2)]
        mix_ps = [ps(f"mix{p}") for p in range(2)]
        prep_ps, fin_ps = ps("prep"), ps("fin")

        weights_in, ctx_in = sem("weights_in"), [sem(f"ctx_in{p}") for p in range(2)]
        weights_ready = sem("weights_ready")
        xn_ready, xn_t, xn_copied = sem("xn_ready"), sem("xn_t"), sem("xn_copied")
        z_ready, feat_ready, kfeat_ready = sem("z_ready"), sem("feat_ready"), sem("kfeat_ready")
        value_t, value_copied = sem("value_t"), sem("value_copied")
        score_ready, top_ready, shifted, exped = sem("score_ready"), sem("top_ready"), sem("shifted"), sem("exped")
        prob_ready, prob_copied = sem("prob_ready"), sem("prob_copied")
        mix_ready, rden_ready, mixed_ready = sem("mix_ready"), sem("rden_ready"), sem("mixed_ready")
        mixed_turned, mixed_copied = sem("mixed_turned"), sem("mixed_copied")
        y_ready, x_biased, x_ready = sem("y_ready"), sem("x_biased"), sem("x_ready")
        stats_ready = sem("stats_ready")

        LO, HI, LAST = 4, B - 2, B + 2
        WEIGHTS = [(w_rep, io["fm_w"]), (w_sign, io["fm_sign"]), (b_rep, io["fm_b"]), (b_sign, io["row_sign"]),
                   (head_mask, io["head_mask"]), (fc_b, io["fc_b"])]

        with nc.Block(name="a0") as block:
            @block.sync
            def _(sp):
                for t, src in WEIGHTS:
                    sp.dma_start(t[:, :], src).then_inc(weights_in, 16)
                sp.dma_start(fc_w[:, :, :], io["fc_w"]).then_inc(weights_in, 16)

                def slot(n, p):
                    if inside(n, 0, B):
                        wait(sp, z_ready, n - 1)
                        sp.dma_start(xc[p][:, P:P + KC], io["ctx"][n]).then_inc(ctx_in[p], 16)

                slots(sp, 0, LO, HI, B, slot)

            @block.tensor
            def _(pe):
                def prep_turn(n, p):
                    if inside(n, 0, B):
                        wait(pe, xn_ready, n + 1)
                        wait(pe, value_copied, n)
                        nc.tensor.transpose(prep_ps[:, 0:P], xn[p][:, :], ident[:, :]).then_inc(xn_t, 1)

                def prep_z(n, p):
                    if inside(n, 0, B):
                        wait(pe, xn_copied, n + 1)
                        wait(pe, ctx_in[p], (n - p) * 8 + 16)
                        if isinstance(n, int) and n == 0:
                            pe.wait_ge(weights_ready, 4)
                        for c in range(2):
                            mm = nc.tensor.matmul(prep_ps[:, 256 * c:256 * c + P + KC], fm_w[:, c, :], xc[p][:, :],
                                                  start=True, stop=True)
                        mm.then_inc(z_ready, 1)

                def prep_value(n, p):
                    if inside(n, 0, B):
                        wait(pe, feat_ready, n + 1)
                        for c in range(2):
                            mm = nc.tensor.transpose(prep_ps[0:KC, P * c:P * (c + 1)], feat[p][:, c, P:P + KC],
                                                     ident[:, :])
                        mm.then_inc(value_t, 1)

                def scores(n, p, u):
                    if inside(n, 0, B):
                        if u % 2 == 0:
                            wait(pe, kfeat_ready, 2 * n + u // 2 + 1)
                        wait(pe, shifted, 4 * n + u - 1)
                        c = u // 2
                        nc.tensor.matmul(score_ps[u % 2][:, 0:QW], feat[p][:, c, 0:P],
                                         kfeat[p][:, c, 4 * (u % 2):4 * (u % 2) + 4, :],
                                         start=True, stop=True).then_inc(score_ready, 1)

                def turn(n, u):
                    if inside(n, 0, B):
                        wait(pe, exped, 4 * n + u + 1)
                        wait(pe, prob_copied, 4 * n + u - 1)
                        for h in range(HQ):
                            mm = nc.tensor.transpose(trans_ps[u % 2][0:KC, P * h:P * (h + 1)], prob[u][:, h, :],
                                                     ident[:, :])
                        mm.then_inc(prob_ready, 1)

                def mix(n, p, u):
                    if inside(n, 0, B):
                        wait(pe, prob_copied, 4 * n + u + 1)
                        if u == 0:
                            wait(pe, value_copied, n + 1)
                            wait(pe, mixed_ready, n - 1)
                        for h in range(HQ):
                            head = 4 * u + h
                            mm = nc.tensor.matmul(mix_ps[p][:, head * (FD + 1):(head + 1) * (FD + 1)],
                                                  prob_t[u][:, h, :], vfeat[p][:, head, :], start=True, stop=True)
                        if u == 3:
                            mm.then_inc(mix_ready, 1)

                def fin_turn(n, p):
                    if inside(n, 0, B):
                        wait(pe, mixed_ready, n + 1)
                        wait(pe, x_ready, n)
                        flat = mixed[p][:, :, :].rearrange("q h f -> q (h f)")
                        for c in range(2):
                            mm = nc.tensor.transpose(fin_ps[:, P * c:P * (c + 1)], flat[:, P * c:P * (c + 1)],
                                                     ident[:, :])
                        mm.then_inc(mixed_turned, 1)

                def fin_project(n, p):
                    if inside(n, 0, B):
                        wait(pe, mixed_copied, n + 1)
                        for c in range(2):
                            mm = nc.tensor.matmul(fin_ps[:, 0:D], mixed_t[p][:, c, :], fc_w[:, c, :],
                                                  start=(c == 0), stop=(c == 1))
                        mm.then_inc(y_ready, 1)

                def slot(n, p):
                    o = 1 - p
                    scores(n, p, 0)
                    turn(n - 1, 2)
                    mix(n - 1, o, 1)
                    fin_project(n - 2, p)
                    prep_turn(n + 1, o)
                    scores(n, p, 1)
                    turn(n - 1, 3)
                    mix(n - 1, o, 2)
                    prep_z(n + 1, o)
                    scores(n, p, 2)
                    turn(n, 0)
                    mix(n - 1, o, 3)
                    prep_value(n + 1, o)
                    scores(n, p, 3)
                    turn(n, 1)
                    mix(n, p, 0)
                    fin_turn(n - 1, o)

                slots(pe, -1, LO, HI, LAST, slot)

            @block.scalar
            def _(act):
                def copy_xn(n, p):
                    if inside(n, 0, B):
                        wait(act, xn_t, n + 1)
                        wait(act, z_ready, n - 1)
                        nc.scalar.activation(xc[p][:, 0:P], prep_ps[:, 0:P], ACT.Copy).then_inc(xn_copied, 1)

                def features(n, p):
                    if inside(n, 0, B):
                        wait(act, z_ready, n + 1)
                        z = prep_ps[:, :].rearrange("r (c t) -> r c t", c=2)[:, :, 0:P + KC]
                        nc.scalar.activation(feat[p][:, :, :], z, ACT.Exp, bias=fm_b[:, 0:1]).then_inc(feat_ready, 1)

                def copy_value(n, p):
                    if inside(n, 0, B):
                        wait(act, value_t, n + 1)
                        v = prep_ps[0:KC, 0:NH * FD].rearrange("k (h f) -> k h f", h=NH)
                        nc.scalar.activation(vfeat[p][:, :, 0:FD], v, ACT.Copy).then_inc(value_copied, 1)

                def exp(n, u):
                    if inside(n, 0, B):
                        wait(act, shifted, 4 * n + u + 1)
                        nc.scalar.activation(prob[u][:, :, :], prob[u][:, :, :], ACT.Exp,
                                             scale=float(D) ** -0.5).then_inc(exped, 1)

                def copy_prob(n, u):
                    if inside(n, 0, B):
                        wait(act, prob_ready, 4 * n + u + 1)
                        nc.scalar.activation(prob_t[u][:, :, :],
                                             trans_ps[u % 2][0:KC, :].rearrange("k (h q) -> k h q", h=HQ),
                                             ACT.Copy).then_inc(prob_copied, 1)

                def copy_mixed(n, p):
                    if inside(n, 0, B):
                        wait(act, mixed_turned, n + 1)
                        nc.scalar.activation(mixed_t[p][:, :, :],
                                             fin_ps[:, 0:2 * P].rearrange("f (c q) -> f c q", c=2),
                                             ACT.Copy).then_inc(mixed_copied, 1)

                def slot(n, p):
                    o = 1 - p
                    copy_prob(n - 1, 2)
                    copy_xn(n + 1, o)
                    exp(n, 0)
                    copy_prob(n - 1, 3)
                    features(n + 1, o)
                    exp(n, 1)
                    copy_prob(n, 0)
                    copy_value(n + 1, o)
                    exp(n, 2)
                    copy_prob(n, 1)
                    copy_mixed(n - 1, o)
                    exp(n, 3)

                act.wait_ge(weights_ready, 4)
                slots(act, -1, LO, HI, LAST, slot)

            @block.gpsimd
            def _(pool):
                for p in range(2):
                    nc.gpsimd.memset(vfeat[p][:, :, FD:FD + 1], 1.0)

                def slot(n, p):
                    if inside(n, 0, B):
                        wait(pool, feat_ready, n + 1)
                        wait(pool, score_ready, 4 * n - 4)
                        for c in range(2):
                            nc.gpsimd.tensor_tensor(
                                kfeat[p][:, c, :, :], feat[p][:, c, P:P + KC].unsqueeze(1).broadcast_to([P, 8, KC]),
                                head_mask[:, :].unsqueeze(2).broadcast_to([P, 8, KC]), ALU.mult).then_inc(kfeat_ready, 1)
                        nc.gpsimd.tensor_tensor(x_all[:, n, :], x_all[:, n, :], fc_b[:, :],
                                                ALU.add).then_inc(x_biased, 1)

                pool.wait_ge(weights_ready, 4)
                slots(pool, 0, LO, HI, B, slot)

            @block.vector
            def _(dve):
                dve.wait_ge(weights_in, 16 * (len(WEIGHTS) + 1))
                nc.vector.tensor_tensor(
                    fm_w[:, :, :].rearrange("r c (g e) -> r (c g) e", e=HD),
                    w_rep[:, :].unsqueeze(1).broadcast_to([P, 2 * 8 * 2, HD]),
                    w_sign[:, :].unsqueeze(2).broadcast_to([P, 2 * 8 * 2, HD]), ALU.mult).then_inc(weights_ready, 1)
                nc.vector.tensor_tensor(fm_b[:, :], b_rep[:, :], b_sign[:, :], ALU.mult).then_inc(weights_ready, 1)
                nc.vector.tensor_scalar(fc_w[:, :, :], fc_w[:, :, :], gates[:, 0:1], None,
                                        ALU.mult).then_inc(weights_ready, 1)
                nc.vector.tensor_scalar(fc_b[:, :], fc_b[:, :], gates[:, 0:1], None,
                                        ALU.mult).then_inc(weights_ready, 1)

                def normalize(n, p):
                    if inside(n, 0, B):
                        wait(dve, xn_t, n - 1)
                        nc.vector.tensor_scalar(xn[p][:, :], x_all[:, n, :], mean[:, n, :], rstd[:, n, :],
                                                ALU.subtract, ALU.mult).then_inc(xn_ready, 1)

                def softmax_shift(n, u):
                    if inside(n, 0, B):
                        s = score_ps[u % 2][:, 0:QW].rearrange("q (h k) -> q h k", h=HQ)
                        wait(dve, score_ready, 4 * n + u + 1)
                        nc.vector.tensor_reduce(top[u][:, :], s, AX_X, ALU.max).then_inc(top_ready, 1)
                        wait(dve, top_ready, 4 * n + u + 1)
                        wait(dve, prob_ready, 4 * n + u - 3)
                        nc.vector.tensor_tensor(prob[u][:, :, :], s, top[u][:, :].unsqueeze(2).broadcast_to([P, HQ, KC]),
                                                ALU.subtract).then_inc(shifted, 1)

                def divide(n, p):
                    if inside(n, 0, B):
                        m = mix_ps[p][:, 0:NH * (FD + 1)].rearrange("q (h f) -> q h f", h=NH)
                        wait(dve, mix_ready, n + 1)
                        nc.vector.reciprocal(rden[p][:, :], m[:, :, FD]).then_inc(rden_ready, 1)
                        wait(dve, rden_ready, n + 1)
                        wait(dve, mixed_turned, n - 1)
                        nc.vector.tensor_tensor(mixed[p][:, :, :], m[:, :, 0:FD],
                                                rden[p][:, :].unsqueeze(2).broadcast_to([P, NH, FD]),
                                                ALU.mult).then_inc(mixed_ready, 1)

                def residual(n):
                    if inside(n, 0, B):
                        wait(dve, y_ready, n + 1)
                        wait(dve, x_biased, n + 1)
                        nc.vector.tensor_tensor(x_all[:, n, :], x_all[:, n, :], fin_ps[:, 0:D],
                                                ALU.add).then_inc(x_ready, 1)

                def statistics(n):
                    if inside(n, 0, B):
                        wait(dve, x_ready, n + 1)
                        nc.vector.bn_stats(stats[:, n, :], x_all[:, n, :]).then_inc(stats_ready, 1)

                def slot(n, p):
                    o = 1 - p
                    softmax_shift(n, 0)
                    residual(n - 2)
                    softmax_shift(n, 1)
                    statistics(n - 2)
                    normalize(n + 2, p)
                    softmax_shift(n, 2)
                    divide(n - 1, o)
                    softmax_shift(n, 3)

                normalize(0, 0)
                normalize(1, 1)
                slots(dve, 0, LO, HI, LAST, slot)


def split_weights(nc, name, weights):
    with ExitStack() as ctx:
        loaded = ctx.enter_context(nc.semaphore(f"{name}_loaded"))
        high_ready = ctx.enter_context(nc.semaphore(f"{name}_high_ready"))
        stage = [ctx.enter_context(nc.sbuf_tensor(f"{name}_stage{k}", list(high.shape), F32))
                 for k, (_, high, _) in enumerate(weights)]
        with nc.Block(name=name) as block:
            @block.sync
            def _(sp):
                for t, (src, _, _) in zip(stage, weights):
                    sp.dma_start(t[:, :, :], src).then_inc(loaded, 16)
                    sp.wait_ge(loaded, 16 * (stage.index(t) + 1))

            @block.scalar
            def _(act):
                for k, (t, (_, high, _)) in enumerate(zip(stage, weights)):
                    act.wait_ge(loaded, 16 * (k + 1))
                    nc.scalar.activation(high[:, :, :], t[:, :, :], ACT.Copy, scale=WSCALE).then_inc(high_ready, 1)

            @block.vector
            def _(dve):
                for k, (t, (_, high, low)) in enumerate(zip(stage, weights)):
                    dve.wait_ge(high_ready, k + 1)
                    flat = [v[:, :, :].rearrange("p a b -> p (a b)") for v in (t, high, low)]
                    nc.vector.scalar_tensor_tensor(out=flat[2], in0=flat[0], scalar=WSCALE, in1=flat[1],
                                                   op0=ALU.mult, op1=ALU.subtract)


def router(nc, name, B, io, x_all, mean, rstd, ident, x_high, x_low, logits, actor=None):
    G = B // GB
    with ExitStack() as ctx:
        def sb(n, s):
            return ctx.enter_context(nc.sbuf_tensor(f"{name}_{n}", s, F32))

        def ps(n):
            return [ctx.enter_context(nc.psum_tensor(f"{name}_{n}{p}", [P, GT], F32)) for p in range(2)]

        def sem(n):
            return ctx.enter_context(nc.semaphore(f"{name}_{n}"))

        w_router = sb("w_router", [P, NE])
        xn = [sb(f"xn{p}", [P, GB, D]) for p in range(2)]
        xt = [sb(f"xt{p}", [P, GT]) for p in range(2)]
        turn_ps, logit_ps = ps("turn_ps"), ps("logit_ps")
        weights_in = sem("weights_in")
        xn_ready, turned, xt_ready = sem("xn_ready"), sem("turned"), sem("xt_ready")
        high_ready, low_ready = sem("high_ready"), sem("low_ready")
        logits_ready, logits_copied = sem("logits_ready"), sem("logits_copied")
        loads = [(w_router, io[name + "_router"])]
        if actor:
            w1, b1 = sb("w1", [P, AH]), sb("b1", [AH, 1])
            w2, b2 = sb("w2", [AH, MAX_K]), sb("b2", [P, MAX_K])
            pre = [sb(f"pre{p}", [AH, GT]) for p in range(2)]
            cube = [sb(f"cube{p}", [AH, GT]) for p in range(2)]
            hidden = [sb(f"hidden{p}", [AH, GT]) for p in range(2)]
            hidden_ps, actor_ps = ps("hidden_ps"), ps("actor_ps")
            loads += [(w1, io["actor_w1"]), (b1, io["actor_b1"]), (w2, io["actor_w2"]), (b2, io["actor_b2"])]
            w2_halved, pre_ps_ready, pre_ready = sem("w2_halved"), sem("pre_ps_ready"), sem("pre_ready")
            square_ready, factor_ready, cube_ready = sem("square_ready"), sem("factor_ready"), sem("cube_ready")
            tanh_ready, hidden_ready = sem("tanh_ready"), sem("hidden_ready")
            actor_ready, actor_copied = sem("actor_ready"), sem("actor_copied")

        with nc.Block(name=name) as block:
            @block.sync
            def _(sp):
                for t, src in loads:
                    sp.dma_start(t[:, :], src).then_inc(weights_in, 16)
                sp.wait_ge(weights_in, 16 * len(loads))

            def groups(eng, body, shift=0):
                slots(eng, 0, 2, G + shift - (G + shift) % 2, G + shift, body)

            @block.vector
            def _(dve):
                dve.wait_ge(weights_in, 16 * len(loads))
                if actor:
                    nc.vector.tensor_scalar(w2[:, :], w2[:, :], 0.5, None, ALU.mult).then_inc(w2_halved, 1)

                def normalize(g, p):
                    wait(dve, turned, g - 1)
                    for t in range(GB):
                        n = GB * g + t
                        last = nc.vector.tensor_scalar(xn[p][:, t, :], x_all[:, n, :], mean[:, n, :], rstd[:, n, :],
                                                       ALU.subtract, ALU.mult)
                    last.then_inc(xn_ready, 1)

                def gelu(g, p):
                    wait(dve, pre_ready, g + 1)
                    wait(dve, tanh_ready, g - 1)
                    nc.vector.tensor_tensor(cube[p][:, :], pre[p][:, :], pre[p][:, :], ALU.mult).then_inc(square_ready, 1)
                    wait(dve, square_ready, g + 1)
                    nc.vector.tensor_scalar(cube[p][:, :], cube[p][:, :], 0.044715, 1.0, ALU.mult,
                                            ALU.add).then_inc(factor_ready, 1)
                    wait(dve, factor_ready, g + 1)
                    nc.vector.tensor_tensor(cube[p][:, :], cube[p][:, :], pre[p][:, :], ALU.mult).then_inc(cube_ready, 1)
                    wait(dve, tanh_ready, g + 1)
                    wait(dve, actor_ready, g - 1)
                    nc.vector.scalar_tensor_tensor(out=hidden[p][:, :], in0=cube[p][:, :], scalar=1.0, in1=pre[p][:, :],
                                                   op0=ALU.add, op1=ALU.mult).then_inc(hidden_ready, 1)

                def group(g, p):
                    normalize(g, p)
                    wait(dve, xt_ready, g + 1)
                    wait(dve, low_ready, g - 1)
                    nc.vector.tensor_copy(x_high[:, g, :], xt[p][:, :]).then_inc(high_ready, 1)
                    if actor:
                        gelu(g, p)
                    wait(dve, logits_ready, g + 1)
                    nc.vector.tensor_copy(logits[:, g, :], logit_ps[p][:, 0:GB * NE]).then_inc(logits_copied, 1)
                    if actor:
                        wait(dve, actor_ready, g + 1)
                        nc.vector.tensor_tensor(
                            actor[:, g, :].rearrange("q (t k) -> q t k", t=GB),
                            actor_ps[p][:, 0:GB * MAX_K].rearrange("q (t k) -> q t k", t=GB),
                            b2[:, :].unsqueeze(1).broadcast_to([P, GB, MAX_K]), ALU.add).then_inc(actor_copied, 1)

                groups(dve, group)

            @block.tensor
            def _(pe):
                pe.wait_ge(weights_in, 16 * len(loads))
                if actor:
                    pe.wait_ge(w2_halved, 1)

                def group(g, p):
                    wait(pe, xn_ready, g + 1)
                    wait(pe, xt_ready, g - 1)
                    for t in range(GB):
                        mm = nc.tensor.transpose(turn_ps[p][:, P * t:P * (t + 1)], xn[p][:, t, :], ident[:, :])
                    mm.then_inc(turned, 1)
                    wait(pe, xt_ready, g + 1)
                    if actor:
                        wait(pe, pre_ready, g - 1)
                        nc.tensor.matmul(hidden_ps[p][0:AH, :], w1[:, :], xt[p][:, :],
                                         start=True, stop=True).then_inc(pre_ps_ready, 1)
                    wait(pe, logits_copied, g - 1)
                    for t in range(GB):
                        mm = nc.tensor.matmul(logit_ps[p][:, NE * t:NE * (t + 1)], xt[p][:, P * t:P * (t + 1)],
                                              w_router[:, :], start=True, stop=True)
                    mm.then_inc(logits_ready, 1)
                    if actor:
                        wait(pe, hidden_ready, g + 1)
                        wait(pe, actor_copied, g - 1)
                        for t in range(GB):
                            mm = nc.tensor.matmul(actor_ps[p][:, MAX_K * t:MAX_K * (t + 1)],
                                                  hidden[p][:, P * t:P * (t + 1)], w2[:, :], start=True, stop=True)
                        mm.then_inc(actor_ready, 1)

                groups(pe, group)

            @block.scalar
            def _(act):
                act.wait_ge(weights_in, 16 * len(loads))

                def group(g, p):
                    wait(act, turned, g + 1)
                    wait(act, low_ready, g - 1)
                    wait(act, logits_ready, g - 1)
                    nc.scalar.activation(xt[p][:, :], turn_ps[p][:, :], ACT.Copy).then_inc(xt_ready, 1)
                    if actor:
                        wait(act, pre_ps_ready, g + 1)
                        wait(act, hidden_ready, g - 1)
                        nc.scalar.activation(pre[p][:, :], hidden_ps[p][0:AH, :], ACT.Identity,
                                             bias=b1[:, 0:1]).then_inc(pre_ready, 1)
                        wait(act, cube_ready, g + 1)
                        nc.scalar.activation(cube[p][:, :], cube[p][:, :], ACT.Tanh,
                                             scale=(2.0 / 3.141592653589793) ** 0.5).then_inc(tanh_ready, 1)

                groups(act, group)

            @block.gpsimd
            def _(pool):
                def group(g, p):
                    wait(pool, high_ready, g + 1)
                    nc.gpsimd.tensor_tensor(x_low[:, g, :], xt[p][:, :], x_high[:, g, :],
                                            ALU.subtract).then_inc(low_ready, 1)

                groups(pool, group)


def expert_scores(nc, name, B, io, logits, actor, scores, gate):
    with ExitStack() as ctx:
        def sb(n, s):
            return ctx.enter_context(nc.sbuf_tensor(f"{name}_{n}", s, F32))

        probs, rank, cmp_ = sb("probs", [P, B, NE]), sb("rank", [P, B, NE]), sb("cmp", [P, B, NE])
        one, total = sb("one", [P, B]), sb("total", [P, B])
        after = sb("after", [P, NE])
        first, allowed, best = sb("first", [P, MAX_K]), sb("allowed", [P, B]), sb("best", [P, B])
        consts_in = ctx.enter_context(nc.semaphore(f"{name}_consts_in"))
        step = ctx.enter_context(nc.semaphore(f"{name}_step"))
        exped = ctx.enter_context(nc.semaphore(f"{name}_exped"))

        def wide(t, n=NE):
            return t[:, :].unsqueeze(2).broadcast_to([P, B, n])

        with nc.Block(name=name) as block:
            @block.sync
            def _(sp):
                sp.dma_start(after[:, :], io["experts_after"]).then_inc(consts_in, 16)
                sp.dma_start(first[:, :], io["first_k"]).then_inc(consts_in, 16)
                sp.wait_ge(consts_in, 32)

            @block.scalar
            def _(act):
                act.wait_ge(step, 2)
                nc.scalar.activation(probs[:, :, :], probs[:, :, :], ACT.Exp).then_inc(exped, 1)

            @block.vector
            def _(dve):
                done = 0

                def link(ins):
                    nonlocal done
                    done += 1
                    ins.then_inc(step, 1)
                    dve.wait_ge(step, done)

                l3 = logits[:, :, :].rearrange("q g (t e) -> q (g t) e", e=NE)
                link(nc.vector.tensor_reduce(one[:, :], l3, AX_X, ALU.max))
                link(nc.vector.tensor_tensor(probs[:, :, :], l3, wide(one), ALU.subtract))
                dve.wait_ge(consts_in, 32)
                if actor is not None:
                    a3 = actor[:, :, :].rearrange("q g (t k) -> q (g t) k", k=MAX_K)
                    link(nc.vector.tensor_scalar(a3, a3, 30.0, -30.0, ALU.min, ALU.max))
                    link(nc.vector.tensor_reduce(best[:, :], a3, AX_X, ALU.max))
                    link(nc.vector.tensor_tensor(a3, a3, wide(best, MAX_K), ALU.is_equal))
                    link(nc.vector.tensor_tensor(a3, a3, first[:, :].unsqueeze(1).broadcast_to([P, B, MAX_K]), ALU.mult))
                    link(nc.vector.tensor_reduce(allowed[:, :], a3, AX_X, ALU.min))
                    link(nc.vector.tensor_scalar(allowed[:, :], allowed[:, :], MAX_K + 1.0, None, ALU.add))
                else:
                    link(nc.vector.memset(allowed[:, :], float(TOP_K)))
                dve.wait_ge(exped, 1)
                link(nc.vector.tensor_reduce(total[:, :], probs[:, :, :], AX_X, ALU.add))
                link(nc.vector.reciprocal(one[:, :], total[:, :]))
                link(nc.vector.tensor_tensor(probs[:, :, :], probs[:, :, :], wide(one), ALU.mult))
                link(nc.vector.tensor_copy(rank[:, :, :], after[:, :].unsqueeze(1).broadcast_to([P, B, NE])))
                for d in range(1, NE):
                    ge, front, back = cmp_[:, :, 0:NE - d], slice(0, NE - d), slice(d, NE)
                    link(nc.vector.tensor_tensor(ge, probs[:, :, front], probs[:, :, back], ALU.is_ge))
                    link(nc.vector.tensor_tensor(rank[:, :, front], rank[:, :, front], ge, ALU.subtract))
                    link(nc.vector.tensor_tensor(rank[:, :, back], rank[:, :, back], ge, ALU.add))
                link(nc.vector.tensor_tensor(rank[:, :, :], rank[:, :, :], wide(allowed), ALU.is_lt))
                link(nc.vector.tensor_tensor(probs[:, :, :], probs[:, :, :], rank[:, :, :], ALU.mult))
                if actor is None:
                    link(nc.vector.tensor_reduce(total[:, :], probs[:, :, :], AX_X, ALU.add))
                    link(nc.vector.tensor_scalar(total[:, :], total[:, :], 1e-8, None, ALU.add))
                    link(nc.vector.reciprocal(one[:, :], total[:, :]))
                    link(nc.vector.tensor_tensor(probs[:, :, :], probs[:, :, :], wide(one), ALU.mult))
                flat = [t[:, :, :].rearrange("q n e -> q (n e)") for t in (scores[:, :, :, 0], probs)]
                link(nc.vector.tensor_scalar(flat[0], flat[1], gate, 1.0 / WSCALE, ALU.mult, ALU.mult))


def experts(nc, name, B, x_high, x_low, x_all, scores, w_in, w_down, rows, per, out=None, stats=None):
    G, M = B // GB, NE * per
    with ExitStack() as ctx:
        def sb(n, s, d=F32):
            return [ctx.enter_context(nc.sbuf_tensor(f"{name}_{n}{k}", s, d)) for k in range(RING)]

        def ps(n, k):
            return [ctx.enter_context(nc.psum_tensor(f"{name}_{n}{p}", [P, GT], F32)) for p in range(k)]

        def sem(n):
            return ctx.enter_context(nc.semaphore(f"{name}_{n}"))

        act_out, hidden = sb("act_out", [rows, GT]), sb("hidden", [rows, GT])
        high, low = sb("high", [rows, GT], F16), sb("low", [rows, GT], F16)
        in_ps = [ps(f"in{k}_", 2) for k in range(len(w_in))]
        y_ps = ps("y", 2)
        in_ready, act_ready, hidden_ready = sem("in_ready"), sem("act_ready"), sem("hidden_ready")
        high_ready, low_ready, down_done = sem("high_ready"), sem("low_ready"), sem("down_done")
        x_ready, x_stored, stats_ready = sem("x_ready"), sem("x_stored"), sem("stats_ready")
        gated = len(w_in) == 2

        def groups(eng, body):
            body(0)
            with eng.Fori(1, G) as g:
                body(g)

        with nc.Block(name=name) as block:
            @block.tensor
            def _(pe):
                def project(g, m):
                    for k, (wh, wl) in enumerate(w_in):
                        if k == 0:
                            wait(pe, hidden_ready, M * g + m - 1)
                        dst, own = in_ps[k][m % 2][0:rows, :], slice(rows * m, rows * (m + 1))
                        nc.tensor.matmul(dst, wh[:, 0, own], x_high[:, g, :], start=True, stop=False)
                        nc.tensor.matmul(dst, wl[:, 0, own], x_high[:, g, :], start=False, stop=False)
                        mm = nc.tensor.matmul(dst, wh[:, 0, own], x_low[:, g, :], start=False, stop=True)
                    mm.then_inc(in_ready, 1)

                def down(g, m):
                    e, c = m // per, m % per
                    wait(pe, low_ready, M * g + m + 1)
                    if c == 0:
                        wait(pe, x_ready, NE * g + e - 1)
                    for t in range(GB):
                        own, dst = slice(P * t, P * (t + 1)), y_ps[e % 2][:, D * t:D * (t + 1)]
                        parts = [(high, 0), (high, 1), (low, 0)]
                        for k, (h, part) in enumerate(parts):
                            mm = nc.tensor.matmul(dst, h[m % RING][:, own], w_down[part][:, m, :],
                                                  start=(c == 0 and t == 0 and k == 0), stop=(c == per - 1 and k == 2),
                                                  skip_group_check=True)
                    mm.then_inc(down_done, 1)

                def group(g):
                    for m in range(M + LAG):
                        if m < M:
                            project(g, m)
                        if m >= LAG:
                            down(g, m - LAG)

                groups(pe, group)

            @block.scalar
            def _(act):
                def split(g, m):
                    wait(act, hidden_ready, M * g + m + 1)
                    wait(act, down_done, M * g + m + 1 - RING)
                    nc.scalar.activation(high[m % RING][:, :], hidden[m % RING][:, :], ACT.Copy).then_inc(high_ready, 1)

                def group(g):
                    for m in range(M + 1):
                        if m < M:
                            wait(act, in_ready, M * g + m + 1)
                            wait(act, hidden_ready, M * g + m + 1 - RING)
                            func, scale = (ACT.Silu, 1.0 / WSCALE) if gated else (ACT.Relu, 1.0 / WSCALE ** 2)
                            nc.scalar.activation(act_out[m % RING][:, :], in_ps[0][m % 2][0:rows, :], func,
                                                 scale=scale).then_inc(act_ready, 1)
                        if m >= 1:
                            split(g, m - 1)

                groups(act, group)

            @block.vector
            def _(dve):
                def accumulate(g, e):
                    wait(dve, down_done, M * g + per * (e + 1))
                    for t in range(GB):
                        n = GB * g + t
                        wait(dve, x_ready, NE * g + e)
                        last = nc.vector.scalar_tensor_tensor(
                            out=x_all[:, n, :], in0=y_ps[e % 2][:, D * t:D * (t + 1)], scalar=scores[:, n, e, :],
                            in1=x_all[:, n, :], op0=ALU.mult, op1=ALU.add)
                    last.then_inc(x_ready, 1)
                    if e == NE - 1 and stats is not None:
                        wait(dve, x_ready, NE * (g + 1))
                        for t in range(GB):
                            n = GB * g + t
                            last = nc.vector.bn_stats(stats[:, n, :], x_all[:, n, :])
                        last.then_inc(stats_ready, 1)

                def group(g):
                    for m in range(M + LAG + 1):
                        if m < M:
                            k = m % RING
                            wait(dve, act_ready, M * g + m + 1)
                            wait(dve, low_ready, M * g + m + 1 - RING)
                            dst, a = hidden[k][:, :], act_out[k][:, :]
                            src = in_ps[-1][m % 2][0:rows, :]
                            scalar, op = (1.0 / WSCALE, ALU.mult) if gated else (0.0, ALU.max)
                            nc.vector.scalar_tensor_tensor(out=dst, in0=src, scalar=scalar, in1=a, op0=op,
                                                           op1=ALU.mult).then_inc(hidden_ready, 1)
                        e = m - LAG - 1
                        if e >= 0 and e % per == per - 1:
                            accumulate(g, e // per)

                groups(dve, group)

            @block.gpsimd
            def _(pool):
                def group(g):
                    for m in range(M):
                        k = m % RING
                        wait(pool, high_ready, M * g + m + 1)
                        nc.gpsimd.tensor_tensor(low[k][:, :], hidden[k][:, :], high[k][:, :],
                                                ALU.subtract).then_inc(low_ready, 1)

                groups(pool, group)

            if out is not None:
                @block.sync
                def _(sp):
                    def group(g):
                        wait(sp, x_ready, NE * (g + 1))
                        for t in range(GB):
                            sp.dma_start(out[GB * g + t], x_all[:, GB * g + t, :]).then_inc(x_stored, 16)

                    groups(sp, group)
                    sp.wait_ge(x_stored, 16 * B)


def relative_attention(nc, B, io, x_all, stats, mean, rstd, ident, gates, q_dram, r_dram):
    with ExitStack() as ctx:
        def sb(n, s):
            return ctx.enter_context(nc.sbuf_tensor("a1_" + n, s, F32))

        def ps(n):
            return ctx.enter_context(nc.psum_tensor("a1_" + n, [P, 512], F32))

        def sem(n):
            return ctx.enter_context(nc.semaphore("a1_" + n))

        w_q, w_k, w_v, w_o = (sb(n, [P, D]) for n in ("w_q", "w_k", "w_v", "w_o"))
        b_q, b_k, b_v, b_o = sb("b_q", [P, 1]), sb("b_k", [P, 1]), sb("b_v", [P, P]), sb("b_o", [P, D])
        head_mask = sb("head_mask", [P, NH])
        key_table, value_table = sb("key_table", [QC * HD, KT]), sb("value_table", [KC, P, HD])
        xn = [sb(f"xn{p}", [P, D]) for p in range(2)]
        xt = [sb(f"xt{p}", [P, P]) for p in range(2)]
        ctx_t = [sb(f"ctx_t{p}", [P, KC]) for p in range(2)]
        q_t = [sb(f"q_t{p}", [P, P]) for p in range(2)]
        k_t = [sb(f"k_t{p}", [P, KC]) for p in range(2)]
        value = [sb(f"value{p}", [KC, NH, HD + 1]) for p in range(2)]
        q_rows = [sb(f"q_rows{p}", [P, HD, NH]) for p in range(2)]
        q_head = [sb(f"q_head{p}", [P, P, NH]) for p in range(2)]
        q_pos = [sb(f"q_pos{p}", [QC * HD, QG, QC, NH]) for p in range(2)]
        prob_t = [sb(f"prob_t{p}", [KC, QG, P]) for p in range(2)]
        rel_all = [sb(f"rel_all{p}", [P, QG, QC, HD]) for p in range(2)]
        rel = [sb(f"rel{p}", [P, NH, HD]) for p in range(2)]
        mixed = [sb(f"mixed{p}", [P, NH, HD]) for p in range(2)]
        rden = [sb(f"rden{p}", [P, NH]) for p in range(2)]
        mixed_t = [sb(f"mixed_t{p}", [P, P]) for p in range(2)]
        top = [sb(f"top{k}", [P, 4]) for k in range(4)]
        prob = [sb(f"prob{k}", [P, 4, KC]) for k in range(4)]

        score_ps = [ps(f"score{k}") for k in range(2)]
        trans_ps = [ps(f"trans{k}") for k in range(2)]
        prep_ps, rel_ps, mix_ps, fin_ps = ps("prep"), ps("rel"), ps("mix"), ps("fin")

        weights_in, weights_ready, bias_ready = sem("weights_in"), sem("weights_ready"), sem("bias_ready")
        cleared = sem("cleared")
        ctx_in, q_in = [sem(f"ctx_in{p}") for p in range(2)], [sem(f"q_in{p}") for p in range(2)]
        q_out, rel_out, rel_in = (sem(n) for n in ("q_out", "rel_out", "rel_in"))
        xn_ready, xn_t, xt_ready = sem("xn_ready"), sem("xn_t"), sem("xt_ready")
        proj_ready, value_ps_ready = sem("proj_ready"), sem("value_ps_ready")
        q_ready, k_ready, value_ready = sem("q_ready"), sem("k_ready"), sem("value_ready")
        q_turned, q_rows_ready, q_head_ready = sem("q_turned"), sem("q_rows_ready"), sem("q_head_ready")
        score_ready, top_ready, shifted, exped = sem("score_ready"), sem("top_ready"), sem("shifted"), sem("exped")
        prob_ready, prob_copied = sem("prob_ready"), sem("prob_copied")
        rel_ready, rel_copied = sem("rel_ready"), sem("rel_copied")
        mix_ready, rden_ready, divided = sem("mix_ready"), sem("rden_ready"), sem("divided")
        rel_divided, mixed_ready = sem("rel_divided"), sem("mixed_ready")
        mixed_turned, mixed_copied = sem("mixed_turned"), sem("mixed_copied")
        y_ready, x_biased, x_ready, stats_ready = sem("y_ready"), sem("x_biased"), sem("x_ready"), sem("stats_ready")

        LO, HI, LAST = 4, B - 2, B + 3
        WEIGHTS = [(w_q, "w_q"), (w_k, "w_k"), (w_v, "w_v"), (w_o, "w_o"), (b_q, "b_q"), (b_k, "b_k"), (b_v, "b_v"),
                   (b_o, "b_o"), (head_mask, "head_mask16"), (key_table, "key_table")]

        with nc.Block(name="a1") as block:
            @block.sync
            def _(sp):
                for t, src in WEIGHTS:
                    sp.dma_start(t[:, :], io[src]).then_inc(weights_in, 16)
                sp.dma_start(value_table[:, :, :], io["value_table"]).then_inc(weights_in, 16)

                def context(n, p):
                    if inside(n, 0, B):
                        wait(sp, value_ps_ready, n - 1)
                        sp.dma_start(ctx_t[p][:, :], io["ctx"][n]).then_inc(ctx_in[p], 16)

                def queries(n, p):
                    if inside(n, 0, B):
                        wait(sp, q_rows_ready, n + 1)
                        sp.dma_start(q_dram[p], q_rows[p][:, :, :].rearrange("q d h -> q (d h)")).then_inc(q_out, 16)
                        wait(sp, q_out, 16 * n + 16)
                        src = q_dram[p].rearrange("(g c) (d h) -> c d g h", c=QC, d=HD)
                        for c in range(QC):
                            sp.dma_start(q_pos[p][HD * c:HD * (c + 1), :, c, :], src[c]).then_inc(q_in[p], 16)

                def relative(n, p):
                    if inside(n, 0, B):
                        wait(sp, rel_copied, 4 * n + 4)
                        dst = r_dram[p].rearrange("(g c) (h d) -> c h g d", c=QC, d=HD)
                        for c in range(QC):
                            sp.dma_start(dst[c], rel_all[p][NH * c:NH * (c + 1), :, c, :]).then_inc(rel_out, 16)
                        wait(sp, rel_out, 128 * n + 128)
                        sp.dma_start(rel[p][:, :, :].rearrange("q h d -> q (h d)"), r_dram[p]).then_inc(rel_in, 16)

                def slot(n, p):
                    o = 1 - p
                    queries(n + 1, o)
                    context(n + 2, p)
                    relative(n - 1, o)

                sp.wait_ge(cleared, 1)
                context(0, 0)
                slots(sp, -1, LO, HI, LAST, slot)

            @block.tensor
            def _(pe):
                def prep_turn(n, p):
                    if inside(n, 0, B):
                        wait(pe, xn_ready, n + 1)
                        wait(pe, q_rows_ready, n)
                        nc.tensor.transpose(prep_ps[:, 0:P], xn[p][:, :], ident[:, :]).then_inc(xn_t, 1)

                def project(n, p):
                    if inside(n, 0, B):
                        wait(pe, xt_ready, n + 1)
                        wait(pe, ctx_in[p], (n - p) * 8 + 16)
                        nc.tensor.matmul(prep_ps[:, 0:P], w_q[:, :], xt[p][:, :], start=True, stop=True)
                        nc.tensor.matmul(prep_ps[:, P:P + KC], w_k[:, :], ctx_t[p][:, :],
                                         start=True, stop=True).then_inc(proj_ready, 1)

                def project_value(n, p):
                    if inside(n, 0, B):
                        wait(pe, xt_ready, min(n + 2, B) if isinstance(n, int) else n + 2)
                        nc.tensor.matmul(prep_ps[0:KC, 256:256 + D], ctx_t[p][:, :], w_v[:, :],
                                         start=True, stop=True).then_inc(value_ps_ready, 1)

                def query_turn(n, p):
                    if inside(n, 0, B):
                        wait(pe, q_ready, n + 1)
                        wait(pe, k_ready, n + 1)
                        wait(pe, value_ready, n)
                        nc.tensor.transpose(prep_ps[:, 384:384 + P], q_t[p][:, :], ident[:, :]).then_inc(q_turned, 1)

                def scores(n, p, u):
                    if inside(n, 0, B):
                        if u == 0:
                            wait(pe, q_head_ready, n + 1)
                            wait(pe, k_ready, n + 1)
                            wait(pe, q_in[p], (n - p) * 64 + 128)
                        wait(pe, shifted, 4 * n + u - 1)
                        for j in range(4):
                            g = 4 * u + j
                            dst = score_ps[u % 2][:, KC * j:KC * (j + 1)]
                            nc.tensor.matmul(dst, q_head[p][:, QC * g:QC * (g + 1), :], k_t[p][:, :],
                                             start=True, stop=False)
                            mm = nc.tensor.matmul(dst, q_pos[p][:, g, :, :],
                                                  key_table[:, KT - KC - QC * g:KT - QC * g], start=False, stop=True)
                        mm.then_inc(score_ready, 1)

                def turn(n, u):
                    if inside(n, 0, B):
                        wait(pe, exped, 4 * n + u + 1)
                        wait(pe, prob_copied, 4 * n + u - 1)
                        for j in range(4):
                            mm = nc.tensor.transpose(trans_ps[u % 2][0:KC, P * j:P * (j + 1)], prob[u][:, j, :],
                                                     ident[:, :])
                        mm.then_inc(prob_ready, 1)

                def relative(n, p, u):
                    if inside(n, 0, B):
                        wait(pe, prob_copied, 4 * n + u + 1)
                        wait(pe, rel_copied, 4 * n + u)
                        for j in range(4):
                            g = 4 * u + j
                            mm = nc.tensor.matmul(rel_ps[:, QC * HD * j:QC * HD * (j + 1)], prob_t[p][:, g, :],
                                                  value_table[:, QC * g:QC * (g + 1), :], start=True, stop=True)
                        mm.then_inc(rel_ready, 1)

                def mix(n, p, half):
                    if inside(n, 0, B):
                        if half == 0:
                            wait(pe, prob_copied, 4 * n + 4)
                            wait(pe, value_ready, n + 1)
                            wait(pe, divided, n)
                        by_head = prob_t[p][:, :, :].rearrange("k g (c h) -> k (g c) h", h=NH)
                        for h in range(8 * half, 8 * half + 8):
                            mm = nc.tensor.matmul(mix_ps[:, (HD + 1) * h:(HD + 1) * (h + 1)], by_head[:, :, h],
                                                  value[p][:, h, :], start=True, stop=True)
                        if half == 1:
                            mm.then_inc(mix_ready, 1)

                def fin_turn(n, p):
                    if inside(n, 0, B):
                        wait(pe, mixed_ready, n + 1)
                        wait(pe, x_ready, n)
                        nc.tensor.transpose(fin_ps[:, 0:P], mixed[p][:, :, :].rearrange("q h d -> q (h d)"),
                                            ident[:, :]).then_inc(mixed_turned, 1)

                def fin_project(n, p):
                    if inside(n, 0, B):
                        wait(pe, mixed_copied, n + 1)
                        nc.tensor.matmul(fin_ps[:, 0:D], mixed_t[p][:, :], w_o[:, :],
                                         start=True, stop=True).then_inc(y_ready, 1)

                def slot(n, p):
                    o = 1 - p
                    scores(n, p, 0)
                    turn(n - 1, 2)
                    relative(n - 1, o, 1)
                    project(n + 1, o)
                    project_value(n, p)
                    fin_turn(n - 3, o)
                    scores(n, p, 1)
                    turn(n - 1, 3)
                    relative(n - 1, o, 2)
                    query_turn(n + 1, o)
                    scores(n, p, 2)
                    turn(n, 0)
                    relative(n - 1, o, 3)
                    mix(n - 1, o, 0)
                    fin_project(n - 3, o)
                    scores(n, p, 3)
                    turn(n, 1)
                    mix(n - 1, o, 1)
                    relative(n, p, 0)
                    prep_turn(n + 2, p)

                pe.wait_ge(weights_ready, 2)
                nc.tensor.matmul(fin_ps[:, 0:D], b_v[:, :], w_o[:, :], start=True, stop=True).then_inc(bias_ready, 1)
                pe.wait_ge(weights_ready, 3)
                prep_turn(0, 0)
                slots(pe, -1, LO, HI, LAST, slot)

            @block.scalar
            def _(act):
                act.wait_ge(weights_in, 16 * (len(WEIGHTS) + 1))

                def copy_xn(n, p):
                    if inside(n, 0, B):
                        wait(act, xn_t, n + 1)
                        wait(act, proj_ready, n - 1)
                        nc.scalar.activation(xt[p][:, :], prep_ps[:, 0:P], ACT.Copy).then_inc(xt_ready, 1)

                def biased(n, p):
                    if inside(n, 0, B):
                        wait(act, proj_ready, n + 1)
                        wait(act, value_ps_ready, n)
                        wait(act, q_turned, n - 1)
                        wait(act, q_head_ready, n - 1)
                        wait(act, score_ready, 4 * n - 4)
                        nc.scalar.activation(q_t[p][:, :], prep_ps[:, 0:P], ACT.Identity,
                                             bias=b_q[:, 0:1]).then_inc(q_ready, 1)
                        nc.scalar.activation(k_t[p][:, :], prep_ps[:, P:P + KC], ACT.Identity,
                                             bias=b_k[:, 0:1]).then_inc(k_ready, 1)

                def copy_value(n, p):
                    if inside(n, 0, B):
                        wait(act, value_ps_ready, n + 1)
                        wait(act, mix_ready, n - 1)
                        nc.scalar.activation(value[p][:, :, 0:HD],
                                             prep_ps[0:KC, 256:256 + D].rearrange("k (h d) -> k h d", d=HD),
                                             ACT.Copy).then_inc(value_ready, 1)

                def copy_queries(n, p):
                    if inside(n, 0, B):
                        wait(act, q_turned, n + 1)
                        wait(act, q_out, 16 * n - 16)
                        wait(act, q_in[p], (n - p) * 64)
                        wait(act, score_ready, 4 * n - 4)
                        nc.scalar.activation(q_rows[p][:, :, :].rearrange("q d h -> q h d"),
                                             prep_ps[:, 384:384 + P].rearrange("q (h d) -> q h d", d=HD),
                                             ACT.Copy).then_inc(q_rows_ready, 1)

                def exp(n, u):
                    if inside(n, 0, B):
                        wait(act, shifted, 4 * n + u + 1)
                        nc.scalar.activation(prob[u][:, :, :], prob[u][:, :, :], ACT.Exp,
                                             scale=float(HD) ** -0.5).then_inc(exped, 1)

                def copy_prob(n, p, u):
                    if inside(n, 0, B):
                        wait(act, prob_ready, 4 * n + u + 1)
                        wait(act, rel_ready, 4 * n + u - 7)
                        wait(act, mix_ready, n - 1)
                        nc.scalar.activation(prob_t[p][:, 4 * u:4 * u + 4, :],
                                             trans_ps[u % 2][0:KC, :].rearrange("k (g r) -> k g r", g=4),
                                             ACT.Copy).then_inc(prob_copied, 1)

                def copy_mixed(n, p):
                    if inside(n, 0, B):
                        wait(act, mixed_turned, n + 1)
                        wait(act, y_ready, n - 1)
                        nc.scalar.activation(mixed_t[p][:, :], fin_ps[:, 0:P], ACT.Copy).then_inc(mixed_copied, 1)

                def slot(n, p):
                    o = 1 - p
                    copy_prob(n - 1, o, 2)
                    biased(n + 1, o)
                    copy_value(n, p)
                    exp(n, 0)
                    copy_mixed(n - 3, o)
                    copy_prob(n - 1, o, 3)
                    copy_queries(n + 1, o)
                    exp(n, 1)
                    copy_prob(n, p, 0)
                    exp(n, 2)
                    copy_prob(n, p, 1)
                    copy_xn(n + 2, p)
                    exp(n, 3)

                copy_xn(0, 0)
                slots(act, -1, LO, HI, LAST, slot)

            @block.gpsimd
            def _(pool):
                for p in range(2):
                    nc.gpsimd.memset(value[p][:, :, HD:HD + 1], 1.0)
                    last = nc.gpsimd.memset(q_pos[p][:, :, :, :], 0.0)
                last.then_inc(cleared, 1)
                pool.wait_ge(weights_ready, 3)

                def slot(n, p):
                    if inside(n, 0, B):
                        wait(pool, q_ready, n + 1)
                        wait(pool, score_ready, 4 * n - 4)
                        nc.gpsimd.tensor_tensor(q_head[p][:, :, :], q_t[p][:, :].unsqueeze(2).broadcast_to([P, P, NH]),
                                                head_mask[:, :].unsqueeze(1).broadcast_to([P, P, NH]),
                                                ALU.mult).then_inc(q_head_ready, 1)
                        wait(pool, xn_ready, n + 1)
                        nc.gpsimd.tensor_tensor(x_all[:, n, :], x_all[:, n, :], b_o[:, :], ALU.add).then_inc(x_biased, 1)

                slots(pool, 0, LO, HI, B, slot)

            @block.vector
            def _(dve):
                dve.wait_ge(weights_in, 16 * (len(WEIGHTS) + 1))
                nc.vector.tensor_scalar(w_o[:, :], w_o[:, :], gates[:, 2:3], None, ALU.mult).then_inc(weights_ready, 1)
                nc.vector.tensor_scalar(b_o[:, :], b_o[:, :], gates[:, 2:3], None, ALU.mult).then_inc(weights_ready, 1)
                dve.wait_ge(weights_ready, 2)
                dve.wait_ge(bias_ready, 1)
                nc.vector.tensor_tensor(b_o[:, :], b_o[:, :], fin_ps[:, 0:D], ALU.add).then_inc(weights_ready, 1)

                def normalize(n, p):
                    if inside(n, 0, B):
                        wait(dve, xn_t, n - 1)
                        nc.vector.tensor_scalar(xn[p][:, :], x_all[:, n, :], mean[:, n, :], rstd[:, n, :],
                                                ALU.subtract, ALU.mult).then_inc(xn_ready, 1)

                def softmax_shift(n, u):
                    if inside(n, 0, B):
                        s = score_ps[u % 2][:, 0:4 * KC].rearrange("r (g k) -> r g k", g=4)
                        wait(dve, score_ready, 4 * n + u + 1)
                        nc.vector.tensor_reduce(top[u][:, :], s, AX_X, ALU.max).then_inc(top_ready, 1)
                        wait(dve, top_ready, 4 * n + u + 1)
                        wait(dve, prob_ready, 4 * n + u - 3)
                        nc.vector.tensor_tensor(prob[u][:, :, :], s, top[u][:, :].unsqueeze(2).broadcast_to([P, 4, KC]),
                                                ALU.subtract).then_inc(shifted, 1)

                def copy_relative(n, p, u):
                    if inside(n, 0, B):
                        wait(dve, rel_ready, 4 * n + u + 1)
                        if u == 0:
                            wait(dve, rel_out, 128 * n - 128)
                            wait(dve, rel_in, 16 * n - 16)
                        nc.vector.tensor_copy(rel_all[p][:, 4 * u:4 * u + 4, :, :].rearrange("r g c d -> r (g c d)"),
                                              rel_ps[:, 0:4 * QC * HD]).then_inc(rel_copied, 1)

                def divide(n, p):
                    if inside(n, 0, B):
                        m = mix_ps[:, 0:NH * (HD + 1)].rearrange("q (h d) -> q h d", h=NH)
                        wait(dve, mix_ready, n + 1)
                        nc.vector.reciprocal(rden[p][:, :], m[:, :, HD]).then_inc(rden_ready, 1)
                        wait(dve, rden_ready, n + 1)
                        wait(dve, mixed_turned, n - 1)
                        nc.vector.tensor_tensor(mixed[p][:, :, :], m[:, :, 0:HD],
                                                rden[p][:, :].unsqueeze(2).broadcast_to([P, NH, HD]),
                                                ALU.mult).then_inc(divided, 1)

                def add_relative(n, p):
                    if inside(n, 0, B):
                        wait(dve, rel_in, 16 * n + 16)
                        nc.vector.tensor_tensor(rel[p][:, :, :], rel[p][:, :, :],
                                                rden[p][:, :].unsqueeze(2).broadcast_to([P, NH, HD]),
                                                ALU.mult).then_inc(rel_divided, 1)
                        wait(dve, rel_divided, n + 1)
                        wait(dve, divided, n + 1)
                        nc.vector.tensor_tensor(mixed[p][:, :, :], mixed[p][:, :, :], rel[p][:, :, :],
                                                ALU.add).then_inc(mixed_ready, 1)

                def residual(n):
                    if inside(n, 0, B):
                        wait(dve, y_ready, n + 1)
                        wait(dve, x_biased, n + 1)
                        nc.vector.tensor_tensor(x_all[:, n, :], x_all[:, n, :], fin_ps[:, 0:D],
                                                ALU.add).then_inc(x_ready, 1)

                def statistics(n):
                    if inside(n, 0, B):
                        wait(dve, x_ready, n + 1)
                        nc.vector.bn_stats(stats[:, n, :], x_all[:, n, :]).then_inc(stats_ready, 1)

                def slot(n, p):
                    o = 1 - p
                    softmax_shift(n, 0)
                    copy_relative(n - 1, o, 1)
                    divide(n - 2, p)
                    normalize(n + 2, p)
                    softmax_shift(n, 1)
                    copy_relative(n - 1, o, 2)
                    softmax_shift(n, 2)
                    copy_relative(n - 1, o, 3)
                    residual(n - 3)
                    softmax_shift(n, 3)
                    copy_relative(n, p, 0)
                    statistics(n - 3)
                    add_relative(n - 2, p)

                normalize(0, 0)
                normalize(1, 1)
                slots(dve, 0, LO, HI, LAST, slot)


def flamingo_kernel(nc, io, out):
    B = io["x"].shape[0]
    with ExitStack() as ctx:
        def sb(n, s):
            return ctx.enter_context(nc.sbuf_tensor(n, s, F32))

        x_all = sb("x_all", [P, B, D])
        stats, mean, rstd = sb("stats", [P, B, 6]), sb("mean", [P, B, 1]), sb("rstd", [P, B, 1])
        ident, gates = sb("ident", [P, P]), sb("gates", [P, 4])

        consts_in = ctx.enter_context(nc.semaphore("consts_in"))
        gates_ready = ctx.enter_context(nc.semaphore("gates_ready"))
        with nc.Block(name="consts") as block:
            @block.scalar
            def _(act):
                act.dma_start(ident[:, :], io["ident"]).then_inc(consts_in, 16)
                act.dma_start(gates[:, :], io["gates"]).then_inc(consts_in, 16)
                act.wait_ge(consts_in, 32)
                nc.scalar.activation(gates[:, :], gates[:, :], ACT.Tanh).then_inc(gates_ready, 1)

        load_x(nc, B, io["x"], x_all, stats)
        layernorm_constants(nc, "ln0", stats, mean[:, :, 0], rstd[:, :, 0], B)
        feature_attention(nc, B, io, x_all, stats, mean, rstd, ident, gates)
        layernorm_constants(nc, "ln1", stats, mean[:, :, 0], rstd[:, :, 0], B)
        x_high = ctx.enter_context(nc.sbuf_tensor("x_high", [P, B // GB, GT], F16))
        x_low = ctx.enter_context(nc.sbuf_tensor("x_low", [P, B // GB, GT], F16))
        logits, scores = sb("logits", [P, B // GB, GB * NE]), sb("scores", [P, B, NE, 1])
        with ExitStack() as layer:
            def parts(n, s):
                return [layer.enter_context(nc.sbuf_tensor(f"{n}_{k}", s, F16)) for k in ("high", "low")]

            actor = layer.enter_context(nc.sbuf_tensor("actor", [P, B // GB, GB * MAX_K], F32))
            w_gate, w_up = parts("w_gate", [P, 1, NE * I0]), parts("w_up", [P, 1, NE * I0])
            w_down = parts("w_down", [R0, NE * C0, D])
            split_weights(nc, "split0", [(io["gate_w"], *w_gate), (io["up_w"], *w_up), (io["down_w"], *w_down)])
            router(nc, "r0", B, io, x_all, mean, rstd, ident, x_high, x_low, logits, actor)
            expert_scores(nc, "e0", B, io, logits, actor, scores, gates[:, 1:2])
            experts(nc, "f0", B, x_high, x_low, x_all, scores, [w_gate, w_up], w_down, R0, C0, stats=stats)
        layernorm_constants(nc, "ln2", stats, mean[:, :, 0], rstd[:, :, 0], B)
        q_dram = nc.dram_tensor("queries", [2, P, D], F32).ap()
        r_dram = nc.dram_tensor("relative_values", [2, P, D], F32).ap()
        relative_attention(nc, B, io, x_all, stats, mean, rstd, ident, gates, q_dram, r_dram)
        layernorm_constants(nc, "ln3", stats, mean[:, :, 0], rstd[:, :, 0], B)
        with ExitStack() as layer:
            def parts(n, s):
                return [layer.enter_context(nc.sbuf_tensor(f"{n}_{k}", s, F16)) for k in ("high", "low")]

            w1, w2 = parts("w1", [P, 1, NE * I1]), parts("w2", [R1, NE * C1, D])
            split_weights(nc, "split1", [(io["w1"], *w1), (io["w2"], *w2)])
            router(nc, "r1", B, io, x_all, mean, rstd, ident, x_high, x_low, logits)
            expert_scores(nc, "e1", B, io, logits, None, scores, gates[:, 3:4])
            experts(nc, "f1", B, x_high, x_low, x_all, scores, [w1], w2, R1, C1, out=out)


def _layout(np, a):
    B = a["x"].shape[0]
    row = np.arange(P)
    tile = np.tile
    d = {}
    d["x"] = a["x"]
    d["ident"] = np.eye(P, dtype=np.float32)
    d["gates"] = tile(np.stack([a["g_xattn"][0], a["g_ffn"][0], a["g_xattn"][1], a["g_ffn"][1]])[None, :], (P, 1))
    d["ctx"] = a["ctx_1024"].transpose(0, 2, 1)
    d["fm_w"] = tile(a["L0_xattn_fm_w"].T, (NH, 1))
    head = row[:, None] // HD == np.arange(NH)[None, :]
    d["fm_sign"] = np.stack([head, -1.0 * head], axis=2).reshape(P, 2 * NH).astype(np.float32)
    d["fm_b"] = tile(a["L0_xattn_fm_b"], NH)[:, None]
    d["row_sign"] = np.where(row % FD < HD, 1.0, -1.0).astype(np.float32)[:, None]
    d["head_mask"] = (row[:, None] // FD == np.arange(8)[None, :]).astype(np.float32)
    d["fc_w"] = a["L0_xattn_fc_w"].T.reshape(2, P, D).transpose(1, 0, 2)
    d["fc_b"] = tile(a["L0_xattn_fc_b"][None, :], (P, 1))
    d["r0_router"] = a["L0_ffn_router_w"].T
    d["actor_w1"] = a["L0_ffn_actor_w1"].T
    d["actor_b1"] = a["L0_ffn_actor_b1"][:, None]
    d["actor_w2"] = a["L0_ffn_actor_w2"].T
    d["actor_b2"] = tile(a["L0_ffn_actor_b2"][None, :], (P, 1))
    d["experts_after"] = tile(np.arange(NE - 1, -1, -1, dtype=np.float32)[None, :], (P, 1))
    d["first_k"] = tile(np.arange(-MAX_K, 0, dtype=np.float32)[None, :], (P, 1))
    d["gate_w"] = a["L0_ffn_gate_w"].reshape(NE * I0, 1, D).transpose(2, 1, 0)
    d["up_w"] = a["L0_ffn_up_w"].reshape(NE * I0, 1, D).transpose(2, 1, 0)
    d["down_w"] = a["L0_ffn_down_w"].transpose(0, 2, 1).reshape(NE * C0, R0, D).transpose(1, 0, 2)
    d["r1_router"] = a["L1_ffn_Wg"]
    d["w1"] = a["L1_ffn_W1"].transpose(1, 0, 2).reshape(D, 1, NE * I1)
    d["w2"] = a["L1_ffn_W2"].reshape(NE * C1, R1, D).transpose(1, 0, 2)
    for n in "qkvo":
        d[f"w_{n}"] = a[f"L1_xattn_W{n}"]
    d["b_q"], d["b_k"] = a["L1_xattn_bq"][:, None], a["L1_xattn_bk"][:, None]
    d["b_v"] = tile(a["L1_xattn_bv"][:, None], (1, P))
    d["b_o"] = tile(a["L1_xattn_bo"][None, :], (P, 1))
    d["head_mask16"] = head.astype(np.float32)
    zero = a["L1_xattn_rel_key_table"].shape[0] // 2
    q, k, c, j = np.arange(P), np.arange(KC), np.arange(QC), np.arange(KT)
    keys = a["L1_xattn_rel_key_table"][zero + P - QC + c[:, None] - j[None, :]]
    d["key_table"] = keys.transpose(0, 2, 1).reshape(QC * HD, KT)
    d["value_table"] = a["L1_xattn_rel_value_table"][zero + q[None, :] - k[:, None]]
    return {k: np.ascontiguousarray(v) for k, v in d.items()}


def kernel(**inputs):
    import numpy as np
    import concourse.bacc as bacc
    from concourse.bass_utils import run_bass_kernel_spmd as run

    arrays = _layout(np, {k: np.asarray(v) for k, v in inputs.items()})
    nc = bacc.Bacc("TRN2", target_bir_lowering=False, num_devices=1)
    io = {k: nc.dram_tensor(f"in_{k}", v.shape, mybir.dt.from_np(v.dtype), kind="ExternalInput").ap()
          for k, v in arrays.items()}
    out = nc.dram_tensor("out_x", arrays["x"].shape, F32, kind="ExternalOutput").ap()
    flamingo_kernel(nc, io, out)
    r = run(nc, [{f"in_{k}": v for k, v in arrays.items()}], core_ids=[0])
    return r.results[0]["out_x"]
```

```python
from contextlib import ExitStack

import concourse.bass as bass
from concourse import mybir

F32 = mybir.dt.float32
F16 = mybir.dt.float16
ALU = mybir.AluOpType
ACT = mybir.ActivationFunctionType
AX_X = mybir.AxisListType.X

P = 128
D = 128
KC = 77
NH = 16
HD = D // NH
FD = 2 * HD
HQ = 4
QW = HQ * KC
EPS = 1e-5

QC = 8
QG = P // QC
KT = KC + P - QC
QB = 2 * HD
Q_STEP = QC * QB * NH + NH
Q_PITCH = QC * Q_STEP
R_STEP = NH * QC * HD + HD
R_PITCH = QC * R_STEP

NE = 8
GB = 4
GT = GB * P
AH = 50
MAX_K = 6
TOP_K = 2
I0, R0, C0 = 336, 112, 3
I1, R1, C1 = 256, 128, 2
WSCALE = 256.0
RING = 8


def wait(eng, sem, value):
    if isinstance(value, int) and value <= 0:
        return
    eng.wait_ge(sem, value)


def inside(n, lo, hi):
    return lo <= n < hi if isinstance(n, int) else True


def slots(eng, first, lo, hi, last, body):
    for n in range(first, lo):
        body(n, n % 2)
    with eng.Fori(0, (hi - lo) // 2) as i:
        for r in range(2):
            body(2 * i + (lo + r), (lo + r) % 2)
    for n in range(hi, last):
        body(n, n % 2)


class Program:
    pass


def layernorm_constants(nc, name, stats, mean, rstd, B):
    with ExitStack() as ctx:
        def sb(n, w):
            return ctx.enter_context(nc.sbuf_tensor(f"{name}_{n}", [P, w], F32))

        diff, var, sd, newton = sb("diff", B), sb("var", B), sb("sd", B), sb("newton", B)
        step = ctx.enter_context(nc.semaphore(f"{name}_step"))
        root = ctx.enter_context(nc.semaphore(f"{name}_root"))
        with nc.Block(name=name) as block:
            @block.scalar
            def _(act):
                act.wait_ge(step, 6)
                nc.scalar.activation(sd[:, :], var[:, :], ACT.Sqrt).then_inc(root, 1)

            @block.vector
            def _(dve):
                done = 0

                def link(ins):
                    nonlocal done
                    done += 1
                    ins.then_inc(step, 1)
                    dve.wait_ge(step, done)

                half = [stats[:, :, k] for k in range(6)]
                link(nc.vector.tensor_tensor(mean[:, :], half[1], half[4], ALU.add))
                link(nc.vector.tensor_tensor(diff[:, :], half[1], half[4], ALU.subtract))
                link(nc.vector.tensor_tensor(var[:, :], half[2], half[5], ALU.add))
                link(nc.vector.scalar_tensor_tensor(out=diff[:, :], in0=diff[:, :], scalar=0.25, in1=diff[:, :],
                                                    op0=ALU.mult, op1=ALU.mult))
                link(nc.vector.scalar_tensor_tensor(out=var[:, :], in0=var[:, :], scalar=1.0 / D, in1=diff[:, :],
                                                    op0=ALU.mult, op1=ALU.add))
                link(nc.vector.tensor_scalar(var[:, :], var[:, :], EPS, None, ALU.add))
                link(nc.vector.tensor_scalar(mean[:, :], mean[:, :], 0.5, None, ALU.mult))
                dve.wait_ge(root, 1)
                link(nc.vector.reciprocal(rstd[:, :], sd[:, :]))
                link(nc.vector.tensor_tensor(newton[:, :], rstd[:, :], rstd[:, :], ALU.mult))
                link(nc.vector.tensor_tensor(newton[:, :], newton[:, :], var[:, :], ALU.mult))
                link(nc.vector.tensor_scalar(newton[:, :], newton[:, :], -0.5, 1.5, ALU.mult, ALU.add))
                link(nc.vector.tensor_tensor(rstd[:, :], rstd[:, :], newton[:, :], ALU.mult))


def load_x(nc, B, x, x_all, stats):
    G = 4
    with ExitStack() as ctx:
        loaded = [ctx.enter_context(nc.semaphore(f"x_loaded{g}")) for g in range(G)]
        with nc.Block(name="load") as block:
            @block.sync
            def _(sp):
                for g in range(G):
                    own = slice(g * B // G, (g + 1) * B // G)
                    sp.dma_start(x_all[:, own, :], x[own].rearrange("b q d -> q b d")).then_inc(loaded[g], 16)

            @block.vector
            def _(dve):
                for g in range(G):
                    dve.wait_ge(loaded[g], 16)
                    with dve.Fori(g * B // G, (g + 1) * B // G) as n:
                        nc.vector.bn_stats(stats[:, n, :], x_all[:, n, :])


def feature_attention(nc, B, io, x_all, stats, mean, rstd, ident, gates):
    with ExitStack() as ctx:
        def sb(n, s):
            return ctx.enter_context(nc.sbuf_tensor("a0_" + n, s, F32))

        def ps(n):
            return ctx.enter_context(nc.psum_tensor("a0_" + n, [P, 512], F32))

        def sem(n):
            return ctx.enter_context(nc.semaphore("a0_" + n))

        w_rep, w_sign = sb("w_rep", [P, HD]), sb("w_sign", [P, 2 * 8 * 2])
        fm_w = sb("fm_w", [P, 2, P])
        b_rep, b_sign, fm_b = sb("b_rep", [P, 1]), sb("b_sign", [P, 1]), sb("fm_b", [P, 1])
        head_mask = sb("head_mask", [P, 8])
        fc_w, fc_b = sb("fc_w", [P, 2, D]), sb("fc_b", [P, D])
        xn = [sb(f"xn{p}", [P, D]) for p in range(2)]
        xc = [sb(f"xc{p}", [P, P + KC]) for p in range(2)]
        feat = [sb(f"feat{p}", [P, 2, P + KC]) for p in range(2)]
        kfeat = [sb(f"kfeat{p}", [P, 2, 8, KC]) for p in range(2)]
        vfeat = [sb(f"vfeat{p}", [KC, NH, FD + 1]) for p in range(2)]
        mixed = [sb(f"mixed{p}", [P, NH, FD]) for p in range(2)]
        mixed_t = [sb(f"mixed_t{p}", [P, 2, P]) for p in range(2)]
        top = [sb(f"top{k}", [P, HQ]) for k in range(4)]
        prob = [sb(f"prob{k}", [P, HQ, KC]) for k in range(4)]
        prob_t = [sb(f"prob_t{k}", [KC, HQ, P]) for k in range(4)]
        rden = [sb(f"rden{p}", [P, NH]) for p in range(2)]

        score_ps = [ps(f"score{k}") for k in range(2)]
        trans_ps = [ps(f"trans{k}") for k in range(2)]
        mix_ps = [ps(f"mix{p}") for p in range(2)]
        prep_ps, fin_ps = ps("prep"), ps("fin")

        weights_in, ctx_in = sem("weights_in"), [sem(f"ctx_in{p}") for p in range(2)]
        weights_ready = sem("weights_ready")
        xn_ready, xn_t, xn_copied = sem("xn_ready"), sem("xn_t"), sem("xn_copied")
        z_ready, feat_ready, kfeat_ready = sem("z_ready"), sem("feat_ready"), sem("kfeat_ready")
        value_t, value_copied = sem("value_t"), sem("value_copied")
        score_ready, top_ready, shifted, exped = sem("score_ready"), sem("top_ready"), sem("shifted"), sem("exped")
        prob_ready, prob_copied = sem("prob_ready"), sem("prob_copied")
        mix_ready, rden_ready, mixed_ready = sem("mix_ready"), sem("rden_ready"), sem("mixed_ready")
        mixed_turned, mixed_copied = sem("mixed_turned"), sem("mixed_copied")
        y_ready, x_biased, x_ready = sem("y_ready"), sem("x_biased"), sem("x_ready")
        stats_ready = sem("stats_ready")

        LO, HI, LAST = 4, B - 2, B + 2
        WEIGHTS = [(w_rep, io["fm_w"]), (w_sign, io["fm_sign"]), (b_rep, io["fm_b"]), (b_sign, io["row_sign"]),
                   (head_mask, io["head_mask"]), (fc_b, io["fc_b"])]

        with nc.Block(name="a0") as block:
            @block.sync
            def _(sp):
                for t, src in WEIGHTS:
                    sp.dma_start(t[:, :], src).then_inc(weights_in, 16)
                sp.dma_start(fc_w[:, :, :], io["fc_w"]).then_inc(weights_in, 16)

                def slot(n, p):
                    if inside(n, 0, B):
                        wait(sp, z_ready, n - 1)
                        sp.dma_start(xc[p][:, P:P + KC], io["ctx"][:, n, :]).then_inc(ctx_in[p], 16)

                slots(sp, 0, LO, HI, B, slot)

            @block.tensor
            def _(pe):
                def prep_turn(n, p):
                    if inside(n, 0, B):
                        wait(pe, xn_ready, n + 1)
                        wait(pe, value_copied, n)
                        nc.tensor.transpose(prep_ps[:, 0:P], xn[p][:, :], ident[:, :]).then_inc(xn_t, 1)

                def prep_z(n, p):
                    if inside(n, 0, B):
                        wait(pe, xn_copied, n + 1)
                        wait(pe, ctx_in[p], (n - p) * 8 + 16)
                        if isinstance(n, int) and n == 0:
                            pe.wait_ge(weights_ready, 4)
                        for c in range(2):
                            mm = nc.tensor.matmul(prep_ps[:, 256 * c:256 * c + P + KC], fm_w[:, c, :], xc[p][:, :],
                                                  start=True, stop=True)
                        mm.then_inc(z_ready, 1)

                def prep_value(n, p):
                    if inside(n, 0, B):
                        wait(pe, feat_ready, n + 1)
                        for c in range(2):
                            mm = nc.tensor.transpose(prep_ps[0:KC, P * c:P * (c + 1)], feat[p][:, c, P:P + KC],
                                                     ident[:, :])
                        mm.then_inc(value_t, 1)

                def scores(n, p, u):
                    if inside(n, 0, B):
                        if u % 2 == 0:
                            wait(pe, kfeat_ready, 2 * n + u // 2 + 1)
                        wait(pe, shifted, 4 * n + u - 1)
                        c = u // 2
                        nc.tensor.matmul(score_ps[u % 2][:, 0:QW], feat[p][:, c, 0:P],
                                         kfeat[p][:, c, 4 * (u % 2):4 * (u % 2) + 4, :],
                                         start=True, stop=True).then_inc(score_ready, 1)

                def turn(n, u):
                    if inside(n, 0, B):
                        wait(pe, exped, 4 * n + u + 1)
                        wait(pe, prob_copied, 4 * n + u - 1)
                        for h in range(HQ):
                            mm = nc.tensor.transpose(trans_ps[u % 2][0:KC, P * h:P * (h + 1)], prob[u][:, h, :],
                                                     ident[:, :])
                        mm.then_inc(prob_ready, 1)

                def mix(n, p, u):
                    if inside(n, 0, B):
                        wait(pe, prob_copied, 4 * n + u + 1)
                        if u == 0:
                            wait(pe, value_copied, n + 1)
                            wait(pe, mixed_ready, n - 1)
                        for h in range(HQ):
                            head = 4 * u + h
                            mm = nc.tensor.matmul(mix_ps[p][:, head * (FD + 1):(head + 1) * (FD + 1)],
                                                  prob_t[u][:, h, :], vfeat[p][:, head, :], start=True, stop=True)
                        if u == 3:
                            mm.then_inc(mix_ready, 1)

                def fin_turn(n, p):
                    if inside(n, 0, B):
                        wait(pe, mixed_ready, n + 1)
                        wait(pe, x_ready, n)
                        flat = mixed[p][:, :, :].rearrange("q h f -> q (h f)")
                        for c in range(2):
                            mm = nc.tensor.transpose(fin_ps[:, P * c:P * (c + 1)], flat[:, P * c:P * (c + 1)],
                                                     ident[:, :])
                        mm.then_inc(mixed_turned, 1)

                def fin_project(n, p):
                    if inside(n, 0, B):
                        wait(pe, mixed_copied, n + 1)
                        for c in range(2):
                            mm = nc.tensor.matmul(fin_ps[:, 0:D], mixed_t[p][:, c, :], fc_w[:, c, :],
                                                  start=(c == 0), stop=(c == 1))
                        mm.then_inc(y_ready, 1)

                def slot(n, p):
                    o = 1 - p
                    scores(n, p, 0)
                    turn(n - 1, 2)
                    mix(n - 1, o, 1)
                    fin_project(n - 2, p)
                    prep_turn(n + 1, o)
                    scores(n, p, 1)
                    turn(n - 1, 3)
                    mix(n - 1, o, 2)
                    prep_z(n + 1, o)
                    scores(n, p, 2)
                    turn(n, 0)
                    mix(n - 1, o, 3)
                    prep_value(n + 1, o)
                    scores(n, p, 3)
                    turn(n, 1)
                    mix(n, p, 0)
                    fin_turn(n - 1, o)

                slots(pe, -1, LO, HI, LAST, slot)

            @block.scalar
            def _(act):
                def copy_xn(n, p):
                    if inside(n, 0, B):
                        wait(act, xn_t, n + 1)
                        wait(act, z_ready, n - 1)
                        nc.scalar.activation(xc[p][:, 0:P], prep_ps[:, 0:P], ACT.Copy).then_inc(xn_copied, 1)

                def features(n, p):
                    if inside(n, 0, B):
                        wait(act, z_ready, n + 1)
                        z = prep_ps[:, :].rearrange("r (c t) -> r c t", c=2)[:, :, 0:P + KC]
                        nc.scalar.activation(feat[p][:, :, :], z, ACT.Exp, bias=fm_b[:, 0:1]).then_inc(feat_ready, 1)

                def copy_value(n, p):
                    if inside(n, 0, B):
                        wait(act, value_t, n + 1)
                        v = prep_ps[0:KC, 0:NH * FD].rearrange("k (h f) -> k h f", h=NH)
                        nc.scalar.activation(vfeat[p][:, :, 0:FD], v, ACT.Copy).then_inc(value_copied, 1)

                def exp(n, u):
                    if inside(n, 0, B):
                        wait(act, shifted, 4 * n + u + 1)
                        nc.scalar.activation(prob[u][:, :, :], prob[u][:, :, :], ACT.Exp,
                                             scale=float(D) ** -0.5).then_inc(exped, 1)

                def copy_prob(n, u):
                    if inside(n, 0, B):
                        wait(act, prob_ready, 4 * n + u + 1)
                        nc.scalar.activation(prob_t[u][:, :, :],
                                             trans_ps[u % 2][0:KC, :].rearrange("k (h q) -> k h q", h=HQ),
                                             ACT.Copy).then_inc(prob_copied, 1)

                def copy_mixed(n, p):
                    if inside(n, 0, B):
                        wait(act, mixed_turned, n + 1)
                        nc.scalar.activation(mixed_t[p][:, :, :],
                                             fin_ps[:, 0:2 * P].rearrange("f (c q) -> f c q", c=2),
                                             ACT.Copy).then_inc(mixed_copied, 1)

                def slot(n, p):
                    o = 1 - p
                    copy_prob(n - 1, 2)
                    copy_xn(n + 1, o)
                    exp(n, 0)
                    copy_prob(n - 1, 3)
                    features(n + 1, o)
                    exp(n, 1)
                    copy_prob(n, 0)
                    copy_value(n + 1, o)
                    exp(n, 2)
                    copy_prob(n, 1)
                    copy_mixed(n - 1, o)
                    exp(n, 3)

                act.wait_ge(weights_ready, 4)
                slots(act, -1, LO, HI, LAST, slot)

            @block.gpsimd
            def _(pool):
                for p in range(2):
                    nc.gpsimd.memset(vfeat[p][:, :, FD:FD + 1], 1.0)

                def slot(n, p):
                    if inside(n, 0, B):
                        wait(pool, feat_ready, n + 1)
                        wait(pool, score_ready, 4 * n - 4)
                        for c in range(2):
                            nc.gpsimd.tensor_tensor(
                                kfeat[p][:, c, :, :], feat[p][:, c, P:P + KC].unsqueeze(1).broadcast_to([P, 8, KC]),
                                head_mask[:, :].unsqueeze(2).broadcast_to([P, 8, KC]), ALU.mult).then_inc(kfeat_ready, 1)
                        nc.gpsimd.tensor_tensor(x_all[:, n, :], x_all[:, n, :], fc_b[:, :],
                                                ALU.add).then_inc(x_biased, 1)

                pool.wait_ge(weights_ready, 4)
                slots(pool, 0, LO, HI, B, slot)

            @block.vector
            def _(dve):
                dve.wait_ge(weights_in, 16 * (len(WEIGHTS) + 1))
                nc.vector.tensor_tensor(
                    fm_w[:, :, :].rearrange("r c (g e) -> r (c g) e", e=HD),
                    w_rep[:, :].unsqueeze(1).broadcast_to([P, 2 * 8 * 2, HD]),
                    w_sign[:, :].unsqueeze(2).broadcast_to([P, 2 * 8 * 2, HD]), ALU.mult).then_inc(weights_ready, 1)
                nc.vector.tensor_tensor(fm_b[:, :], b_rep[:, :], b_sign[:, :], ALU.mult).then_inc(weights_ready, 1)
                nc.vector.tensor_scalar(fc_w[:, :, :], fc_w[:, :, :], gates[:, 0:1], None,
                                        ALU.mult).then_inc(weights_ready, 1)
                nc.vector.tensor_scalar(fc_b[:, :], fc_b[:, :], gates[:, 0:1], None,
                                        ALU.mult).then_inc(weights_ready, 1)

                def normalize(n, p):
                    if inside(n, 0, B):
                        wait(dve, xn_t, n - 1)
                        nc.vector.tensor_scalar(xn[p][:, :], x_all[:, n, :], mean[:, n, :], rstd[:, n, :],
                                                ALU.subtract, ALU.mult).then_inc(xn_ready, 1)

                def softmax_shift(n, u):
                    if inside(n, 0, B):
                        s = score_ps[u % 2][:, 0:QW].rearrange("q (h k) -> q h k", h=HQ)
                        wait(dve, score_ready, 4 * n + u + 1)
                        nc.vector.tensor_reduce(top[u][:, :], s, AX_X, ALU.max).then_inc(top_ready, 1)
                        wait(dve, top_ready, 4 * n + u + 1)
                        wait(dve, prob_ready, 4 * n + u - 3)
                        nc.vector.tensor_tensor(prob[u][:, :, :], s, top[u][:, :].unsqueeze(2).broadcast_to([P, HQ, KC]),
                                                ALU.subtract).then_inc(shifted, 1)

                def divide(n, p):
                    if inside(n, 0, B):
                        m = mix_ps[p][:, 0:NH * (FD + 1)].rearrange("q (h f) -> q h f", h=NH)
                        wait(dve, mix_ready, n + 1)
                        nc.vector.reciprocal(rden[p][:, :], m[:, :, FD]).then_inc(rden_ready, 1)
                        wait(dve, rden_ready, n + 1)
                        wait(dve, mixed_turned, n - 1)
                        nc.vector.tensor_tensor(mixed[p][:, :, :], m[:, :, 0:FD],
                                                rden[p][:, :].unsqueeze(2).broadcast_to([P, NH, FD]),
                                                ALU.mult).then_inc(mixed_ready, 1)

                def residual(n):
                    if inside(n, 0, B):
                        wait(dve, y_ready, n + 1)
                        wait(dve, x_biased, n + 1)
                        nc.vector.tensor_tensor(x_all[:, n, :], x_all[:, n, :], fin_ps[:, 0:D],
                                                ALU.add).then_inc(x_ready, 1)

                def statistics(n):
                    if inside(n, 0, B):
                        wait(dve, x_ready, n + 1)
                        nc.vector.bn_stats(stats[:, n, :], x_all[:, n, :]).then_inc(stats_ready, 1)

                def slot(n, p):
                    o = 1 - p
                    softmax_shift(n, 0)
                    residual(n - 2)
                    softmax_shift(n, 1)
                    statistics(n - 2)
                    normalize(n + 2, p)
                    softmax_shift(n, 2)
                    divide(n - 1, o)
                    softmax_shift(n, 3)

                normalize(0, 0)
                normalize(1, 1)
                slots(dve, 0, LO, HI, LAST, slot)


def split_float16(nc, name, parts):
    with ExitStack() as ctx:
        loaded = [ctx.enter_context(nc.semaphore(f"{name}_loaded{k}")) for k in range(len(parts))]
        high_ready = ctx.enter_context(nc.semaphore(f"{name}_high_ready"))
        stage = [ctx.enter_context(nc.sbuf_tensor(f"{name}_stage{k}", list(high.shape), F32))
                 for k, (_, high, _, _) in enumerate(parts)]
        with nc.Block(name=name) as block:
            @block.sync
            def _(sp):
                for k, (t, (src, _, _, _)) in enumerate(zip(stage, parts)):
                    sp.dma_start(t[:, :, :], src).then_inc(loaded[k], 16)

            @block.scalar
            def _(act):
                for k, (t, (_, high, _, scale)) in enumerate(zip(stage, parts)):
                    act.wait_ge(loaded[k], 16)
                    nc.scalar.activation(high, t[:, :, :], ACT.Copy, scale=scale).then_inc(high_ready, 1)

            @block.vector
            def _(dve):
                for k, (t, (_, high, low, scale)) in enumerate(zip(stage, parts)):
                    dve.wait_ge(high_ready, k + 1)
                    flat = [v.rearrange("p a b -> p (a b)") for v in (t[:, :, :], high, low)]
                    nc.vector.scalar_tensor_tensor(out=flat[2], in0=flat[0], scalar=scale, in1=flat[1],
                                                   op0=ALU.mult, op1=ALU.subtract)


def router(nc, name, B, io, x_all, mean, rstd, ident, x_high, x_low, logits, actor=None):
    G = B // GB
    with ExitStack() as ctx:
        def sb(n, s):
            return ctx.enter_context(nc.sbuf_tensor(f"{name}_{n}", s, F32))

        def ps(n):
            return [ctx.enter_context(nc.psum_tensor(f"{name}_{n}{p}", [P, GT], F32)) for p in range(2)]

        def sem(n):
            return ctx.enter_context(nc.semaphore(f"{name}_{n}"))

        w_router = sb("w_router", [P, NE])
        xn = [sb(f"xn{p}", [P, GB, D]) for p in range(2)]
        xt = [sb(f"xt{p}", [P, GT]) for p in range(2)]
        turn_ps, logit_ps = ps("turn_ps"), ps("logit_ps")
        weights_in = sem("weights_in")
        xn_ready, turned, xt_ready = sem("xn_ready"), sem("turned"), sem("xt_ready")
        high_ready, low_ready = sem("high_ready"), sem("low_ready")
        logits_ready, logits_copied = sem("logits_ready"), sem("logits_copied")
        loads = [(w_router, io[name + "_router"])]
        if actor:
            w1, b1 = sb("w1", [P, AH]), sb("b1", [AH, 1])
            w2, b2 = sb("w2", [AH, MAX_K]), sb("b2", [P, MAX_K])
            pre = [sb(f"pre{p}", [AH, GT]) for p in range(2)]
            cube = [sb(f"cube{p}", [AH, GT]) for p in range(2)]
            hidden = [sb(f"hidden{p}", [AH, GT]) for p in range(2)]
            hidden_ps, actor_ps = ps("hidden_ps"), ps("actor_ps")
            loads += [(w1, io["actor_w1"]), (b1, io["actor_b1"]), (w2, io["actor_w2"]), (b2, io["actor_b2"])]
            w2_halved, pre_ps_ready, pre_ready = sem("w2_halved"), sem("pre_ps_ready"), sem("pre_ready")
            square_ready, factor_ready, cube_ready = sem("square_ready"), sem("factor_ready"), sem("cube_ready")
            tanh_ready, hidden_ready = sem("tanh_ready"), sem("hidden_ready")
            actor_ready, actor_copied = sem("actor_ready"), sem("actor_copied")

        with nc.Block(name=name) as block:
            @block.sync
            def _(sp):
                for t, src in loads:
                    sp.dma_start(t[:, :], src).then_inc(weights_in, 16)
                sp.wait_ge(weights_in, 16 * len(loads))

            def groups(eng, body, shift=0):
                slots(eng, 0, 2, G + shift - (G + shift) % 2, G + shift, body)

            @block.vector
            def _(dve):
                dve.wait_ge(weights_in, 16 * len(loads))
                if actor:
                    nc.vector.tensor_scalar(w2[:, :], w2[:, :], 0.5, None, ALU.mult).then_inc(w2_halved, 1)

                def normalize(g, p):
                    wait(dve, turned, g - 1)
                    for t in range(GB):
                        n = GB * g + t
                        last = nc.vector.tensor_scalar(xn[p][:, t, :], x_all[:, n, :], mean[:, n, :], rstd[:, n, :],
                                                       ALU.subtract, ALU.mult)
                    last.then_inc(xn_ready, 1)

                def gelu(g, p):
                    wait(dve, pre_ready, g + 1)
                    wait(dve, tanh_ready, g - 1)
                    nc.vector.tensor_tensor(cube[p][:, :], pre[p][:, :], pre[p][:, :], ALU.mult).then_inc(square_ready, 1)
                    wait(dve, square_ready, g + 1)
                    nc.vector.tensor_scalar(cube[p][:, :], cube[p][:, :], 0.044715, 1.0, ALU.mult,
                                            ALU.add).then_inc(factor_ready, 1)
                    wait(dve, factor_ready, g + 1)
                    nc.vector.tensor_tensor(cube[p][:, :], cube[p][:, :], pre[p][:, :], ALU.mult).then_inc(cube_ready, 1)
                    wait(dve, tanh_ready, g + 1)
                    wait(dve, actor_ready, g - 1)
                    nc.vector.scalar_tensor_tensor(out=hidden[p][:, :], in0=cube[p][:, :], scalar=1.0, in1=pre[p][:, :],
                                                   op0=ALU.add, op1=ALU.mult).then_inc(hidden_ready, 1)

                def group(g, p):
                    normalize(g, p)
                    wait(dve, xt_ready, g + 1)
                    wait(dve, low_ready, g - 1)
                    nc.vector.tensor_copy(x_high[:, g, :], xt[p][:, :]).then_inc(high_ready, 1)
                    if actor:
                        gelu(g, p)
                    wait(dve, logits_ready, g + 1)
                    nc.vector.tensor_copy(logits[:, g, :], logit_ps[p][:, 0:GB * NE]).then_inc(logits_copied, 1)
                    if actor:
                        wait(dve, actor_ready, g + 1)
                        nc.vector.tensor_tensor(
                            actor[:, g, :].rearrange("q (t k) -> q t k", t=GB),
                            actor_ps[p][:, 0:GB * MAX_K].rearrange("q (t k) -> q t k", t=GB),
                            b2[:, :].unsqueeze(1).broadcast_to([P, GB, MAX_K]), ALU.add).then_inc(actor_copied, 1)

                groups(dve, group)

            @block.tensor
            def _(pe):
                pe.wait_ge(weights_in, 16 * len(loads))
                if actor:
                    pe.wait_ge(w2_halved, 1)

                def group(g, p):
                    wait(pe, xn_ready, g + 1)
                    wait(pe, xt_ready, g - 1)
                    for t in range(GB):
                        mm = nc.tensor.transpose(turn_ps[p][:, P * t:P * (t + 1)], xn[p][:, t, :], ident[:, :])
                    mm.then_inc(turned, 1)
                    wait(pe, xt_ready, g + 1)
                    if actor:
                        wait(pe, pre_ready, g - 1)
                        nc.tensor.matmul(hidden_ps[p][0:AH, :], w1[:, :], xt[p][:, :],
                                         start=True, stop=True).then_inc(pre_ps_ready, 1)
                    wait(pe, logits_copied, g - 1)
                    for t in range(GB):
                        mm = nc.tensor.matmul(logit_ps[p][:, NE * t:NE * (t + 1)], xt[p][:, P * t:P * (t + 1)],
                                              w_router[:, :], start=True, stop=True)
                    mm.then_inc(logits_ready, 1)
                    if actor:
                        wait(pe, hidden_ready, g + 1)
                        wait(pe, actor_copied, g - 1)
                        for t in range(GB):
                            mm = nc.tensor.matmul(actor_ps[p][:, MAX_K * t:MAX_K * (t + 1)],
                                                  hidden[p][:, P * t:P * (t + 1)], w2[:, :], start=True, stop=True)
                        mm.then_inc(actor_ready, 1)

                groups(pe, group)

            @block.scalar
            def _(act):
                act.wait_ge(weights_in, 16 * len(loads))

                def group(g, p):
                    wait(act, turned, g + 1)
                    wait(act, low_ready, g - 1)
                    wait(act, logits_ready, g - 1)
                    nc.scalar.activation(xt[p][:, :], turn_ps[p][:, :], ACT.Copy).then_inc(xt_ready, 1)
                    if actor:
                        wait(act, pre_ps_ready, g + 1)
                        wait(act, hidden_ready, g - 1)
                        nc.scalar.activation(pre[p][:, :], hidden_ps[p][0:AH, :], ACT.Identity,
                                             bias=b1[:, 0:1]).then_inc(pre_ready, 1)
                        wait(act, cube_ready, g + 1)
                        nc.scalar.activation(cube[p][:, :], cube[p][:, :], ACT.Tanh,
                                             scale=(2.0 / 3.141592653589793) ** 0.5).then_inc(tanh_ready, 1)

                groups(act, group)

            @block.gpsimd
            def _(pool):
                def group(g, p):
                    wait(pool, high_ready, g + 1)
                    nc.gpsimd.tensor_tensor(x_low[:, g, :], xt[p][:, :], x_high[:, g, :],
                                            ALU.subtract).then_inc(low_ready, 1)

                groups(pool, group)


def expert_scores(nc, name, B, io, logits, actor, scores, gate):
    with ExitStack() as ctx:
        def sb(n, s):
            return ctx.enter_context(nc.sbuf_tensor(f"{name}_{n}", s, F32))

        probs, rank, cmp_ = sb("probs", [P, B, NE]), sb("rank", [P, B, NE]), sb("cmp", [P, B, NE])
        one, total = sb("one", [P, B]), sb("total", [P, B])
        after = sb("after", [P, NE])
        first, allowed, best = sb("first", [P, MAX_K]), sb("allowed", [P, B]), sb("best", [P, B])
        consts_in = ctx.enter_context(nc.semaphore(f"{name}_consts_in"))
        step = ctx.enter_context(nc.semaphore(f"{name}_step"))
        exped = ctx.enter_context(nc.semaphore(f"{name}_exped"))

        def wide(t, n=NE):
            return t[:, :].unsqueeze(2).broadcast_to([P, B, n])

        with nc.Block(name=name) as block:
            @block.sync
            def _(sp):
                sp.dma_start(after[:, :], io["experts_after"]).then_inc(consts_in, 16)
                sp.dma_start(first[:, :], io["first_k"]).then_inc(consts_in, 16)
                sp.wait_ge(consts_in, 32)

            @block.scalar
            def _(act):
                act.wait_ge(step, 2)
                nc.scalar.activation(probs[:, :, :], probs[:, :, :], ACT.Exp).then_inc(exped, 1)

            @block.vector
            def _(dve):
                done = 0

                def link(ins):
                    nonlocal done
                    done += 1
                    ins.then_inc(step, 1)
                    dve.wait_ge(step, done)

                l3 = logits[:, :, :].rearrange("q g (t e) -> q (g t) e", e=NE)
                link(nc.vector.tensor_reduce(one[:, :], l3, AX_X, ALU.max))
                link(nc.vector.tensor_tensor(probs[:, :, :], l3, wide(one), ALU.subtract))
                dve.wait_ge(consts_in, 32)
                if actor is not None:
                    a3 = actor[:, :, :].rearrange("q g (t k) -> q (g t) k", k=MAX_K)
                    link(nc.vector.tensor_scalar(a3, a3, 30.0, -30.0, ALU.min, ALU.max))
                    link(nc.vector.tensor_reduce(best[:, :], a3, AX_X, ALU.max))
                    link(nc.vector.tensor_tensor(a3, a3, wide(best, MAX_K), ALU.is_equal))
                    link(nc.vector.tensor_tensor(a3, a3, first[:, :].unsqueeze(1).broadcast_to([P, B, MAX_K]), ALU.mult))
                    link(nc.vector.tensor_reduce(allowed[:, :], a3, AX_X, ALU.min))
                    link(nc.vector.tensor_scalar(allowed[:, :], allowed[:, :], MAX_K + 1.0, None, ALU.add))
                else:
                    link(nc.vector.memset(allowed[:, :], float(TOP_K)))
                dve.wait_ge(exped, 1)
                link(nc.vector.tensor_reduce(total[:, :], probs[:, :, :], AX_X, ALU.add))
                link(nc.vector.reciprocal(one[:, :], total[:, :]))
                link(nc.vector.tensor_tensor(probs[:, :, :], probs[:, :, :], wide(one), ALU.mult))
                link(nc.vector.tensor_copy(rank[:, :, :], after[:, :].unsqueeze(1).broadcast_to([P, B, NE])))
                for d in range(1, NE):
                    ge, front, back = cmp_[:, :, 0:NE - d], slice(0, NE - d), slice(d, NE)
                    link(nc.vector.tensor_tensor(ge, probs[:, :, front], probs[:, :, back], ALU.is_ge))
                    link(nc.vector.tensor_tensor(rank[:, :, front], rank[:, :, front], ge, ALU.subtract))
                    link(nc.vector.tensor_tensor(rank[:, :, back], rank[:, :, back], ge, ALU.add))
                link(nc.vector.tensor_tensor(rank[:, :, :], rank[:, :, :], wide(allowed), ALU.is_lt))
                link(nc.vector.tensor_tensor(probs[:, :, :], probs[:, :, :], rank[:, :, :], ALU.mult))
                if actor is None:
                    link(nc.vector.tensor_reduce(total[:, :], probs[:, :, :], AX_X, ALU.add))
                    link(nc.vector.tensor_scalar(total[:, :], total[:, :], 1e-8, None, ALU.add))
                    link(nc.vector.reciprocal(one[:, :], total[:, :]))
                    link(nc.vector.tensor_tensor(probs[:, :, :], probs[:, :, :], wide(one), ALU.mult))
                flat = [t[:, :, :].rearrange("q n e -> q (n e)") for t in (scores[:, :, :, 0], probs)]
                link(nc.vector.tensor_scalar(flat[0], flat[1], gate, 1.0 / WSCALE, ALU.mult, ALU.mult))


def experts(nc, name, B, x_high, x_low, x_all, scores, w_in, w_down, rows, per, lag, banks, out=None, stats=None):
    G, M = B // GB, NE * per
    with ExitStack() as ctx:
        def sb(n, s, d=F32):
            return [ctx.enter_context(nc.sbuf_tensor(f"{name}_{n}{k}", s, d)) for k in range(RING)]

        def ps(n, k):
            return [ctx.enter_context(nc.psum_tensor(f"{name}_{n}{p}", [P, GT], F32)) for p in range(k)]

        def sem(n):
            return ctx.enter_context(nc.semaphore(f"{name}_{n}"))

        act_out, hidden = sb("act_out", [rows, GT]), sb("hidden", [rows, GT])
        high, low = sb("high", [rows, GT], F16), sb("low", [rows, GT], F16)
        in_ps = [ps(f"in{k}_", banks) for k in range(len(w_in))]
        y_ps = ps("y", 2)
        in_ready, act_ready, hidden_ready = sem("in_ready"), sem("act_ready"), sem("hidden_ready")
        high_ready, low_ready, down_done = sem("high_ready"), sem("low_ready"), sem("down_done")
        x_ready, x_stored, stats_ready = sem("x_ready"), sem("x_stored"), sem("stats_ready")
        gated = len(w_in) == 2

        def groups(eng, body):
            body(0)
            with eng.Fori(1, G) as g:
                body(g)

        def late(g, m, by, body):
            if m >= by:
                body(g, m - by)
            elif not isinstance(g, int) or g > 0:
                body(g - 1, m - by + M)

        with nc.Block(name=name) as block:
            @block.tensor
            def _(pe):
                def project(g, m):
                    for k, (wh, wl) in enumerate(w_in):
                        if k == 0:
                            wait(pe, hidden_ready, M * g + m + 1 - banks)
                        dst, own = in_ps[k][m % banks][0:rows, :], slice(rows * m, rows * (m + 1))
                        nc.tensor.matmul(dst, wh[:, 0, own], x_high[:, g, :], start=True, stop=False)
                        nc.tensor.matmul(dst, wl[:, 0, own], x_high[:, g, :], start=False, stop=False)
                        mm = nc.tensor.matmul(dst, wh[:, 0, own], x_low[:, g, :], start=False, stop=True)
                    mm.then_inc(in_ready, 1)

                def down(g, m):
                    e, c = m // per, m % per
                    wait(pe, low_ready, M * g + m + 1)
                    if c == 0:
                        wait(pe, x_ready, NE * g + e - 1)
                    for t in range(GB):
                        own, dst = slice(P * t, P * (t + 1)), y_ps[e % 2][:, D * t:D * (t + 1)]
                        parts = [(high, 0), (high, 1), (low, 0)]
                        for k, (h, part) in enumerate(parts):
                            mm = nc.tensor.matmul(dst, h[m % RING][:, own], w_down[part][:, m, :],
                                                  start=(c == 0 and t == 0 and k == 0), stop=(c == per - 1 and k == 2),
                                                  skip_group_check=True)
                    mm.then_inc(down_done, 1)

                def group(g):
                    for m in range(M):
                        project(g, m)
                        late(g, m, lag, down)

                groups(pe, group)
                for m in range(M - lag, M):
                    down(G - 1, m)

            @block.scalar
            def _(act):
                def split(g, m):
                    wait(act, hidden_ready, M * g + m + 1)
                    wait(act, down_done, M * g + m + 1 - RING)
                    nc.scalar.activation(high[m % RING][:, :], hidden[m % RING][:, :], ACT.Copy).then_inc(high_ready, 1)

                def group(g):
                    for m in range(M):
                        wait(act, in_ready, M * g + m + 1)
                        wait(act, hidden_ready, M * g + m + 1 - RING)
                        func, scale = (ACT.Silu, 1.0 / WSCALE) if gated else (ACT.Relu, 1.0 / WSCALE ** 2)
                        nc.scalar.activation(act_out[m % RING][:, :], in_ps[0][m % banks][0:rows, :], func,
                                             scale=scale).then_inc(act_ready, 1)
                        late(g, m, 1, split)

                groups(act, group)
                split(G - 1, M - 1)

            @block.vector
            def _(dve):
                def accumulate(g, e):
                    wait(dve, down_done, M * g + per * (e + 1))
                    for t in range(GB):
                        n = GB * g + t
                        wait(dve, x_ready, NE * g + e)
                        last = nc.vector.scalar_tensor_tensor(
                            out=x_all[:, n, :], in0=y_ps[e % 2][:, D * t:D * (t + 1)], scalar=scores[:, n, e, :],
                            in1=x_all[:, n, :], op0=ALU.mult, op1=ALU.add)
                    last.then_inc(x_ready, 1)
                    if e == NE - 1 and stats is not None:
                        wait(dve, x_ready, NE * (g + 1))
                        for t in range(GB):
                            n = GB * g + t
                            last = nc.vector.bn_stats(stats[:, n, :], x_all[:, n, :])
                        last.then_inc(stats_ready, 1)

                def finish(g, m):
                    if m % per == per - 1:
                        accumulate(g, m // per)

                def group(g):
                    for m in range(M):
                        k = m % RING
                        wait(dve, act_ready, M * g + m + 1)
                        wait(dve, low_ready, M * g + m + 1 - RING)
                        dst, a = hidden[k][:, :], act_out[k][:, :]
                        src = in_ps[-1][m % banks][0:rows, :]
                        scalar, op = (1.0 / WSCALE, ALU.mult) if gated else (0.0, ALU.max)
                        nc.vector.scalar_tensor_tensor(out=dst, in0=src, scalar=scalar, in1=a, op0=op,
                                                       op1=ALU.mult).then_inc(hidden_ready, 1)
                        late(g, m, lag + 1, finish)

                groups(dve, group)
                for m in range(M - lag - 1, M):
                    finish(G - 1, m)

            @block.gpsimd
            def _(pool):
                def group(g):
                    for m in range(M):
                        k = m % RING
                        wait(pool, high_ready, M * g + m + 1)
                        nc.gpsimd.tensor_tensor(low[k][:, :], hidden[k][:, :], high[k][:, :],
                                                ALU.subtract).then_inc(low_ready, 1)

                groups(pool, group)

            if out is not None:
                @block.sync
                def _(sp):
                    def group(g):
                        wait(sp, x_ready, NE * (g + 1))
                        for t in range(GB):
                            sp.dma_start(out[GB * g + t], x_all[:, GB * g + t, :]).then_inc(x_stored, 16)

                    groups(sp, group)
                    sp.wait_ge(x_stored, 16 * B)


def relative_attention(nc, B, io, x_all, stats, mean, rstd, ident, gates, q_dram, r_dram):
    with ExitStack() as ctx:
        def sb(n, s, d=F32):
            return ctx.enter_context(nc.sbuf_tensor("a1_" + n, s, d))

        def parts(n, s):
            return [sb(f"{n}_{k}", s, F16) for k in ("high", "low")]

        def ps(n):
            return ctx.enter_context(nc.psum_tensor("a1_" + n, [P, 512], F32))

        def sem(n):
            return ctx.enter_context(nc.semaphore("a1_" + n))

        w_q, w_rows, w_k, w_v = (parts(n, [P, 1, D]) for n in ("w_q", "w_rows", "w_k", "w_v"))
        key_table, value_table = parts("key_table", [QC * QB, 1, KT]), parts("value_table", [KC, P, HD])
        ctx_t = parts("ctx_t", [P, B, KC])
        quarters = [slice(k * B // 4, (k + 1) * B // 4) for k in range(4)]
        split_float16(nc, "split_a1", [(io["ctx"][:, own, :], ctx_t[0][:, own, :], ctx_t[1][:, own, :], 1.0)
                                       for own in quarters] +
                      [(src, t[0][:, :, :], t[1][:, :, :], 1.0)
                       for src, t in ((io["w_q"].unsqueeze(1), w_q), (io["w_rows"].unsqueeze(1), w_rows),
                                      (io["w_k"].unsqueeze(1), w_k), (io["w_v"].unsqueeze(1), w_v),
                                      (io["key_table"].unsqueeze(1), key_table), (io["value_table"], value_table))])

        w_o, w_out = sb("w_o", [P, D]), parts("w_out", [P, D])
        b_q, b_k, b_v, b_o = sb("b_q", [P, 1]), sb("b_k", [P, 1]), sb("b_v", [P, P]), sb("b_o", [P, D])
        b_rows, head_mask, high_rows = sb("b_rows", [P, D]), sb("head_mask", [P, NH]), sb("high_rows", [P, 1])
        xn = [sb(f"xn{p}", [P, D]) for p in range(2)]
        xt = [parts(f"xt{p}", [P, P]) for p in range(2)]
        q_t = [parts(f"q_t{p}", [P, P]) for p in range(2)]
        k_t = [parts(f"k_t{p}", [P, KC]) for p in range(2)]
        value = [parts(f"value{p}", [KC, NH, HD + 1]) for p in range(2)]
        q_rows = [sb(f"q_rows{p}", [P, D]) for p in range(2)]
        q_parts = [sb(f"q_parts{p}", [P, 2, D], F16) for p in range(2)]
        q_head = [parts(f"q_head{p}", [P, P, NH]) for p in range(2)]
        q_pos = [sb(f"q_pos{p}", [QC * QB, QG, QC * NH], F16) for p in range(2)]
        prob_t = [parts(f"prob_t{p}", [KC, QG, P]) for p in range(2)]
        rel_all = [sb(f"rel_all{p}", [P, QG, QC * HD]) for p in range(2)]
        rel = [sb(f"rel{p}", [P, NH, HD]) for p in range(2)]
        mixed = [sb(f"mixed{p}", [P, NH, HD]) for p in range(2)]
        rden = [sb(f"rden{p}", [P, NH]) for p in range(2)]
        mixed_t = [parts(f"mixed_t{p}", [P, P]) for p in range(2)]
        top = [sb(f"top{k}", [P, 4]) for k in range(4)]
        prob = [sb(f"prob{k}", [P, 4, KC]) for k in range(4)]

        score_ps = [ps(f"score{k}") for k in range(2)]
        trans_ps = [ps(f"trans{k}") for k in range(2)]
        prep_ps, rel_ps, mix_ps, fin_ps = ps("prep"), ps("rel"), ps("mix"), ps("fin")
        Q_COLS, K_COLS, V_COLS, ROW_COLS = slice(0, P), slice(P, P + KC), slice(256, 256 + D), slice(384, 384 + D)

        q_written = [t.rearrange("(q r) -> q r", r=Q_STEP)[:, 0:QC * QB * NH]
                     .rearrange("q (b w) -> q b w", w=QC * NH)[:, :, 0:NH] for t in q_dram]
        q_read = [t.rearrange("(g r) -> g r", r=Q_PITCH)[:, 0:QC * QC * QB * NH]
                  .rearrange("g (b w) -> b g w", w=QC * NH) for t in q_dram]
        r_written = [t.rearrange("(g r) -> g r", r=R_PITCH)[:, 0:P * QC * HD]
                     .rearrange("g (b w) -> b g w", w=QC * HD) for t in r_dram]
        r_read = [t.rearrange("(q r) -> q r", r=R_STEP)[:, 0:NH * QC * HD]
                  .rearrange("q (h w) -> q h w", w=QC * HD)[:, :, 0:HD] for t in r_dram]

        weights_in, weights_ready, bias_ready = sem("weights_in"), sem("weights_ready"), sem("bias_ready")
        w_out_high, w_out_low, table_ready = sem("w_out_high"), sem("w_out_low"), sem("table_ready")
        cleared, q_zeroed = sem("cleared"), sem("q_zeroed")
        q_out, q_in, r_out, r_in = ([sem(f"{n}{p}") for p in range(2)] for n in ("q_out", "q_in", "r_out", "r_in"))
        xn_ready, xn_t = sem("xn_ready"), sem("xn_t")
        xt_high, xt_low = sem("xt_high"), sem("xt_low")
        proj_ready, proj_high, proj_low = sem("proj_ready"), sem("proj_high"), sem("proj_low")
        rows_ready, rows_high, rows_low, q_head_ready = (sem(n) for n in ("rows", "rows_high", "rows_low", "q_head"))
        score_ready, top_ready, shifted, exped = sem("score_ready"), sem("top_ready"), sem("shifted"), sem("exped")
        prob_ready, prob_high, prob_low = sem("prob_ready"), sem("prob_high"), sem("prob_low")
        rel_ready, rel_copied = sem("rel_ready"), sem("rel_copied")
        mix_ready, rden_ready, divided = sem("mix_ready"), sem("rden_ready"), sem("divided")
        rel_divided, mixed_ready = sem("rel_divided"), sem("mixed_ready")
        mixed_turned, mixed_high, mixed_low = sem("mixed_turned"), sem("mixed_high"), sem("mixed_low")
        y_ready, x_biased, x_ready, stats_ready = sem("y_ready"), sem("x_biased"), sem("x_ready"), sem("stats_ready")

        FIRST, LO, HI, LAST = -3, 4, B - 4, B + 3
        WEIGHTS = [(w_o, "w_o"), (b_q, "b_q"), (b_k, "b_k"), (b_v, "b_v"), (b_o, "b_o"), (b_rows, "b_rows"),
                   (head_mask, "head_mask16"), (high_rows, "high_rows")]

        def products(a, b):
            return [(a[0], b[0]), (a[0], b[1]), (a[1], b[0])]

        with nc.Block(name="a1") as block:
            @block.sync
            def _(sp):
                for t, src in WEIGHTS:
                    sp.dma_start(t[:, :], io[src]).then_inc(weights_in, 16)
                sp.wait_ge(cleared, 1)
                for p in range(2):
                    sp.dma_start(q_read[p], q_pos[p][:, :, :]).then_inc(q_zeroed, 16)
                sp.wait_ge(q_zeroed, 32)

                def write_queries(n, p):
                    if inside(n, 0, B):
                        wait(sp, rows_low, n + 1)
                        sp.dma_start(q_written[p], q_parts[p][:, :, :].rearrange("q a (d h) -> q (a d) h", d=HD)
                                     ).then_inc(q_out[p], 16)

                def write_relative(n, p):
                    if inside(n, 0, B):
                        wait(sp, rel_copied, 4 * n + 4)
                        sp.dma_start(r_written[p], rel_all[p][:, :, :]).then_inc(r_out[p], 16)

                def read_relative(n, p):
                    if inside(n, 0, B):
                        wait(sp, r_out[p], (n - p) * 8 + 16)
                        sp.dma_start(rel[p][:, :, :], r_read[p]).then_inc(r_in[p], 16)

                def slot(n, p):
                    read_relative(n - 2, p)
                    write_queries(n + 2, p)
                    write_relative(n - 1, 1 - p)

                slots(sp, FIRST, LO, HI, LAST, slot)

            @block.tensor
            def _(pe):
                def prep_turn(n, p):
                    if inside(n, 0, B):
                        wait(pe, xn_ready, n + 1)
                        wait(pe, proj_low, n)
                        nc.tensor.transpose(prep_ps[:, 0:P], xn[p][:, :], ident[:, :]).then_inc(xn_t, 1)

                def project(n, p):
                    if inside(n, -2, B):
                        wait(pe, proj_low, n + 2)
                        chain = []
                        if inside(n + 1, 0, B):
                            chain.append((prep_ps[:, K_COLS], [w[:, 0, :] for w in w_k], [t[:, n + 1, :] for t in ctx_t]))
                        if inside(n, 0, B):
                            chain.append((prep_ps[0:KC, V_COLS], [t[:, n, :] for t in ctx_t], [w[:, 0, :] for w in w_v]))
                        if inside(n + 2, 0, B):
                            wait(pe, xt_low, n + 3)
                            x_t = [t[:, :] for t in xt[p]]
                            chain.append((prep_ps[:, Q_COLS], [w[:, 0, :] for w in w_q], x_t))
                            chain.append((prep_ps[:, ROW_COLS], x_t, [w[:, 0, :] for w in w_rows]))
                        for dst, a, b in chain:
                            for k, (lhs, rhs) in enumerate(products(a, b)):
                                mm = nc.tensor.matmul(dst, lhs, rhs, start=(k == 0), stop=(k == 2))
                        mm.then_inc(proj_ready, 1)

                def scores(n, p, u):
                    if inside(n, 0, B):
                        if u == 0:
                            wait(pe, q_head_ready, 2 * n + 2)
                            wait(pe, proj_low, n + 2)
                            wait(pe, q_in[p], (n - p) * 8 + 16)
                        wait(pe, shifted, 4 * n + u - 1)
                        for j in range(4):
                            g = 4 * u + j
                            dst, window = score_ps[u % 2][:, KC * j:KC * (j + 1)], slice(KT - KC - QC * g, KT - QC * g)
                            for k, (q, t) in enumerate(products(q_head[p], k_t[p])):
                                nc.tensor.matmul(dst, q[:, QC * g:QC * (g + 1), :], t[:, :], start=(k == 0), stop=False)
                            for k in range(2):
                                mm = nc.tensor.matmul(dst, q_pos[p][:, g, :], key_table[k][:, 0, window],
                                                      start=False, stop=(k == 1))
                        mm.then_inc(score_ready, 1)

                def turn(n, u):
                    if inside(n, 0, B):
                        wait(pe, exped, 4 * n + u + 1)
                        wait(pe, prob_low, 4 * n + u - 1)
                        for j in range(4):
                            mm = nc.tensor.transpose(trans_ps[u % 2][0:KC, P * j:P * (j + 1)], prob[u][:, j, :],
                                                     ident[:, :])
                        mm.then_inc(prob_ready, 1)

                def relative(n, p, u):
                    if inside(n, 0, B):
                        wait(pe, prob_low, 4 * n + u + 1)
                        wait(pe, rel_copied, 4 * n + u)
                        for j in range(4):
                            g = 4 * u + j
                            for k, (pr, t) in enumerate(products(prob_t[p], value_table)):
                                mm = nc.tensor.matmul(rel_ps[:, QC * HD * j:QC * HD * (j + 1)], pr[:, g, :],
                                                      t[:, QC * g:QC * (g + 1), :], start=(k == 0), stop=(k == 2))
                        mm.then_inc(rel_ready, 1)

                def mix(n, p, half):
                    if inside(n, 0, B):
                        if half == 0:
                            wait(pe, prob_low, 4 * n + 4)
                            wait(pe, proj_low, n + 3)
                            wait(pe, divided, n)
                        by_head = [t[:, :, :].rearrange("k g (c h) -> k (g c) h", h=NH) for t in prob_t[p]]
                        for h in range(8 * half, 8 * half + 8):
                            for k, (pr, v) in enumerate(products(by_head, value[p])):
                                mm = nc.tensor.matmul(mix_ps[:, (HD + 1) * h:(HD + 1) * (h + 1)], pr[:, :, h],
                                                      v[:, h, :], start=(k == 0), stop=(k == 2))
                        if half == 1:
                            mm.then_inc(mix_ready, 1)

                def fin_turn(n, p):
                    if inside(n, 0, B):
                        wait(pe, mixed_ready, n + 1)
                        wait(pe, x_ready, n)
                        nc.tensor.transpose(fin_ps[:, 0:P], mixed[p][:, :, :].rearrange("q h d -> q (h d)"),
                                            ident[:, :]).then_inc(mixed_turned, 1)

                def fin_project(n, p):
                    if inside(n, 0, B):
                        wait(pe, mixed_low, n + 1)
                        for k, (m, w) in enumerate(products(mixed_t[p], w_out)):
                            mm = nc.tensor.matmul(fin_ps[:, 0:D], m[:, :], w[:, :], start=(k == 0), stop=(k == 2))
                        mm.then_inc(y_ready, 1)

                def slot(n, p):
                    o = 1 - p
                    scores(n, p, 0)
                    turn(n - 1, 2)
                    relative(n - 1, o, 1)
                    project(n, p)
                    scores(n, p, 1)
                    turn(n - 1, 3)
                    relative(n - 1, o, 2)
                    fin_turn(n - 3, o)
                    scores(n, p, 2)
                    turn(n, 0)
                    relative(n - 1, o, 3)
                    mix(n - 1, o, 0)
                    scores(n, p, 3)
                    turn(n, 1)
                    fin_project(n - 3, o)
                    mix(n - 1, o, 1)
                    relative(n, p, 0)
                    prep_turn(n + 3, o)

                pe.wait_ge(weights_ready, 2)
                nc.tensor.matmul(fin_ps[:, 0:D], b_v[:, :], w_o[:, :], start=True, stop=True).then_inc(bias_ready, 1)
                pe.wait_ge(weights_ready, 3)
                pe.wait_ge(w_out_low, 1)
                pe.wait_ge(table_ready, 1)
                slots(pe, FIRST, LO, HI, LAST, slot)

            @block.scalar
            def _(act):
                act.wait_ge(weights_in, 16 * len(WEIGHTS))
                act.wait_ge(weights_ready, 1)
                nc.scalar.activation(w_out[0][:, :], w_o[:, :], ACT.Copy).then_inc(w_out_high, 1)

                def read_queries(n, p):
                    if inside(n, 0, B):
                        wait(act, q_out[p], (n - p) * 8 + 16)
                        wait(act, score_ready, 4 * n - 4)
                        act.dma_start(q_pos[p][:, :, :], q_read[p]).then_inc(q_in[p], 16)

                def copy_xn(n, p):
                    if inside(n, 0, B):
                        wait(act, xn_t, n + 1)
                        wait(act, proj_ready, n - 1)
                        nc.scalar.activation(xt[p][0][:, :], prep_ps[:, 0:P], ACT.Copy).then_inc(xt_high, 1)

                def high_parts(n, p):
                    o = 1 - p
                    if inside(n, -2, B):
                        wait(act, proj_ready, n + 3)
                        if inside(n + 1, 0, B):
                            wait(act, score_ready, 4 * n)
                            last = nc.scalar.activation(k_t[o][0][:, :], prep_ps[:, K_COLS], ACT.Identity,
                                                        bias=b_k[:, 0:1])
                        if inside(n, 0, B):
                            wait(act, mix_ready, n - 1)
                            last = nc.scalar.activation(value[p][0][:, :, 0:HD],
                                                        prep_ps[0:KC, V_COLS].rearrange("k (h d) -> k h d", d=HD),
                                                        ACT.Copy)
                        if inside(n + 2, 0, B):
                            wait(act, q_head_ready, 2 * n + 2)
                            last = nc.scalar.activation(q_t[p][0][:, :], prep_ps[:, Q_COLS], ACT.Identity,
                                                        bias=b_q[:, 0:1])
                        last.then_inc(proj_high, 1)

                def high_rows_of(n, p):
                    if inside(n, 0, B):
                        wait(act, rows_ready, n + 1)
                        wait(act, q_out[p], (n - p) * 8)
                        nc.scalar.activation(q_parts[p][:, 0, :], q_rows[p][:, :], ACT.Copy).then_inc(rows_high, 1)

                def exp(n, u):
                    if inside(n, 0, B):
                        wait(act, shifted, 4 * n + u + 1)
                        nc.scalar.activation(prob[u][:, :, :], prob[u][:, :, :], ACT.Exp,
                                             scale=float(HD) ** -0.5).then_inc(exped, 1)

                def high_prob(n, p, u):
                    if inside(n, 0, B):
                        wait(act, prob_ready, 4 * n + u + 1)
                        wait(act, rel_ready, 4 * n + u - 7)
                        wait(act, mix_ready, n - 1)
                        nc.scalar.activation(prob_t[p][0][:, 4 * u:4 * u + 4, :],
                                             trans_ps[u % 2][0:KC, :].rearrange("k (g r) -> k g r", g=4),
                                             ACT.Copy).then_inc(prob_high, 1)

                def copy_relative(n, p, u):
                    if inside(n, 0, B):
                        wait(act, rel_ready, 4 * n + u + 1)
                        if u == 0:
                            wait(act, r_out[p], (n - p) * 8)
                            wait(act, r_in[p], (n - p) * 8)
                        nc.scalar.activation(rel_all[p][:, 4 * u:4 * u + 4, :].rearrange("r g w -> r (g w)"),
                                             rel_ps[:, 0:4 * QC * HD], ACT.Copy).then_inc(rel_copied, 1)

                def high_mixed(n, p):
                    if inside(n, 0, B):
                        wait(act, mixed_turned, n + 1)
                        wait(act, y_ready, n - 1)
                        nc.scalar.activation(mixed_t[p][0][:, :], fin_ps[:, 0:P], ACT.Copy).then_inc(mixed_high, 1)

                def slot(n, p):
                    o = 1 - p
                    read_queries(n + 1, o)
                    high_prob(n - 1, o, 2)
                    copy_relative(n - 1, o, 1)
                    exp(n, 0)
                    high_parts(n, p)
                    high_prob(n - 1, o, 3)
                    copy_relative(n - 1, o, 2)
                    exp(n, 1)
                    high_rows_of(n + 2, p)
                    high_mixed(n - 3, o)
                    high_prob(n, p, 0)
                    copy_relative(n - 1, o, 3)
                    exp(n, 2)
                    high_prob(n, p, 1)
                    copy_relative(n, p, 0)
                    exp(n, 3)
                    copy_xn(n + 3, o)

                slots(act, FIRST, LO, HI, LAST, slot)

            @block.gpsimd
            def _(pool):
                for p in range(2):
                    for k in range(2):
                        nc.gpsimd.memset(value[p][k][:, :, HD:HD + 1], 1.0 - k)
                    last = nc.gpsimd.memset(q_pos[p][:, :, :], 0.0)
                last.then_inc(cleared, 1)
                pool.wait_ge(weights_ready, 3)

                def slot(n, p):
                    o = 1 - p
                    if inside(n + 1, 0, B):
                        wait(pool, proj_low, n + 2)
                        wait(pool, score_ready, 4 * n)
                        for k in range(2):
                            nc.gpsimd.tensor_tensor(q_head[o][k][:, :, :],
                                                    q_t[o][k][:, :].unsqueeze(2).broadcast_to([P, P, NH]),
                                                    head_mask[:, :].unsqueeze(1).broadcast_to([P, P, NH]),
                                                    ALU.mult).then_inc(q_head_ready, 1)
                    if inside(n, 0, B):
                        wait(pool, xn_ready, n + 1)
                        nc.gpsimd.tensor_tensor(x_all[:, n, :], x_all[:, n, :], b_o[:, :], ALU.add).then_inc(x_biased, 1)

                slots(pool, -1, LO, HI, B, slot)

            @block.vector
            def _(dve):
                dve.wait_ge(weights_in, 16 * len(WEIGHTS))
                nc.vector.tensor_scalar(w_o[:, :], w_o[:, :], gates[:, 2:3], None, ALU.mult).then_inc(weights_ready, 1)
                nc.vector.tensor_scalar(b_o[:, :], b_o[:, :], gates[:, 2:3], None, ALU.mult).then_inc(weights_ready, 1)
                nc.vector.tensor_scalar(key_table[1][:, 0, :], key_table[1][:, 0, :], high_rows[:, 0:1], None,
                                        ALU.mult).then_inc(table_ready, 1)
                dve.wait_ge(weights_ready, 2)
                dve.wait_ge(w_out_high, 1)
                nc.vector.tensor_tensor(w_out[1][:, :], w_o[:, :], w_out[0][:, :], ALU.subtract).then_inc(w_out_low, 1)
                dve.wait_ge(bias_ready, 1)
                nc.vector.tensor_tensor(b_o[:, :], b_o[:, :], fin_ps[:, 0:D], ALU.add).then_inc(weights_ready, 1)

                def normalize(n, p):
                    if inside(n, 0, B):
                        wait(dve, xn_t, n - 1)
                        nc.vector.tensor_scalar(xn[p][:, :], x_all[:, n, :], mean[:, n, :], rstd[:, n, :],
                                                ALU.subtract, ALU.mult).then_inc(xn_ready, 1)

                def low_xn(n, p):
                    if inside(n, 0, B):
                        wait(dve, xt_high, n + 1)
                        nc.vector.tensor_tensor(xt[p][1][:, :], prep_ps[:, 0:P], xt[p][0][:, :],
                                                ALU.subtract).then_inc(xt_low, 1)

                def low_parts(n, p):
                    o = 1 - p
                    if inside(n, -2, B):
                        wait(dve, proj_high, n + 3)
                        if inside(n + 2, 0, B):
                            wait(dve, rows_high, n + 1)
                            nc.vector.tensor_tensor(q_rows[p][:, :], prep_ps[:, ROW_COLS], b_rows[:, :],
                                                    ALU.add).then_inc(rows_ready, 1)
                            last = nc.vector.scalar_tensor_tensor(
                                out=q_t[p][1][:, :], in0=prep_ps[:, Q_COLS], scalar=b_q[:, 0:1], in1=q_t[p][0][:, :],
                                op0=ALU.add, op1=ALU.subtract)
                        if inside(n + 1, 0, B):
                            last = nc.vector.scalar_tensor_tensor(
                                out=k_t[o][1][:, :], in0=prep_ps[:, K_COLS], scalar=b_k[:, 0:1], in1=k_t[o][0][:, :],
                                op0=ALU.add, op1=ALU.subtract)
                        if inside(n, 0, B):
                            last = nc.vector.tensor_tensor(value[p][1][:, :, 0:HD],
                                                           prep_ps[0:KC, V_COLS].rearrange("k (h d) -> k h d", d=HD),
                                                           value[p][0][:, :, 0:HD], ALU.subtract)
                        last.then_inc(proj_low, 1)

                def low_rows_of(n, p):
                    if inside(n, 0, B):
                        wait(dve, rows_high, n + 1)
                        nc.vector.tensor_tensor(q_parts[p][:, 1, :], q_rows[p][:, :], q_parts[p][:, 0, :],
                                                ALU.subtract).then_inc(rows_low, 1)

                def softmax_shift(n, u):
                    if inside(n, 0, B):
                        s = score_ps[u % 2][:, 0:4 * KC].rearrange("r (g k) -> r g k", g=4)
                        wait(dve, score_ready, 4 * n + u + 1)
                        nc.vector.tensor_reduce(top[u][:, :], s, AX_X, ALU.max).then_inc(top_ready, 1)
                        wait(dve, top_ready, 4 * n + u + 1)
                        wait(dve, prob_ready, 4 * n + u - 3)
                        nc.vector.tensor_tensor(prob[u][:, :, :], s, top[u][:, :].unsqueeze(2).broadcast_to([P, 4, KC]),
                                                ALU.subtract).then_inc(shifted, 1)

                def low_prob(n, p, u):
                    if inside(n, 0, B):
                        wait(dve, prob_high, 4 * n + u + 1)
                        own = [t[:, 4 * u:4 * u + 4, :].rearrange("k g r -> k (g r)") for t in prob_t[p]]
                        nc.vector.tensor_tensor(own[1], trans_ps[u % 2][0:KC, :], own[0],
                                                ALU.subtract).then_inc(prob_low, 1)

                def low_mixed(n, p):
                    if inside(n, 0, B):
                        wait(dve, mixed_high, n + 1)
                        nc.vector.tensor_tensor(mixed_t[p][1][:, :], fin_ps[:, 0:P], mixed_t[p][0][:, :],
                                                ALU.subtract).then_inc(mixed_low, 1)

                def divide(n, p):
                    if inside(n, 0, B):
                        m = mix_ps[:, 0:NH * (HD + 1)].rearrange("q (h d) -> q h d", h=NH)
                        wait(dve, mix_ready, n + 1)
                        nc.vector.reciprocal(rden[p][:, :], m[:, :, HD]).then_inc(rden_ready, 1)
                        wait(dve, rden_ready, n + 1)
                        wait(dve, mixed_turned, n - 1)
                        nc.vector.tensor_tensor(mixed[p][:, :, :], m[:, :, 0:HD],
                                                rden[p][:, :].unsqueeze(2).broadcast_to([P, NH, HD]),
                                                ALU.mult).then_inc(divided, 1)

                def add_relative(n, p):
                    if inside(n, 0, B):
                        wait(dve, r_in[p], (n - p) * 8 + 16)
                        nc.vector.tensor_tensor(rel[p][:, :, :], rel[p][:, :, :],
                                                rden[p][:, :].unsqueeze(2).broadcast_to([P, NH, HD]),
                                                ALU.mult).then_inc(rel_divided, 1)
                        wait(dve, rel_divided, n + 1)
                        wait(dve, divided, n + 1)
                        nc.vector.tensor_tensor(mixed[p][:, :, :], mixed[p][:, :, :], rel[p][:, :, :],
                                                ALU.add).then_inc(mixed_ready, 1)

                def residual(n):
                    if inside(n, 0, B):
                        wait(dve, y_ready, n + 1)
                        wait(dve, x_biased, n + 1)
                        nc.vector.tensor_tensor(x_all[:, n, :], x_all[:, n, :], fin_ps[:, 0:D],
                                                ALU.add).then_inc(x_ready, 1)

                def statistics(n):
                    if inside(n, 0, B):
                        wait(dve, x_ready, n + 1)
                        nc.vector.bn_stats(stats[:, n, :], x_all[:, n, :]).then_inc(stats_ready, 1)

                def slot(n, p):
                    o = 1 - p
                    softmax_shift(n, 0)
                    low_prob(n - 1, o, 2)
                    low_parts(n, p)
                    divide(n - 2, p)
                    softmax_shift(n, 1)
                    low_prob(n - 1, o, 3)
                    normalize(n + 3, o)
                    low_rows_of(n + 2, p)
                    softmax_shift(n, 2)
                    low_mixed(n - 3, o)
                    low_prob(n, p, 0)
                    softmax_shift(n, 3)
                    low_prob(n, p, 1)
                    residual(n - 3)
                    low_xn(n + 3, o)
                    add_relative(n - 2, p)
                    statistics(n - 3)

                slots(dve, FIRST, LO, HI, LAST, slot)


def flamingo_kernel(nc, io, out):
    B = io["x"].shape[0]
    with ExitStack() as ctx:
        def sb(n, s):
            return ctx.enter_context(nc.sbuf_tensor(n, s, F32))

        x_all = sb("x_all", [P, B, D])
        stats, mean, rstd = sb("stats", [P, B, 6]), sb("mean", [P, B, 1]), sb("rstd", [P, B, 1])
        ident, gates = sb("ident", [P, P]), sb("gates", [P, 4])

        consts_in = ctx.enter_context(nc.semaphore("consts_in"))
        gates_ready = ctx.enter_context(nc.semaphore("gates_ready"))
        with nc.Block(name="consts") as block:
            @block.scalar
            def _(act):
                act.dma_start(ident[:, :], io["ident"]).then_inc(consts_in, 16)
                act.dma_start(gates[:, :], io["gates"]).then_inc(consts_in, 16)
                act.wait_ge(consts_in, 32)
                nc.scalar.activation(gates[:, :], gates[:, :], ACT.Tanh).then_inc(gates_ready, 1)

        load_x(nc, B, io["x"], x_all, stats)
        layernorm_constants(nc, "ln0", stats, mean[:, :, 0], rstd[:, :, 0], B)
        feature_attention(nc, B, io, x_all, stats, mean, rstd, ident, gates)
        layernorm_constants(nc, "ln1", stats, mean[:, :, 0], rstd[:, :, 0], B)
        x_high = ctx.enter_context(nc.sbuf_tensor("x_high", [P, B // GB, GT], F16))
        x_low = ctx.enter_context(nc.sbuf_tensor("x_low", [P, B // GB, GT], F16))
        logits, scores = sb("logits", [P, B // GB, GB * NE]), sb("scores", [P, B, NE, 1])
        with ExitStack() as layer:
            def parts(n, s):
                return [layer.enter_context(nc.sbuf_tensor(f"{n}_{k}", s, F16)) for k in ("high", "low")]

            actor = layer.enter_context(nc.sbuf_tensor("actor", [P, B // GB, GB * MAX_K], F32))
            w_gate, w_up = parts("w_gate", [P, 1, NE * I0]), parts("w_up", [P, 1, NE * I0])
            w_down = parts("w_down", [R0, NE * C0, D])
            split_float16(nc, "split0", [(io[src], t[0][:, :, :], t[1][:, :, :], WSCALE)
                                         for src, t in (("gate_w", w_gate), ("up_w", w_up), ("down_w", w_down))])
            router(nc, "r0", B, io, x_all, mean, rstd, ident, x_high, x_low, logits, actor)
            expert_scores(nc, "e0", B, io, logits, actor, scores, gates[:, 1:2])
            experts(nc, "f0", B, x_high, x_low, x_all, scores, [w_gate, w_up], w_down, R0, C0, 3, 3, stats=stats)
        layernorm_constants(nc, "ln2", stats, mean[:, :, 0], rstd[:, :, 0], B)
        q_dram = [nc.dram_tensor(f"queries{p}", [QG * Q_PITCH], F16).ap() for p in range(2)]
        r_dram = [nc.dram_tensor(f"relative_values{p}", [QG * R_PITCH], F32).ap() for p in range(2)]
        relative_attention(nc, B, io, x_all, stats, mean, rstd, ident, gates, q_dram, r_dram)
        layernorm_constants(nc, "ln3", stats, mean[:, :, 0], rstd[:, :, 0], B)
        with ExitStack() as layer:
            def parts(n, s):
                return [layer.enter_context(nc.sbuf_tensor(f"{n}_{k}", s, F16)) for k in ("high", "low")]

            w1, w2 = parts("w1", [P, 1, NE * I1]), parts("w2", [R1, NE * C1, D])
            split_float16(nc, "split1", [(io[src], t[0][:, :, :], t[1][:, :, :], WSCALE)
                                         for src, t in (("w1", w1), ("w2", w2))])
            router(nc, "r1", B, io, x_all, mean, rstd, ident, x_high, x_low, logits)
            expert_scores(nc, "e1", B, io, logits, None, scores, gates[:, 3:4])
            experts(nc, "f1", B, x_high, x_low, x_all, scores, [w1], w2, R1, C1, 4, 4, out=out)


def _layout(np, a):
    B = a["x"].shape[0]
    row = np.arange(P)
    tile = np.tile
    d = {}
    d["x"] = a["x"]
    d["ident"] = np.eye(P, dtype=np.float32)
    d["gates"] = tile(np.stack([a["g_xattn"][0], a["g_ffn"][0], a["g_xattn"][1], a["g_ffn"][1]])[None, :], (P, 1))
    d["ctx"] = a["ctx_1024"].transpose(2, 0, 1)
    d["fm_w"] = tile(a["L0_xattn_fm_w"].T, (NH, 1))
    head = row[:, None] // HD == np.arange(NH)[None, :]
    d["fm_sign"] = np.stack([head, -1.0 * head], axis=2).reshape(P, 2 * NH).astype(np.float32)
    d["fm_b"] = tile(a["L0_xattn_fm_b"], NH)[:, None]
    d["row_sign"] = np.where(row % FD < HD, 1.0, -1.0).astype(np.float32)[:, None]
    d["head_mask"] = (row[:, None] // FD == np.arange(8)[None, :]).astype(np.float32)
    d["fc_w"] = a["L0_xattn_fc_w"].T.reshape(2, P, D).transpose(1, 0, 2)
    d["fc_b"] = tile(a["L0_xattn_fc_b"][None, :], (P, 1))
    d["r0_router"] = a["L0_ffn_router_w"].T
    d["actor_w1"] = a["L0_ffn_actor_w1"].T
    d["actor_b1"] = a["L0_ffn_actor_b1"][:, None]
    d["actor_w2"] = a["L0_ffn_actor_w2"].T
    d["actor_b2"] = tile(a["L0_ffn_actor_b2"][None, :], (P, 1))
    d["experts_after"] = tile(np.arange(NE - 1, -1, -1, dtype=np.float32)[None, :], (P, 1))
    d["first_k"] = tile(np.arange(-MAX_K, 0, dtype=np.float32)[None, :], (P, 1))
    d["gate_w"] = a["L0_ffn_gate_w"].reshape(NE * I0, 1, D).transpose(2, 1, 0)
    d["up_w"] = a["L0_ffn_up_w"].reshape(NE * I0, 1, D).transpose(2, 1, 0)
    d["down_w"] = a["L0_ffn_down_w"].transpose(0, 2, 1).reshape(NE * C0, R0, D).transpose(1, 0, 2)
    d["r1_router"] = a["L1_ffn_Wg"]
    d["w1"] = a["L1_ffn_W1"].transpose(1, 0, 2).reshape(D, 1, NE * I1)
    d["w2"] = a["L1_ffn_W2"].reshape(NE * C1, R1, D).transpose(1, 0, 2)
    for n in "qkvo":
        d[f"w_{n}"] = a[f"L1_xattn_W{n}"]
    d["b_q"], d["b_k"] = a["L1_xattn_bq"][:, None], a["L1_xattn_bk"][:, None]
    by_d = np.arange(D).reshape(NH, HD).T.reshape(D)
    d["w_rows"] = a["L1_xattn_Wq"][:, by_d]
    d["b_rows"] = tile(a["L1_xattn_bq"][by_d][None, :], (P, 1))
    d["high_rows"] = (row % QB < HD).astype(np.float32)[:, None]
    d["b_v"] = tile(a["L1_xattn_bv"][:, None], (1, P))
    d["b_o"] = tile(a["L1_xattn_bo"][None, :], (P, 1))
    d["head_mask16"] = head.astype(np.float32)
    zero = a["L1_xattn_rel_key_table"].shape[0] // 2
    q, k, c, j = np.arange(P), np.arange(KC), np.arange(QC), np.arange(KT)
    keys = a["L1_xattn_rel_key_table"][zero + P - QC + c[:, None] - j[None, :]]
    d["key_table"] = tile(keys.transpose(0, 2, 1)[:, None], (1, 2, 1, 1)).reshape(QC * QB, KT)
    d["value_table"] = a["L1_xattn_rel_value_table"][zero + q[None, :] - k[:, None]]
    return {k: np.ascontiguousarray(v) for k, v in d.items()}


def kernel(**inputs):
    import numpy as np
    import concourse.bacc as bacc
    from concourse.bass_utils import run_bass_kernel_spmd as run

    arrays = _layout(np, {k: np.asarray(v) for k, v in inputs.items()})
    nc = bacc.Bacc("TRN2", target_bir_lowering=False, num_devices=1)
    io = {k: nc.dram_tensor(f"in_{k}", v.shape, mybir.dt.from_np(v.dtype), kind="ExternalInput").ap()
          for k, v in arrays.items()}
    out = nc.dram_tensor("out_x", arrays["x"].shape, F32, kind="ExternalOutput").ap()
    flamingo_kernel(nc, io, out)
    r = run(nc, [{f"in_{k}": v for k, v in arrays.items()}], core_ids=[0])
    return r.results[0]["out_x"]
```

```python
from contextlib import ExitStack

import concourse.bass as bass
from concourse import mybir

F32 = mybir.dt.float32
F16 = mybir.dt.float16
ALU = mybir.AluOpType
ACT = mybir.ActivationFunctionType
AX_X = mybir.AxisListType.X

P = 128
D = 128
KC = 77
NH = 16
HD = D // NH
VSCALE = 1 / 8
FD = 2 * HD
HQ = 4
QW = HQ * KC
EPS = 1e-5

QC = 8
QG = P // QC
KT = KC + P - QC
QB = 2 * HD
Q_STEP = QC * QB * NH + NH
Q_PITCH = QC * Q_STEP

NE = 8
GB = 4
GT = GB * P
AH = 50
MAX_K = 6
TOP_K = 2
I0, R0, C0 = 336, 112, 3
I1, R1, C1 = 256, 128, 2
WSCALE = 256.0
RING = 8


def wait(eng, sem, value):
    if isinstance(value, int) and value <= 0:
        return
    eng.wait_ge(sem, value)


def inside(n, lo, hi):
    return lo <= n < hi if isinstance(n, int) else True


def slots(eng, first, lo, hi, last, body):
    for n in range(first, lo):
        body(n, n % 2)
    if hi > lo:
        with eng.Fori(0, (hi - lo) // 2) as i:
            for r in range(2):
                body(2 * i + (lo + r), (lo + r) % 2)
    for n in range(max(lo, hi), last):
        body(n, n % 2)


class Program:
    pass


def layernorm_constants(nc, name, stats, mean, rstd, B):
    with ExitStack() as ctx:
        def sb(n, w):
            return ctx.enter_context(nc.sbuf_tensor(f"{name}_{n}", [P, w], F32))

        diff, var, sd, newton = sb("diff", B), sb("var", B), sb("sd", B), sb("newton", B)
        step = ctx.enter_context(nc.semaphore(f"{name}_step"))
        root = ctx.enter_context(nc.semaphore(f"{name}_root"))
        with nc.Block(name=name) as block:
            @block.scalar
            def _(act):
                act.wait_ge(step, 6)
                nc.scalar.activation(sd[:, :], var[:, :], ACT.Sqrt).then_inc(root, 1)

            @block.vector
            def _(dve):
                done = 0

                def link(ins):
                    nonlocal done
                    done += 1
                    ins.then_inc(step, 1)
                    dve.wait_ge(step, done)

                half = [stats[:, :, k] for k in range(6)]
                link(nc.vector.tensor_tensor(mean[:, :], half[1], half[4], ALU.add))
                link(nc.vector.tensor_tensor(diff[:, :], half[1], half[4], ALU.subtract))
                link(nc.vector.tensor_tensor(var[:, :], half[2], half[5], ALU.add))
                link(nc.vector.scalar_tensor_tensor(out=diff[:, :], in0=diff[:, :], scalar=0.25, in1=diff[:, :],
                                                    op0=ALU.mult, op1=ALU.mult))
                link(nc.vector.scalar_tensor_tensor(out=var[:, :], in0=var[:, :], scalar=1.0 / D, in1=diff[:, :],
                                                    op0=ALU.mult, op1=ALU.add))
                link(nc.vector.tensor_scalar(var[:, :], var[:, :], EPS, None, ALU.add))
                link(nc.vector.tensor_scalar(mean[:, :], mean[:, :], 0.5, None, ALU.mult))
                dve.wait_ge(root, 1)
                link(nc.vector.reciprocal(rstd[:, :], sd[:, :]))
                link(nc.vector.tensor_tensor(newton[:, :], rstd[:, :], rstd[:, :], ALU.mult))
                link(nc.vector.tensor_tensor(newton[:, :], newton[:, :], var[:, :], ALU.mult))
                link(nc.vector.tensor_scalar(newton[:, :], newton[:, :], -0.5, 1.5, ALU.mult, ALU.add))
                link(nc.vector.tensor_tensor(rstd[:, :], rstd[:, :], newton[:, :], ALU.mult))


def load_x(nc, B, x, x_all, stats):
    G = 4
    with ExitStack() as ctx:
        loaded = [ctx.enter_context(nc.semaphore(f"x_loaded{g}")) for g in range(G)]
        with nc.Block(name="load") as block:
            @block.sync
            def _(sp):
                for g in range(G):
                    own = slice(g * B // G, (g + 1) * B // G)
                    sp.dma_start(x_all[:, own, :], x[:, own, :]).then_inc(loaded[g], 16)

            @block.vector
            def _(dve):
                for g in range(G):
                    dve.wait_ge(loaded[g], 16)
                    for n in range(g * B // G, (g + 1) * B // G):
                        nc.vector.bn_stats(stats[:, n, :], x_all[:, n, :])


def feature_attention(nc, B, io, x_all, stats, mean, rstd, ident, gates):
    with ExitStack() as ctx:
        def sb(n, s, d=F32):
            return ctx.enter_context(nc.sbuf_tensor("a0_" + n, s, d))

        def parts(n, s):
            return [sb(f"{n}_{k}", s, F16) for k in ("high", "low")]

        def ps(n):
            return ctx.enter_context(nc.psum_tensor("a0_" + n, [P, 512], F32))

        def sem(n):
            return ctx.enter_context(nc.semaphore("a0_" + n))

        w_rep, w_sign = sb("w_rep", [P, HD]), sb("w_sign", [P, 2 * 8 * 2])
        fm_w = sb("fm_w", [P, 2, P])
        b_rep, b_sign, fm_b = sb("b_rep", [P, 1]), sb("b_sign", [P, 1]), sb("fm_b", [P, 1])
        head_mask = sb("head_mask", [P, 8])
        fc_w, fc_b = sb("fc_w", [P, 2, D]), sb("fc_b", [P, D])
        xn = [sb(f"xn{p}", [P, D]) for p in range(2)]
        xc = [sb(f"xc{p}", [P, P + KC]) for p in range(2)]
        feat = [sb(f"feat{p}", [P, 2, P + KC]) for p in range(2)]
        kfeat = [sb(f"kfeat{p}", [P, 2, 8, KC]) for p in range(2)]
        vfeat = [parts(f"vfeat{p}", [KC, NH, FD + 1]) for p in range(2)]
        mixed = [sb(f"mixed{p}", [P, NH, FD]) for p in range(2)]
        mixed_t = [sb(f"mixed_t{p}", [P, 2, P]) for p in range(2)]
        top, shift = ([sb(f"{n}{k}", [P, HQ]) for k in range(4)] for n in ("top", "shift"))
        prob = [sb(f"prob{k}", [P, HQ, KC]) for k in range(4)]
        prob_t = [parts(f"prob_t{k}", [KC, HQ, P]) for k in range(4)]
        rden = [sb(f"rden{p}", [P, NH]) for p in range(2)]

        score_ps = [ps(f"score{k}") for k in range(2)]
        trans_ps = [ps(f"trans{k}") for k in range(2)]
        mix_ps = [ps(f"mix{p}") for p in range(2)]
        prep_ps, fin_ps = ps("prep"), ps("fin")

        weights_in, ctx_in = sem("weights_in"), [sem(f"ctx_in{p}") for p in range(2)]
        weights_ready = sem("weights_ready")
        xn_ready, xn_t, xn_copied = sem("xn_ready"), sem("xn_t"), sem("xn_copied")
        z_ready, feat_ready, kfeat_ready = sem("z_ready"), sem("feat_ready"), sem("kfeat_ready")
        value_t, value_high, value_low = sem("value_t"), sem("value_high"), sem("value_low")
        score_ready, top_ready, shift_ready, exped = sem("score_ready"), sem("top_ready"), sem("shift"), sem("exped")
        prob_ready, prob_high, prob_low = sem("prob_ready"), sem("prob_high"), sem("prob_low")
        mixed_by_quarter, rden_ready, mixed_ready = sem("mixed_by_quarter"), sem("rden_ready"), sem("mixed_ready")
        mixed_turned, mixed_copied = sem("mixed_turned"), sem("mixed_copied")
        y_ready, x_biased, x_ready = sem("y_ready"), sem("x_biased"), sem("x_ready")

        SCALE = float(D) ** -0.5
        ON_DVE = (3,)
        LO, HI, LAST = 4, B - 4, B + 3
        WEIGHTS = [(w_rep, io["fm_w"]), (w_sign, io["fm_sign"]), (b_rep, io["fm_b"]), (b_sign, io["row_sign"]),
                   (head_mask, io["head_mask"]), (fc_b, io["fc_b"])]

        with nc.Block(name="a0") as block:
            @block.sync
            def _(sp):
                for t, src in WEIGHTS:
                    sp.dma_start(t[:, :], src).then_inc(weights_in, 16)
                sp.dma_start(fc_w[:, :, :], io["fc_w"]).then_inc(weights_in, 16)

                def slot(n, p):
                    if inside(n, 0, B):
                        wait(sp, z_ready, n - 1)
                        sp.dma_start(xc[p][:, P:P + KC], io["ctx"][:, n, :]).then_inc(ctx_in[p], 16)

                slots(sp, 0, LO, HI, B, slot)

            @block.tensor
            def _(pe):
                def prep_turn(n, p):
                    if inside(n, 0, B):
                        pe.wait_ge(xn_ready, n + 1)
                        wait(pe, value_low, n - 1)
                        wait(pe, feat_ready, n)
                        nc.tensor.transpose(prep_ps[:, 0:P], xn[p][:, :], ident[:, :]).then_inc(xn_t, 1)

                def prep_z(n, p):
                    if inside(n, 0, B):
                        pe.wait_ge(xn_copied, n + 1)
                        pe.wait_ge(ctx_in[p], (n - p) * 8 + 16)
                        if isinstance(n, int) and n == 0:
                            pe.wait_ge(weights_ready, 4)
                        for c in range(2):
                            mm = nc.tensor.matmul(prep_ps[:, 256 * c:256 * c + P + KC], fm_w[:, c, :], xc[p][:, :],
                                                  start=True, stop=True)
                        mm.then_inc(z_ready, 1)

                def prep_value(n, p):
                    if inside(n, 0, B):
                        pe.wait_ge(feat_ready, min(n + 2, B) if isinstance(n, int) else n + 2)
                        for c in range(2):
                            mm = nc.tensor.transpose(prep_ps[0:KC, P * c:P * (c + 1)], feat[p][:, c, P:P + KC],
                                                     ident[:, :])
                        mm.then_inc(value_t, 1)

                def scores(n, p, u):
                    if inside(n, 0, B):
                        if u % 2 == 0:
                            pe.wait_ge(kfeat_ready, 2 * n + u // 2 + 1)
                        wait(pe, exped, 4 * n + u - 1)
                        c = u // 2
                        nc.tensor.matmul(score_ps[u % 2][:, 0:QW], feat[p][:, c, 0:P],
                                         kfeat[p][:, c, 4 * (u % 2):4 * (u % 2) + 4, :],
                                         start=True, stop=True).then_inc(score_ready, 1)

                def turn(n, u):
                    if inside(n, 0, B):
                        pe.wait_ge(exped, 4 * n + u + 1)
                        wait(pe, prob_low, 4 * n + u - 1)
                        for h in range(HQ):
                            mm = nc.tensor.transpose(trans_ps[u % 2][0:KC, P * h:P * (h + 1)], prob[u][:, h, :],
                                                     ident[:, :])
                        mm.then_inc(prob_ready, 1)

                def mix(n, p, u):
                    if inside(n, 0, B):
                        pe.wait_ge(prob_low, 4 * n + u + 1)
                        if u == 0:
                            pe.wait_ge(value_low, n + 1)
                            wait(pe, mixed_ready, n - 1)
                        for h in range(HQ):
                            head = 4 * u + h
                            for k, (a, b) in enumerate(((0, 0), (0, 1), (1, 0))):
                                mm = nc.tensor.matmul(mix_ps[p][:, head * (FD + 1):(head + 1) * (FD + 1)],
                                                      prob_t[u][a][:, h, :], vfeat[p][b][:, head, :],
                                                      start=(k == 0), stop=(k == 2))
                        mm.then_inc(mixed_by_quarter, 1)

                def fin_turn(n, p):
                    if inside(n, 0, B):
                        pe.wait_ge(mixed_ready, n + 1)
                        wait(pe, x_ready, n)
                        flat = mixed[p][:, :, :].rearrange("q h f -> q (h f)")
                        for c in range(2):
                            mm = nc.tensor.transpose(fin_ps[:, P * c:P * (c + 1)], flat[:, P * c:P * (c + 1)],
                                                     ident[:, :])
                        mm.then_inc(mixed_turned, 1)

                def fin_project(n, p):
                    if inside(n, 0, B):
                        pe.wait_ge(mixed_copied, n + 1)
                        for c in range(2):
                            mm = nc.tensor.matmul(fin_ps[:, 0:D], mixed_t[p][:, c, :], fc_w[:, c, :],
                                                  start=(c == 0), stop=(c == 1))
                        mm.then_inc(y_ready, 1)

                def slot(n, p):
                    o = 1 - p
                    scores(n, p, 0)
                    turn(n - 1, 2)
                    prep_z(n + 1, o)
                    mix(n - 1, o, 0)
                    fin_project(n - 3, o)
                    scores(n, p, 1)
                    turn(n - 1, 3)
                    prep_value(n, p)
                    mix(n - 1, o, 1)
                    scores(n, p, 2)
                    turn(n, 0)
                    mix(n - 1, o, 2)
                    fin_turn(n - 2, p)
                    prep_turn(n + 2, p)
                    scores(n, p, 3)
                    turn(n, 1)
                    mix(n - 1, o, 3)

                slots(pe, -2, LO, HI, LAST, slot)

            @block.scalar
            def _(act):
                def copy_xn(n, p):
                    if inside(n, 0, B):
                        act.wait_ge(xn_t, n + 1)
                        wait(act, z_ready, n - 1)
                        nc.scalar.activation(xc[p][:, 0:P], prep_ps[:, 0:P], ACT.Copy).then_inc(xn_copied, 1)

                def features(n, p):
                    if inside(n, 0, B):
                        act.wait_ge(z_ready, n + 1)
                        z = prep_ps[:, :].rearrange("r (c t) -> r c t", c=2)[:, :, 0:P + KC]
                        nc.scalar.activation(feat[p][:, :, :], z, ACT.Exp, bias=fm_b[:, 0:1]).then_inc(feat_ready, 1)

                def high_value(n, p):
                    if inside(n, 0, B):
                        act.wait_ge(value_t, n + 1)
                        wait(act, mixed_by_quarter, 4 * n - 4)
                        v = prep_ps[0:KC, 0:NH * FD].rearrange("k (h f) -> k h f", h=NH)
                        nc.scalar.activation(vfeat[p][0][:, :, 0:FD], v, ACT.Copy, scale=VSCALE).then_inc(value_high, 1)

                def exp(n, u):
                    if inside(n, 0, B):
                        act.wait_ge(shift_ready, 4 * n + u + 1)
                        if u in ON_DVE:
                            last = nc.scalar.activation(prob[u][:, :, :], prob[u][:, :, :], ACT.Exp, scale=SCALE)
                        else:
                            wait(act, prob_ready, 4 * n + u - 3)
                            for h in range(HQ):
                                last = nc.scalar.activation(prob[u][:, h, :], score_ps[u % 2][:, KC * h:KC * (h + 1)],
                                                            ACT.Exp, bias=shift[u][:, h:h + 1], scale=SCALE)
                        last.then_inc(exped, 1)

                def high_prob(n, u):
                    if inside(n, 0, B):
                        act.wait_ge(prob_ready, 4 * n + u + 1)
                        wait(act, mixed_by_quarter, 4 * n + u - 3)
                        nc.scalar.activation(prob_t[u][0][:, :, :],
                                             trans_ps[u % 2][0:KC, :].rearrange("k (h q) -> k h q", h=HQ),
                                             ACT.Copy).then_inc(prob_high, 1)

                def copy_mixed(n, p):
                    if inside(n, 0, B):
                        act.wait_ge(mixed_turned, n + 1)
                        nc.scalar.activation(mixed_t[p][:, :, :],
                                             fin_ps[:, 0:2 * P].rearrange("f (c q) -> f c q", c=2),
                                             ACT.Copy).then_inc(mixed_copied, 1)

                def slot(n, p):
                    o = 1 - p
                    high_prob(n - 1, 2)
                    features(n + 1, o)
                    exp(n, 0)
                    high_prob(n - 1, 3)
                    high_value(n, p)
                    exp(n, 1)
                    high_prob(n, 0)
                    exp(n, 2)
                    copy_xn(n + 2, p)
                    high_prob(n, 1)
                    copy_mixed(n - 2, p)
                    exp(n, 3)

                act.wait_ge(weights_ready, 4)
                slots(act, -2, LO, HI, LAST, slot)

            @block.gpsimd
            def _(pool):
                for p in range(2):
                    for k in range(2):
                        nc.gpsimd.memset(vfeat[p][k][:, :, FD:FD + 1], VSCALE * (1 - k))

                def slot(n, p):
                    if inside(n, 0, B):
                        pool.wait_ge(feat_ready, n + 1)
                        wait(pool, score_ready, 4 * n - 4)
                        for c in range(2):
                            nc.gpsimd.tensor_tensor(
                                kfeat[p][:, c, :, :], feat[p][:, c, P:P + KC].unsqueeze(1).broadcast_to([P, 8, KC]),
                                head_mask[:, :].unsqueeze(2).broadcast_to([P, 8, KC]), ALU.mult).then_inc(kfeat_ready, 1)
                        nc.gpsimd.tensor_tensor(x_all[:, n, :], x_all[:, n, :], fc_b[:, :],
                                                ALU.add).then_inc(x_biased, 1)

                pool.wait_ge(weights_ready, 4)
                slots(pool, 0, LO, HI, B, slot)

            @block.vector
            def _(dve):
                dve.wait_ge(weights_in, 16 * (len(WEIGHTS) + 1))
                nc.vector.tensor_tensor(
                    fm_w[:, :, :].rearrange("r c (g e) -> r (c g) e", e=HD),
                    w_rep[:, :].unsqueeze(1).broadcast_to([P, 2 * 8 * 2, HD]),
                    w_sign[:, :].unsqueeze(2).broadcast_to([P, 2 * 8 * 2, HD]), ALU.mult).then_inc(weights_ready, 1)
                nc.vector.tensor_tensor(fm_b[:, :], b_rep[:, :], b_sign[:, :], ALU.mult).then_inc(weights_ready, 1)
                nc.vector.tensor_scalar(fc_w[:, :, :], fc_w[:, :, :], gates[:, 0:1], None,
                                        ALU.mult).then_inc(weights_ready, 1)
                nc.vector.tensor_scalar(fc_b[:, :], fc_b[:, :], gates[:, 0:1], None,
                                        ALU.mult).then_inc(weights_ready, 1)

                def normalize(n, p):
                    if inside(n, 0, B):
                        wait(dve, xn_t, n - 1)
                        nc.vector.tensor_scalar(xn[p][:, :], x_all[:, n, :], mean[:, n, :], rstd[:, n, :],
                                                ALU.subtract, ALU.mult).then_inc(xn_ready, 1)

                def row_max(n, u):
                    if inside(n, 0, B):
                        s = score_ps[u % 2][:, 0:QW].rearrange("q (h k) -> q h k", h=HQ)
                        dve.wait_ge(score_ready, 4 * n + u + 1)
                        nc.vector.tensor_reduce(top[u][:, :], s, AX_X, ALU.max).then_inc(top_ready, 1)

                def shift_by_max(n, u):
                    if inside(n, 0, B):
                        dve.wait_ge(top_ready, 4 * n + u + 1)
                        if u in ON_DVE:
                            wait(dve, prob_ready, 4 * n + u - 3)
                            nc.vector.tensor_tensor(
                                prob[u][:, :, :], score_ps[u % 2][:, 0:QW].rearrange("q (h k) -> q h k", h=HQ),
                                top[u][:, :].unsqueeze(2).broadcast_to([P, HQ, KC]), ALU.subtract).then_inc(shift_ready, 1)
                        else:
                            wait(dve, exped, 4 * n + u - 3)
                            nc.vector.tensor_scalar(shift[u][:, :], top[u][:, :], -SCALE, None,
                                                    ALU.mult).then_inc(shift_ready, 1)

                def low_prob(n, u):
                    if inside(n, 0, B):
                        dve.wait_ge(prob_high, 4 * n + u + 1)
                        own = [t[:, :, :].rearrange("k h q -> k (h q)") for t in prob_t[u]]
                        nc.vector.tensor_tensor(own[1], trans_ps[u % 2][0:KC, :], own[0],
                                                ALU.subtract).then_inc(prob_low, 1)

                def low_value(n, p):
                    if inside(n, 0, B):
                        dve.wait_ge(value_high, n + 1)
                        v = prep_ps[0:KC, 0:NH * FD].rearrange("k (h f) -> k h f", h=NH)
                        nc.vector.scalar_tensor_tensor(out=vfeat[p][1][:, :, 0:FD], in0=v, scalar=VSCALE,
                                                       in1=vfeat[p][0][:, :, 0:FD], op0=ALU.mult,
                                                       op1=ALU.subtract).then_inc(value_low, 1)

                def inverse_sum(n, p):
                    if inside(n, 0, B):
                        m = mix_ps[p][:, 0:NH * (FD + 1)].rearrange("q (h f) -> q h f", h=NH)
                        dve.wait_ge(mixed_by_quarter, 4 * n + 4)
                        nc.vector.reciprocal(rden[p][:, :], m[:, :, FD]).then_inc(rden_ready, 1)

                def divide(n, p):
                    if inside(n, 0, B):
                        m = mix_ps[p][:, 0:NH * (FD + 1)].rearrange("q (h f) -> q h f", h=NH)
                        dve.wait_ge(rden_ready, n + 1)
                        wait(dve, mixed_turned, n - 1)
                        nc.vector.tensor_tensor(mixed[p][:, :, :], m[:, :, 0:FD],
                                                rden[p][:, :].unsqueeze(2).broadcast_to([P, NH, FD]),
                                                ALU.mult).then_inc(mixed_ready, 1)

                def residual(n):
                    if inside(n, 0, B):
                        dve.wait_ge(y_ready, n + 1)
                        dve.wait_ge(x_biased, n + 1)
                        nc.vector.tensor_tensor(x_all[:, n, :], x_all[:, n, :], fin_ps[:, 0:D],
                                                ALU.add).then_inc(x_ready, 1)

                def statistics(n):
                    if inside(n, 0, B):
                        dve.wait_ge(x_ready, n + 1)
                        nc.vector.bn_stats(stats[:, n, :], x_all[:, n, :])

                def slot(n, p):
                    o = 1 - p
                    row_max(n, 0)
                    inverse_sum(n - 2, p)
                    shift_by_max(n, 0)
                    low_prob(n - 1, 2)
                    divide(n - 2, p)
                    row_max(n, 1)
                    residual(n - 3)
                    shift_by_max(n, 1)
                    low_prob(n - 1, 3)
                    low_value(n, p)
                    row_max(n, 2)
                    statistics(n - 3)
                    shift_by_max(n, 2)
                    low_prob(n, 0)
                    row_max(n, 3)
                    normalize(n + 3, o)
                    shift_by_max(n, 3)
                    low_prob(n, 1)

                slots(dve, -3, LO, HI, LAST, slot)


def split_float16(nc, name, parts):
    with ExitStack() as ctx:
        loaded = [ctx.enter_context(nc.semaphore(f"{name}_loaded{k}")) for k in range(len(parts))]
        high_ready = ctx.enter_context(nc.semaphore(f"{name}_high_ready"))
        stage = [ctx.enter_context(nc.sbuf_tensor(f"{name}_stage{k}", list(high.shape), F32))
                 for k, (_, high, _, _) in enumerate(parts)]
        with nc.Block(name=name) as block:
            @block.sync
            def _(sp):
                for k, (t, (src, _, _, _)) in enumerate(zip(stage, parts)):
                    sp.dma_start(t[:, :, :], src).then_inc(loaded[k], 16)

            @block.scalar
            def _(act):
                for k, (t, (_, high, _, scale)) in enumerate(zip(stage, parts)):
                    act.wait_ge(loaded[k], 16)
                    nc.scalar.activation(high, t[:, :, :], ACT.Copy, scale=scale).then_inc(high_ready, 1)

            @block.vector
            def _(dve):
                for k, (t, (_, high, low, scale)) in enumerate(zip(stage, parts)):
                    dve.wait_ge(high_ready, k + 1)
                    flat = [v.rearrange("p a b -> p (a b)") for v in (t[:, :, :], high, low)]
                    nc.vector.scalar_tensor_tensor(out=flat[2], in0=flat[0], scalar=scale, in1=flat[1],
                                                   op0=ALU.mult, op1=ALU.subtract)


def router(nc, name, B, io, x_all, mean, rstd, ident, x_high, x_low, logits, weights, actor=None):
    G = B // GB
    with ExitStack() as ctx:
        def sb(n, s):
            return ctx.enter_context(nc.sbuf_tensor(f"{name}_{n}", s, F32))

        def ps(n):
            return [ctx.enter_context(nc.psum_tensor(f"{name}_{n}{p}", [P, GT], F32)) for p in range(2)]

        def sem(n):
            return ctx.enter_context(nc.semaphore(f"{name}_{n}"))

        w_router = sb("w_router", [P, NE])
        xn = [sb(f"xn{p}", [P, GB, D]) for p in range(2)]
        xt = [sb(f"xt{p}", [P, GT]) for p in range(2)]
        turn_ps, logit_ps = ps("turn_ps"), ps("logit_ps")
        weights_in = sem("weights_in")
        xn_ready, turned, xt_ready = sem("xn_ready"), sem("turned"), sem("xt_ready")
        high_ready, low_ready = sem("high_ready"), sem("low_ready")
        logits_ready, logits_copied = sem("logits_ready"), sem("logits_copied")
        loads = [(w_router, io[name + "_router"])]
        stage = [sb(f"stage{k}", list(high.shape)) for k, (_, high, _) in enumerate(weights)]
        pieces = [[t[:, :, :].rearrange("p a b -> p (a b)").rearrange("p (g w) -> p g w", g=G) for t in (t32, high, low)]
                  for t32, (_, high, low) in zip(stage, weights)]
        stage_in = [sem(f"stage{k}_in") for k in range(len(weights))]
        weights_high = sem("weights_high")
        if actor:
            w1, b1 = sb("w1", [P, AH]), sb("b1", [AH, 1])
            w2, b2 = sb("w2", [AH, MAX_K]), sb("b2", [P, MAX_K])
            pre = [sb(f"pre{p}", [AH, GT]) for p in range(2)]
            cube = [sb(f"cube{p}", [AH, GT]) for p in range(2)]
            hidden = [sb(f"hidden{p}", [AH, GT]) for p in range(2)]
            hidden_ps, actor_ps = ps("hidden_ps"), ps("actor_ps")
            loads += [(w1, io["actor_w1"]), (b1, io["actor_b1"]), (w2, io["actor_w2"]), (b2, io["actor_b2"])]
            w2_halved, pre_ps_ready, pre_ready = sem("w2_halved"), sem("pre_ps_ready"), sem("pre_ready")
            square_ready, factor_ready, cube_ready = sem("square_ready"), sem("factor_ready"), sem("cube_ready")
            tanh_ready, hidden_ready = sem("tanh_ready"), sem("hidden_ready")
            actor_ready, actor_copied = sem("actor_ready"), sem("actor_copied")

        with nc.Block(name=name) as block:
            @block.sync
            def _(sp):
                for t, src in loads:
                    sp.dma_start(t[:, :], src).then_inc(weights_in, 16)
                for t, arrived, (src, _, _) in zip(stage, stage_in, weights):
                    sp.dma_start(t[:, :, :], src).then_inc(arrived, 16)

            LO, HI, LAST = 4, G - 2, G + 3

            @block.vector
            def _(dve):
                dve.wait_ge(weights_in, 16 * len(loads))
                if actor:
                    nc.vector.tensor_scalar(w2[:, :], w2[:, :], 0.5, None, ALU.mult).then_inc(w2_halved, 1)

                def normalize(g, p):
                    if inside(g, 0, G):
                        wait(dve, turned, g - 1)
                        for t in range(GB):
                            n = GB * g + t
                            last = nc.vector.tensor_scalar(xn[p][:, t, :], x_all[:, n, :], mean[:, n, :], rstd[:, n, :],
                                                           ALU.subtract, ALU.mult)
                        last.then_inc(xn_ready, 1)

                def high_part(g, p):
                    if inside(g, 0, G):
                        dve.wait_ge(xt_ready, g + 1)
                        nc.vector.tensor_copy(x_high[:, g, :], xt[p][:, :]).then_inc(high_ready, 1)

                def square(g, p):
                    if actor and inside(g, 0, G):
                        dve.wait_ge(pre_ready, g + 1)
                        wait(dve, hidden_ready, g - 1)
                        nc.vector.tensor_tensor(cube[p][:, :], pre[p][:, :], pre[p][:, :],
                                                ALU.mult).then_inc(square_ready, 1)

                def gelu_factor(g, p):
                    if actor and inside(g, 0, G):
                        dve.wait_ge(square_ready, g + 1)
                        nc.vector.tensor_scalar(cube[p][:, :], cube[p][:, :], 0.044715, 1.0, ALU.mult,
                                                ALU.add).then_inc(factor_ready, 1)

                def gelu(g, p):
                    if actor and inside(g, 0, G):
                        dve.wait_ge(tanh_ready, g + 1)
                        wait(dve, actor_ready, g - 1)
                        nc.vector.scalar_tensor_tensor(out=hidden[p][:, :], in0=cube[p][:, :], scalar=1.0,
                                                       in1=pre[p][:, :], op0=ALU.add,
                                                       op1=ALU.mult).then_inc(hidden_ready, 1)

                def copy_logits(g, p):
                    if inside(g, 0, G):
                        dve.wait_ge(logits_ready, g + 1)
                        nc.vector.tensor_copy(logits[:, g, :], logit_ps[p][:, 0:GB * NE]).then_inc(logits_copied, 1)

                def copy_actor(g, p):
                    if actor and inside(g, 0, G):
                        dve.wait_ge(actor_ready, g + 1)
                        nc.vector.tensor_tensor(
                            actor[:, g, :].rearrange("q (t k) -> q t k", t=GB),
                            actor_ps[p][:, 0:GB * MAX_K].rearrange("q (t k) -> q t k", t=GB),
                            b2[:, :].unsqueeze(1).broadcast_to([P, GB, MAX_K]), ALU.add).then_inc(actor_copied, 1)

                def low_weights(g):
                    if inside(g, 0, G):
                        dve.wait_ge(weights_high, g + 1)
                        for t32, high, low in pieces:
                            nc.vector.scalar_tensor_tensor(out=low[:, g, :], in0=t32[:, g, :], scalar=WSCALE,
                                                           in1=high[:, g, :], op0=ALU.mult, op1=ALU.subtract)

                def slot(g, p):
                    o = 1 - p
                    normalize(g + 2, p)
                    high_part(g + 1, o)
                    copy_actor(g - 3, o)
                    gelu(g - 1, o)
                    square(g, p)
                    copy_logits(g, p)
                    gelu_factor(g, p)
                    low_weights(g - 1)

                slots(dve, -2, LO, HI, LAST, slot)

            @block.tensor
            def _(pe):
                pe.wait_ge(weights_in, 16 * len(loads))
                if actor:
                    pe.wait_ge(w2_halved, 1)

                def turn(g, p):
                    if inside(g, 0, G):
                        pe.wait_ge(xn_ready, g + 1)
                        wait(pe, xt_ready, g - 1)
                        for t in range(GB):
                            mm = nc.tensor.transpose(turn_ps[p][:, P * t:P * (t + 1)], xn[p][:, t, :], ident[:, :])
                        mm.then_inc(turned, 1)

                def actor_hidden(g, p):
                    if actor and inside(g, 0, G):
                        pe.wait_ge(xt_ready, g + 1)
                        wait(pe, pre_ready, g - 1)
                        nc.tensor.matmul(hidden_ps[p][0:AH, :], w1[:, :], xt[p][:, :],
                                         start=True, stop=True).then_inc(pre_ps_ready, 1)

                def route(g, p):
                    if inside(g, 0, G):
                        pe.wait_ge(xt_ready, g + 1)
                        wait(pe, logits_copied, g - 1)
                        for t in range(GB):
                            mm = nc.tensor.matmul(logit_ps[p][:, NE * t:NE * (t + 1)], xt[p][:, P * t:P * (t + 1)],
                                                  w_router[:, :], start=True, stop=True)
                        mm.then_inc(logits_ready, 1)

                def actor_out(g, p):
                    if actor and inside(g, 0, G):
                        pe.wait_ge(hidden_ready, g + 1)
                        wait(pe, actor_copied, g - 1)
                        for t in range(GB):
                            mm = nc.tensor.matmul(actor_ps[p][:, MAX_K * t:MAX_K * (t + 1)],
                                                  hidden[p][:, P * t:P * (t + 1)], w2[:, :], start=True, stop=True)
                        mm.then_inc(actor_ready, 1)

                def slot(g, p):
                    o = 1 - p
                    actor_hidden(g, p)
                    turn(g + 1, o)
                    actor_out(g - 2, p)
                    route(g, p)

                slots(pe, -1, LO, HI, LAST, slot)

            @block.scalar
            def _(act):
                act.wait_ge(weights_in, 16 * len(loads))

                def copy_xn(g, p):
                    if inside(g, 0, G):
                        act.wait_ge(turned, g + 1)
                        wait(act, low_ready, g - 1)
                        wait(act, logits_ready, g - 1)
                        nc.scalar.activation(xt[p][:, :], turn_ps[p][:, :], ACT.Copy).then_inc(xt_ready, 1)

                def pre_activation(g, p):
                    if actor and inside(g, 0, G):
                        act.wait_ge(pre_ps_ready, g + 1)
                        wait(act, hidden_ready, g - 1)
                        nc.scalar.activation(pre[p][:, :], hidden_ps[p][0:AH, :], ACT.Identity,
                                             bias=b1[:, 0:1]).then_inc(pre_ready, 1)

                def tanh(g, p):
                    if actor and inside(g, 0, G):
                        act.wait_ge(cube_ready, g + 1)
                        nc.scalar.activation(cube[p][:, :], cube[p][:, :], ACT.Tanh,
                                             scale=(2.0 / 3.141592653589793) ** 0.5).then_inc(tanh_ready, 1)

                def high_weights(g):
                    if inside(g, 0, G):
                        for arrived, (t32, high, _) in zip(stage_in, pieces):
                            act.wait_ge(arrived, 16)
                            last = nc.scalar.activation(high[:, g, :], t32[:, g, :], ACT.Copy, scale=WSCALE)
                        last.then_inc(weights_high, 1)

                def slot(g, p):
                    o = 1 - p
                    copy_xn(g + 1, o)
                    pre_activation(g, p)
                    tanh(g - 1, o)
                    high_weights(g)

                slots(act, -1, LO, HI, LAST, slot)

            @block.gpsimd
            def _(pool):
                def low_part(g, p):
                    if inside(g, 0, G):
                        pool.wait_ge(high_ready, g + 1)
                        nc.gpsimd.tensor_tensor(x_low[:, g, :], xt[p][:, :], x_high[:, g, :],
                                                ALU.subtract).then_inc(low_ready, 1)

                def cubed(g, p):
                    if actor and inside(g, 0, G):
                        pool.wait_ge(factor_ready, g + 1)
                        nc.gpsimd.tensor_tensor(cube[p][:, :], cube[p][:, :], pre[p][:, :],
                                                ALU.mult).then_inc(cube_ready, 1)

                def slot(g, p):
                    low_part(g + 1, 1 - p)
                    cubed(g, p)

                slots(pool, -1, LO, HI, LAST, slot)


def expert_scores(nc, name, B, io, logits, actor, scores, gate):
    with ExitStack() as ctx:
        def sb(n, s):
            return ctx.enter_context(nc.sbuf_tensor(f"{name}_{n}", s, F32))

        probs, rank, cmp_ = sb("probs", [P, B, NE]), sb("rank", [P, B, NE]), sb("cmp", [P, B, NE])
        one, total = sb("one", [P, B]), sb("total", [P, B])
        after = sb("after", [P, NE])
        first, allowed, best = sb("first", [P, MAX_K]), sb("allowed", [P, B]), sb("best", [P, B])
        consts_in = ctx.enter_context(nc.semaphore(f"{name}_consts_in"))
        step = ctx.enter_context(nc.semaphore(f"{name}_step"))
        exped = ctx.enter_context(nc.semaphore(f"{name}_exped"))

        def wide(t, n=NE):
            return t[:, :].unsqueeze(2).broadcast_to([P, B, n])

        with nc.Block(name=name) as block:
            @block.sync
            def _(sp):
                sp.dma_start(after[:, :], io["experts_after"]).then_inc(consts_in, 16)
                sp.dma_start(first[:, :], io["first_k"]).then_inc(consts_in, 16)
                sp.wait_ge(consts_in, 32)

            @block.scalar
            def _(act):
                act.wait_ge(step, 2)
                nc.scalar.activation(probs[:, :, :], probs[:, :, :], ACT.Exp).then_inc(exped, 1)

            @block.vector
            def _(dve):
                done = 0

                def link(ins):
                    nonlocal done
                    done += 1
                    ins.then_inc(step, 1)
                    dve.wait_ge(step, done)

                l3 = logits[:, :, :].rearrange("q g (t e) -> q (g t) e", e=NE)
                link(nc.vector.tensor_reduce(one[:, :], l3, AX_X, ALU.max))
                link(nc.vector.tensor_tensor(probs[:, :, :], l3, wide(one), ALU.subtract))
                dve.wait_ge(consts_in, 32)
                if actor is not None:
                    a3 = actor[:, :, :].rearrange("q g (t k) -> q (g t) k", k=MAX_K)
                    link(nc.vector.tensor_scalar(a3, a3, 30.0, -30.0, ALU.min, ALU.max))
                    link(nc.vector.tensor_reduce(best[:, :], a3, AX_X, ALU.max))
                    link(nc.vector.tensor_tensor(a3, a3, wide(best, MAX_K), ALU.is_equal))
                    link(nc.vector.tensor_tensor(a3, a3, first[:, :].unsqueeze(1).broadcast_to([P, B, MAX_K]), ALU.mult))
                    link(nc.vector.tensor_reduce(allowed[:, :], a3, AX_X, ALU.min))
                    link(nc.vector.tensor_scalar(allowed[:, :], allowed[:, :], MAX_K + 1.0, None, ALU.add))
                else:
                    link(nc.vector.memset(allowed[:, :], float(TOP_K)))
                dve.wait_ge(exped, 1)
                link(nc.vector.tensor_reduce(total[:, :], probs[:, :, :], AX_X, ALU.add))
                link(nc.vector.reciprocal(one[:, :], total[:, :]))
                link(nc.vector.tensor_tensor(probs[:, :, :], probs[:, :, :], wide(one), ALU.mult))
                link(nc.vector.tensor_copy(rank[:, :, :], after[:, :].unsqueeze(1).broadcast_to([P, B, NE])))
                for d in range(1, NE):
                    ge, front, back = cmp_[:, :, 0:NE - d], slice(0, NE - d), slice(d, NE)
                    link(nc.vector.tensor_tensor(ge, probs[:, :, front], probs[:, :, back], ALU.is_ge))
                    link(nc.vector.tensor_tensor(rank[:, :, front], rank[:, :, front], ge, ALU.subtract))
                    link(nc.vector.tensor_tensor(rank[:, :, back], rank[:, :, back], ge, ALU.add))
                link(nc.vector.tensor_tensor(rank[:, :, :], rank[:, :, :], wide(allowed), ALU.is_lt))
                link(nc.vector.tensor_tensor(probs[:, :, :], probs[:, :, :], rank[:, :, :], ALU.mult))
                if actor is None:
                    link(nc.vector.tensor_reduce(total[:, :], probs[:, :, :], AX_X, ALU.add))
                    link(nc.vector.tensor_scalar(total[:, :], total[:, :], 1e-8, None, ALU.add))
                    link(nc.vector.reciprocal(one[:, :], total[:, :]))
                    link(nc.vector.tensor_tensor(probs[:, :, :], probs[:, :, :], wide(one), ALU.mult))
                flat = [t[:, :, :].rearrange("q n e -> q (n e)") for t in (scores[:, :, :, 0], probs)]
                link(nc.vector.tensor_scalar(flat[0], flat[1], gate, 1.0 / WSCALE, ALU.mult, ALU.mult))


def experts(nc, name, B, x_high, x_low, x_all, scores, w_in, w_down, rows, per, lag, banks, out=None, stats=None):
    G, M = B // GB, NE * per
    with ExitStack() as ctx:
        def sb(n, s, d=F32):
            return [ctx.enter_context(nc.sbuf_tensor(f"{name}_{n}{k}", s, d)) for k in range(RING)]

        def ps(n, k):
            return [ctx.enter_context(nc.psum_tensor(f"{name}_{n}{p}", [P, GT], F32)) for p in range(k)]

        def sem(n):
            return ctx.enter_context(nc.semaphore(f"{name}_{n}"))

        act_out, hidden = sb("act_out", [rows, GT]), sb("hidden", [rows, GT])
        high, low = sb("high", [rows, GT], F16), sb("low", [rows, GT], F16)
        in_ps = [ps(f"in{k}_", banks) for k in range(len(w_in))]
        y_ps = ps("y", 2)
        in_ready, act_ready, hidden_ready = sem("in_ready"), sem("act_ready"), sem("hidden_ready")
        high_ready, low_ready, down_done = sem("high_ready"), sem("low_ready"), sem("down_done")
        x_ready = sem("x_ready")
        if out is not None:
            x_stored = sem("x_stored")
        gated = len(w_in) == 2

        def groups(eng, body):
            body(0)
            with eng.Fori(1, G) as g:
                body(g)

        def late(g, m, by, body):
            if m >= by:
                body(g, m - by)
            elif not isinstance(g, int) or g > 0:
                body(g - 1, m - by + M)

        with nc.Block(name=name) as block:
            @block.tensor
            def _(pe):
                def project(g, m):
                    for k, (wh, wl) in enumerate(w_in):
                        if k == 0:
                            wait(pe, hidden_ready, M * g + m + 1 - banks)
                        dst, own = in_ps[k][m % banks][0:rows, :], slice(rows * m, rows * (m + 1))
                        nc.tensor.matmul(dst, wh[:, 0, own], x_high[:, g, :], start=True, stop=False)
                        nc.tensor.matmul(dst, wl[:, 0, own], x_high[:, g, :], start=False, stop=False)
                        mm = nc.tensor.matmul(dst, wh[:, 0, own], x_low[:, g, :], start=False, stop=True)
                    mm.then_inc(in_ready, 1)

                def down(g, m):
                    e, c = m // per, m % per
                    pe.wait_ge(low_ready, M * g + m + 1)
                    if c == 0:
                        wait(pe, x_ready, NE * g + e - 1)
                    for t in range(GB):
                        own, dst = slice(P * t, P * (t + 1)), y_ps[e % 2][:, D * t:D * (t + 1)]
                        parts = [(high, 0), (high, 1), (low, 0)]
                        for k, (h, part) in enumerate(parts):
                            mm = nc.tensor.matmul(dst, h[m % RING][:, own], w_down[part][:, m, :],
                                                  start=(c == 0 and t == 0 and k == 0), stop=(c == per - 1 and k == 2),
                                                  skip_group_check=True)
                    mm.then_inc(down_done, 1)

                def group(g):
                    for m in range(M):
                        project(g, m)
                        late(g, m, lag, down)

                groups(pe, group)
                for m in range(M - lag, M):
                    down(G - 1, m)

            @block.scalar
            def _(act):
                def split(g, m):
                    act.wait_ge(hidden_ready, M * g + m + 1)
                    wait(act, down_done, M * g + m + 1 - RING)
                    nc.scalar.activation(high[m % RING][:, :], hidden[m % RING][:, :], ACT.Copy).then_inc(high_ready, 1)

                def group(g):
                    for m in range(M):
                        act.wait_ge(in_ready, M * g + m + 1)
                        wait(act, hidden_ready, M * g + m + 1 - RING)
                        func, scale = (ACT.Silu, 1.0 / WSCALE) if gated else (ACT.Relu, 1.0 / WSCALE ** 2)
                        nc.scalar.activation(act_out[m % RING][:, :], in_ps[0][m % banks][0:rows, :], func,
                                             scale=scale).then_inc(act_ready, 1)
                        late(g, m, 1, split)

                groups(act, group)
                split(G - 1, M - 1)

            @block.vector
            def _(dve):
                def accumulate(g, e):
                    dve.wait_ge(down_done, M * g + per * (e + 1))
                    for t in range(GB):
                        n = GB * g + t
                        wait(dve, x_ready, NE * g + e)
                        last = nc.vector.scalar_tensor_tensor(
                            out=x_all[:, n, :], in0=y_ps[e % 2][:, D * t:D * (t + 1)], scalar=scores[:, n, e, :],
                            in1=x_all[:, n, :], op0=ALU.mult, op1=ALU.add)
                    last.then_inc(x_ready, 1)
                    if e == NE - 1 and stats is not None:
                        dve.wait_ge(x_ready, NE * (g + 1))
                        for t in range(GB):
                            n = GB * g + t
                            nc.vector.bn_stats(stats[:, n, :], x_all[:, n, :])

                def finish(g, m):
                    if m % per == per - 1:
                        accumulate(g, m // per)

                def group(g):
                    for m in range(M):
                        k = m % RING
                        dve.wait_ge(act_ready, M * g + m + 1)
                        wait(dve, low_ready, M * g + m + 1 - RING)
                        dst, a = hidden[k][:, :], act_out[k][:, :]
                        src = in_ps[-1][m % banks][0:rows, :]
                        scalar, op = (1.0 / WSCALE, ALU.mult) if gated else (0.0, ALU.max)
                        nc.vector.scalar_tensor_tensor(out=dst, in0=src, scalar=scalar, in1=a, op0=op,
                                                       op1=ALU.mult).then_inc(hidden_ready, 1)
                        late(g, m, lag + 1, finish)

                groups(dve, group)
                for m in range(M - lag - 1, M):
                    finish(G - 1, m)

            @block.gpsimd
            def _(pool):
                def group(g):
                    for m in range(M):
                        k = m % RING
                        pool.wait_ge(high_ready, M * g + m + 1)
                        nc.gpsimd.tensor_tensor(low[k][:, :], hidden[k][:, :], high[k][:, :],
                                                ALU.subtract).then_inc(low_ready, 1)

                groups(pool, group)

            if out is not None:
                @block.sync
                def _(sp):
                    def group(g):
                        sp.wait_ge(x_ready, NE * (g + 1))
                        sp.dma_start(by_group[0][:, g, :], by_group[1][:, g, :]).then_inc(x_stored, 16)

                    by_group = [t.rearrange("q (g t) d -> q g (t d)", t=GB) for t in (out, x_all[:, :, :])]
                    groups(sp, group)
                    sp.wait_ge(x_stored, 16 * G)


def relative_attention(nc, B, io, x_all, stats, mean, rstd, ident, gates, q_dram, r_dram):
    with ExitStack() as ctx:
        def sb(n, s, d=F32):
            return ctx.enter_context(nc.sbuf_tensor("a1_" + n, s, d))

        def parts(n, s):
            return [sb(f"{n}_{k}", s, F16) for k in ("high", "low")]

        def ps(n):
            return ctx.enter_context(nc.psum_tensor("a1_" + n, [P, 512], F32))

        def sem(n):
            return ctx.enter_context(nc.semaphore("a1_" + n))

        w_q, w_rows, w_k, w_v = (parts(n, [P, 1, D]) for n in ("w_q", "w_rows", "w_k", "w_v"))
        key_table, value_table = parts("key_table", [QC * QB, 1, KT]), parts("value_table", [KC, P, HD])
        ctx_t = parts("ctx_t", [P, B, KC])
        quarters = [slice(k * B // 4, (k + 1) * B // 4) for k in range(4)]
        split_float16(nc, "split_a1", [(io["ctx"][:, own, :], ctx_t[0][:, own, :], ctx_t[1][:, own, :], 1.0)
                                       for own in quarters] +
                      [(src, t[0][:, :, :], t[1][:, :, :], 1.0)
                       for src, t in ((io["w_q"].unsqueeze(1), w_q), (io["w_rows"].unsqueeze(1), w_rows),
                                      (io["w_k"].unsqueeze(1), w_k), (io["w_v"].unsqueeze(1), w_v),
                                      (io["key_table"].unsqueeze(1), key_table), (io["value_table"], value_table))])

        w_o, w_out = sb("w_o", [P, D]), parts("w_out", [P, D])
        b_q, b_k, b_v, b_o = sb("b_q", [P, 1]), sb("b_k", [P, 1]), sb("b_v", [P, P]), sb("b_o", [P, D])
        b_rows, head_mask, high_rows = sb("b_rows", [P, D]), sb("head_mask", [P, NH]), sb("high_rows", [P, 1])
        xn = [sb(f"xn{p}", [P, D]) for p in range(2)]
        xt = [parts(f"xt{p}", [P, P]) for p in range(2)]
        q_t = [parts(f"q_t{p}", [P, P]) for p in range(2)]
        k_t = [parts(f"k_t{p}", [P, KC]) for p in range(2)]
        value = [parts(f"value{p}", [KC, NH, HD + 1]) for p in range(2)]
        q_rows = [sb(f"q_rows{p}", [P, D]) for p in range(2)]
        q_parts = [sb(f"q_parts{p}", [P, 2, D], F16) for p in range(2)]
        q_head = [parts(f"q_head{p}", [P, P, NH]) for p in range(2)]
        q_pos = [sb(f"q_pos{p}", [QC * QB, QG, QC * NH], F16) for p in range(2)]
        prob_t = [parts(f"prob_t{p}", [KC, QG, P]) for p in range(2)]
        rel_all = [sb(f"rel_all{p}", [P, QG, QC * HD]) for p in range(2)]
        rel = [sb(f"rel{p}", [P, NH, HD]) for p in range(2)]
        mixed = [sb(f"mixed{p}", [P, NH, HD]) for p in range(2)]
        rden = [sb(f"rden{p}", [P, NH]) for p in range(2)]
        mixed_t = [parts(f"mixed_t{p}", [P, P]) for p in range(2)]
        top, shift = ([sb(f"{n}{k}", [P, 4]) for k in range(4)] for n in ("top", "shift"))
        prob = [sb(f"prob{k}", [P, 4, KC]) for k in range(4)]

        score_ps = [ps(f"score{k}") for k in range(2)]
        trans_ps = [ps(f"trans{k}") for k in range(2)]
        prep_ps, rel_ps, mix_ps, fin_ps = ps("prep"), ps("rel"), ps("mix"), ps("fin")
        Q_COLS, K_COLS, V_COLS, ROW_COLS = slice(0, P), slice(P, P + KC), slice(256, 256 + D), slice(384, 384 + D)

        q_written = [t.rearrange("(q r) -> q r", r=Q_STEP)[:, 0:QC * QB * NH]
                     .rearrange("q (b w) -> q b w", w=QC * NH)[:, :, 0:NH] for t in q_dram]
        q_read = [t.rearrange("(g r) -> g r", r=Q_PITCH)[:, 0:QC * QC * QB * NH]
                  .rearrange("g (b w) -> b g w", w=QC * NH) for t in q_dram]
        r_written = [t.rearrange("(g c) (h d) -> c h g d", c=QC, d=HD) for t in r_dram]

        weights_in, weights_ready, bias_ready = sem("weights_in"), sem("weights_ready"), sem("bias_ready")
        w_out_high, w_out_low, table_ready = sem("w_out_high"), sem("w_out_low"), sem("table_ready")
        cleared, q_zeroed = sem("cleared"), sem("q_zeroed")
        q_out, q_in, r_out, r_in = ([sem(f"{n}{p}") for p in range(2)] for n in ("q_out", "q_in", "r_out", "r_in"))
        xn_ready, xn_t = sem("xn_ready"), sem("xn_t")
        xt_high, xt_low = sem("xt_high"), sem("xt_low")
        proj_ready, proj_high, proj_low = sem("proj_ready"), sem("proj_high"), sem("proj_low")
        rows_ready, rows_high, rows_low, q_head_ready = (sem(n) for n in ("rows", "rows_high", "rows_low", "q_head"))
        q_tail_ready = sem("q_tail")
        score_ready, top_ready, shift_ready, exped = sem("score_ready"), sem("top_ready"), sem("shift_ready"), sem("exped")
        prob_ready, prob_high, prob_low = sem("prob_ready"), sem("prob_high"), sem("prob_low")
        rel_ready, rel_copied = sem("rel_ready"), sem("rel_copied")
        mix_ready, rden_ready, divided = sem("mix_ready"), sem("rden_ready"), sem("divided")
        rel_divided, mixed_ready = sem("rel_divided"), sem("mixed_ready")
        mixed_turned, mixed_high, mixed_low = sem("mixed_turned"), sem("mixed_high"), sem("mixed_low")
        y_ready, x_biased, x_ready = sem("y_ready"), sem("x_biased"), sem("x_ready")

        SCALE = float(HD) ** -0.5
        TAIL = 3 * P // 4
        FIRST, LO, HI, LAST = -4, 4, B - 4, B + 4
        WEIGHTS = [(w_o, "w_o"), (b_q, "b_q"), (b_k, "b_k"), (b_v, "b_v"), (b_o, "b_o"), (b_rows, "b_rows"),
                   (head_mask, "head_mask16"), (high_rows, "high_rows")]

        def products(a, b):
            return [(a[0], b[0]), (a[0], b[1]), (a[1], b[0])]

        with nc.Block(name="a1") as block:
            @block.sync
            def _(sp):
                for t, src in WEIGHTS:
                    sp.dma_start(t[:, :], io[src]).then_inc(weights_in, 16)
                sp.wait_ge(cleared, 1)
                for p in range(2):
                    sp.dma_start(q_read[p], q_pos[p][:, :, :]).then_inc(q_zeroed, 16)
                sp.wait_ge(q_zeroed, 32)

                def write_queries(n, p):
                    if inside(n, 0, B):
                        sp.wait_ge(rows_low, n + 1)
                        sp.dma_start(q_written[p], q_parts[p][:, :, :].rearrange("q a (d h) -> q (a d) h", d=HD)
                                     ).then_inc(q_out[p], 16)

                def write_relative(n, p):
                    if inside(n, 0, B):
                        sp.wait_ge(rel_copied, 4 * n + 4)
                        for c in range(QC):
                            sp.dma_start(r_written[p][c], rel_all[p][NH * c:NH * (c + 1), :, HD * c:HD * (c + 1)]
                                         ).then_inc(r_out[p], 16)

                def read_relative(n, p):
                    if inside(n, 0, B):
                        sp.wait_ge(r_out[p], (n - p) * QC * 8 + QC * 16)
                        sp.dma_start(rel[p][:, :, :].rearrange("q h d -> q (h d)"), r_dram[p]).then_inc(r_in[p], 16)

                def slot(n, p):
                    read_relative(n - 2, p)
                    write_queries(n + 2, p)
                    write_relative(n - 1, 1 - p)

                slots(sp, FIRST, LO, HI, LAST, slot)

            @block.tensor
            def _(pe):
                def prep_turn(n, p):
                    if inside(n, 0, B):
                        pe.wait_ge(xn_ready, n + 1)
                        wait(pe, proj_low, n)
                        nc.tensor.transpose(prep_ps[:, 0:P], xn[p][:, :], ident[:, :]).then_inc(xn_t, 1)

                def product(dst, a, b):
                    for k, (lhs, rhs) in enumerate(products(a, b)):
                        mm = nc.tensor.matmul(dst, lhs, rhs, start=(k == 0), stop=(k == 2))
                    return mm

                def project(n, p):
                    if inside(n, -2, B):
                        wait(pe, proj_low, n + 2)
                        if inside(n + 2, 0, B):
                            pe.wait_ge(xt_low, n + 3)
                        if inside(n + 1, 0, B):
                            last = product(prep_ps[:, K_COLS], [w[:, 0, :] for w in w_k], [t[:, n + 1, :] for t in ctx_t])
                        if inside(n, 0, B):
                            last = product(prep_ps[0:KC, V_COLS], [t[:, n, :] for t in ctx_t], [w[:, 0, :] for w in w_v])
                        if inside(n + 2, 0, B):
                            x_t = [t[:, :] for t in xt[p]]
                            product(prep_ps[:, Q_COLS], [w[:, 0, :] for w in w_q], x_t)
                            last = product(prep_ps[:, ROW_COLS], x_t, [w[:, 0, :] for w in w_rows])
                        last.then_inc(proj_ready, 1)

                def scores(n, p, u):
                    if inside(n, 0, B):
                        if u == 0:
                            pe.wait_ge(q_head_ready, 2 * n + 2)
                            pe.wait_ge(proj_low, n + 2)
                            pe.wait_ge(q_in[p], (n - p) * 8 + 16)
                        if u == 3:
                            pe.wait_ge(q_tail_ready, n + 1)
                        wait(pe, exped, 4 * n + u - 1)
                        for j in range(4):
                            g = 4 * u + j
                            dst, window = score_ps[u % 2][:, KC * j:KC * (j + 1)], slice(KT - KC - QC * g, KT - QC * g)
                            for k, (q, t) in enumerate(products(q_head[p], k_t[p])):
                                nc.tensor.matmul(dst, q[:, QC * g:QC * (g + 1), :], t[:, :], start=(k == 0), stop=False)
                            for k in range(2):
                                mm = nc.tensor.matmul(dst, q_pos[p][:, g, :], key_table[k][:, 0, window],
                                                      start=False, stop=(k == 1))
                        mm.then_inc(score_ready, 1)

                def turn(n, u):
                    if inside(n, 0, B):
                        pe.wait_ge(exped, 4 * n + u + 1)
                        wait(pe, prob_low, 4 * n + u - 1)
                        for j in range(4):
                            mm = nc.tensor.transpose(trans_ps[u % 2][0:KC, P * j:P * (j + 1)], prob[u][:, j, :],
                                                     ident[:, :])
                        mm.then_inc(prob_ready, 1)

                def relative(n, p, u):
                    if inside(n, 0, B):
                        pe.wait_ge(prob_low, 4 * n + u + 1)
                        wait(pe, rel_copied, 4 * n + u)
                        for j in range(4):
                            g = 4 * u + j
                            for k, (pr, t) in enumerate(products(prob_t[p], value_table)):
                                mm = nc.tensor.matmul(rel_ps[:, QC * HD * j:QC * HD * (j + 1)], pr[:, g, :],
                                                      t[:, QC * g:QC * (g + 1), :], start=(k == 0), stop=(k == 2))
                        mm.then_inc(rel_ready, 1)

                def mix(n, p, half):
                    if inside(n, 0, B):
                        if half == 0:
                            pe.wait_ge(prob_low, 4 * n + 4)
                            pe.wait_ge(proj_low, n + 3)
                            wait(pe, divided, n)
                        by_head = [t[:, :, :].rearrange("k g (c h) -> k (g c) h", h=NH) for t in prob_t[p]]
                        for h in range(8 * half, 8 * half + 8):
                            for k, (pr, v) in enumerate(products(by_head, value[p])):
                                mm = nc.tensor.matmul(mix_ps[:, (HD + 1) * h:(HD + 1) * (h + 1)], pr[:, :, h],
                                                      v[:, h, :], start=(k == 0), stop=(k == 2))
                        if half == 1:
                            mm.then_inc(mix_ready, 1)

                def fin_turn(n, p):
                    if inside(n, 0, B):
                        pe.wait_ge(mixed_ready, n + 1)
                        wait(pe, x_ready, n)
                        nc.tensor.transpose(fin_ps[:, 0:P], mixed[p][:, :, :].rearrange("q h d -> q (h d)"),
                                            ident[:, :]).then_inc(mixed_turned, 1)

                def fin_project(n, p):
                    if inside(n, 0, B):
                        pe.wait_ge(mixed_low, n + 1)
                        for k, (m, w) in enumerate(products(mixed_t[p], w_out)):
                            mm = nc.tensor.matmul(fin_ps[:, 0:D], m[:, :], w[:, :], start=(k == 0), stop=(k == 2))
                        mm.then_inc(y_ready, 1)

                def slot(n, p):
                    o = 1 - p
                    scores(n, p, 0)
                    turn(n - 1, 2)
                    project(n, p)
                    relative(n - 1, o, 0)
                    scores(n, p, 1)
                    turn(n - 1, 3)
                    relative(n - 1, o, 1)
                    fin_project(n - 4, p)
                    scores(n, p, 2)
                    turn(n, 0)
                    relative(n - 1, o, 2)
                    mix(n - 1, o, 0)
                    prep_turn(n + 3, o)
                    scores(n, p, 3)
                    turn(n, 1)
                    relative(n - 1, o, 3)
                    mix(n - 1, o, 1)
                    fin_turn(n - 3, o)

                pe.wait_ge(weights_ready, 2)
                nc.tensor.matmul(fin_ps[:, 0:D], b_v[:, :], w_o[:, :], start=True, stop=True).then_inc(bias_ready, 1)
                pe.wait_ge(weights_ready, 3)
                pe.wait_ge(w_out_low, 1)
                pe.wait_ge(table_ready, 1)
                slots(pe, FIRST, LO, HI, LAST, slot)

            @block.scalar
            def _(act):
                act.wait_ge(weights_in, 16 * len(WEIGHTS))
                act.wait_ge(weights_ready, 1)
                nc.scalar.activation(w_out[0][:, :], w_o[:, :], ACT.Copy).then_inc(w_out_high, 1)

                def read_queries(n, p):
                    if inside(n, 0, B):
                        act.wait_ge(q_out[p], (n - p) * 8 + 16)
                        wait(act, score_ready, 4 * n - 4)
                        act.dma_start(q_pos[p][:, :, :], q_read[p]).then_inc(q_in[p], 16)

                def copy_xn(n, p):
                    if inside(n, 0, B):
                        act.wait_ge(xn_t, n + 1)
                        wait(act, proj_ready, n - 1)
                        nc.scalar.activation(xt[p][0][:, :], prep_ps[:, 0:P], ACT.Copy).then_inc(xt_high, 1)

                def high_parts(n, p):
                    o = 1 - p
                    if inside(n, -2, B):
                        act.wait_ge(proj_ready, n + 3)
                        if inside(n + 1, 0, B):
                            wait(act, score_ready, 4 * n)
                            last = nc.scalar.activation(k_t[o][0][:, :], prep_ps[:, K_COLS], ACT.Identity,
                                                        bias=b_k[:, 0:1])
                        if inside(n, 0, B):
                            wait(act, mix_ready, n - 1)
                            last = nc.scalar.activation(value[p][0][:, :, 0:HD],
                                                        prep_ps[0:KC, V_COLS].rearrange("k (h d) -> k h d", d=HD),
                                                        ACT.Copy)
                        if inside(n + 2, 0, B):
                            wait(act, q_head_ready, 2 * n + 2)
                            wait(act, q_tail_ready, n + 1)
                            last = nc.scalar.activation(q_t[p][0][:, :], prep_ps[:, Q_COLS], ACT.Identity,
                                                        bias=b_q[:, 0:1])
                        last.then_inc(proj_high, 1)

                def high_rows_of(n, p):
                    if inside(n, 0, B):
                        act.wait_ge(rows_ready, n + 1)
                        wait(act, q_out[p], (n - p) * 8)
                        nc.scalar.activation(q_parts[p][:, 0, :], q_rows[p][:, :], ACT.Copy).then_inc(rows_high, 1)

                def exp(n, u):
                    if inside(n, 0, B):
                        act.wait_ge(shift_ready, 4 * n + u + 1)
                        wait(act, prob_ready, 4 * n + u - 3)
                        for j in range(4):
                            last = nc.scalar.activation(prob[u][:, j, :], score_ps[u % 2][:, KC * j:KC * (j + 1)], ACT.Exp,
                                                        bias=shift[u][:, j:j + 1], scale=SCALE)
                        last.then_inc(exped, 1)

                def high_prob(n, p, u):
                    if inside(n, 0, B):
                        act.wait_ge(prob_ready, 4 * n + u + 1)
                        wait(act, rel_ready, 4 * n + u - 7)
                        wait(act, mix_ready, n - 1)
                        nc.scalar.activation(prob_t[p][0][:, 4 * u:4 * u + 4, :],
                                             trans_ps[u % 2][0:KC, :].rearrange("k (g r) -> k g r", g=4),
                                             ACT.Copy).then_inc(prob_high, 1)

                def copy_relative(n, p, u):
                    if inside(n, 0, B):
                        act.wait_ge(rel_ready, 4 * n + u + 1)
                        if u == 0:
                            wait(act, r_out[p], (n - p) * QC * 8)
                            wait(act, r_in[p], (n - p) * 8)
                        if u == 3:
                            wait(act, mixed_ready, n - 1)
                        nc.scalar.activation(rel_all[p][:, 4 * u:4 * u + 4, :].rearrange("r g w -> r (g w)"),
                                             rel_ps[:, 0:4 * QC * HD], ACT.Copy).then_inc(rel_copied, 1)

                def high_mixed(n, p):
                    if inside(n, 0, B):
                        act.wait_ge(mixed_turned, n + 1)
                        wait(act, y_ready, n - 1)
                        nc.scalar.activation(mixed_t[p][0][:, :], fin_ps[:, 0:P], ACT.Copy).then_inc(mixed_high, 1)

                def slot(n, p):
                    o = 1 - p
                    high_prob(n - 1, o, 2)
                    high_parts(n, p)
                    copy_relative(n - 1, o, 0)
                    exp(n, 0)
                    high_prob(n - 1, o, 3)
                    read_queries(n + 1, o)
                    copy_relative(n - 1, o, 1)
                    exp(n, 1)
                    high_prob(n, p, 0)
                    high_rows_of(n + 2, p)
                    copy_relative(n - 1, o, 2)
                    exp(n, 2)
                    copy_xn(n + 3, o)
                    high_prob(n, p, 1)
                    copy_relative(n - 1, o, 3)
                    high_mixed(n - 3, o)
                    exp(n, 3)

                slots(act, FIRST, LO, HI, LAST, slot)

            @block.gpsimd
            def _(pool):
                for p in range(2):
                    for k in range(2):
                        nc.gpsimd.memset(value[p][k][:, :, HD:HD + 1], 1.0 - k)
                    last = nc.gpsimd.memset(q_pos[p][:, :, :], 0.0)
                last.then_inc(cleared, 1)
                pool.wait_ge(weights_ready, 3)

                def slot(n, p):
                    o = 1 - p
                    if inside(n + 1, 0, B):
                        pool.wait_ge(proj_low, n + 2)
                        wait(pool, score_ready, 4 * n)
                        for k, m in enumerate((P, TAIL)):
                            nc.gpsimd.tensor_tensor(q_head[o][k][:, 0:m, :],
                                                    q_t[o][k][:, 0:m].unsqueeze(2).broadcast_to([P, m, NH]),
                                                    head_mask[:, :].unsqueeze(1).broadcast_to([P, m, NH]),
                                                    ALU.mult).then_inc(q_head_ready, 1)
                    if inside(n, 0, B):
                        pool.wait_ge(xn_ready, n + 1)
                        nc.gpsimd.tensor_tensor(x_all[:, n, :], x_all[:, n, :], b_o[:, :], ALU.add).then_inc(x_biased, 1)

                slots(pool, -1, LO, HI, B, slot)

            @block.vector
            def _(dve):
                dve.wait_ge(weights_in, 16 * len(WEIGHTS))
                nc.vector.tensor_scalar(w_o[:, :], w_o[:, :], gates[:, 2:3], None, ALU.mult).then_inc(weights_ready, 1)
                nc.vector.tensor_scalar(b_o[:, :], b_o[:, :], gates[:, 2:3], None, ALU.mult).then_inc(weights_ready, 1)
                nc.vector.tensor_scalar(key_table[1][:, 0, :], key_table[1][:, 0, :], high_rows[:, 0:1], None,
                                        ALU.mult).then_inc(table_ready, 1)
                dve.wait_ge(weights_ready, 2)
                dve.wait_ge(w_out_high, 1)
                nc.vector.tensor_tensor(w_out[1][:, :], w_o[:, :], w_out[0][:, :], ALU.subtract).then_inc(w_out_low, 1)
                dve.wait_ge(bias_ready, 1)
                nc.vector.tensor_tensor(b_o[:, :], b_o[:, :], fin_ps[:, 0:D], ALU.add).then_inc(weights_ready, 1)

                def normalize(n, p):
                    if inside(n, 0, B):
                        wait(dve, xn_t, n - 1)
                        nc.vector.tensor_scalar(xn[p][:, :], x_all[:, n, :], mean[:, n, :], rstd[:, n, :],
                                                ALU.subtract, ALU.mult).then_inc(xn_ready, 1)

                def low_xn(n, p):
                    if inside(n, 0, B):
                        dve.wait_ge(xt_high, n + 1)
                        nc.vector.tensor_tensor(xt[p][1][:, :], prep_ps[:, 0:P], xt[p][0][:, :],
                                                ALU.subtract).then_inc(xt_low, 1)

                def low_parts(n, p):
                    o = 1 - p
                    if inside(n, -2, B):
                        dve.wait_ge(proj_high, n + 3)
                        if inside(n + 2, 0, B):
                            wait(dve, rows_high, n + 1)
                            nc.vector.tensor_tensor(q_rows[p][:, :], prep_ps[:, ROW_COLS], b_rows[:, :],
                                                    ALU.add).then_inc(rows_ready, 1)
                            last = nc.vector.scalar_tensor_tensor(
                                out=q_t[p][1][:, :], in0=prep_ps[:, Q_COLS], scalar=b_q[:, 0:1], in1=q_t[p][0][:, :],
                                op0=ALU.add, op1=ALU.subtract)
                        if inside(n + 1, 0, B):
                            last = nc.vector.scalar_tensor_tensor(
                                out=k_t[o][1][:, :], in0=prep_ps[:, K_COLS], scalar=b_k[:, 0:1], in1=k_t[o][0][:, :],
                                op0=ALU.add, op1=ALU.subtract)
                        if inside(n, 0, B):
                            last = nc.vector.tensor_tensor(value[p][1][:, :, 0:HD],
                                                           prep_ps[0:KC, V_COLS].rearrange("k (h d) -> k h d", d=HD),
                                                           value[p][0][:, :, 0:HD], ALU.subtract)
                        last.then_inc(proj_low, 1)

                def low_rows_of(n, p):
                    if inside(n, 0, B):
                        dve.wait_ge(rows_high, n + 1)
                        nc.vector.tensor_tensor(q_parts[p][:, 1, :], q_rows[p][:, :], q_parts[p][:, 0, :],
                                                ALU.subtract).then_inc(rows_low, 1)

                def query_tail(n, p):
                    if inside(n, 0, B):
                        dve.wait_ge(proj_low, n + 1)
                        wait(dve, score_ready, 4 * n - 4)
                        nc.vector.tensor_tensor(q_head[p][1][:, TAIL:P, :],
                                                q_t[p][1][:, TAIL:P].unsqueeze(2).broadcast_to([P, P - TAIL, NH]),
                                                head_mask[:, :].unsqueeze(1).broadcast_to([P, P - TAIL, NH]),
                                                ALU.mult).then_inc(q_tail_ready, 1)

                def row_max(n, u):
                    if inside(n, 0, B):
                        s = score_ps[u % 2][:, 0:4 * KC].rearrange("r (g k) -> r g k", g=4)
                        dve.wait_ge(score_ready, 4 * n + u + 1)
                        nc.vector.tensor_reduce(top[u][:, :], s, AX_X, ALU.max).then_inc(top_ready, 1)

                def negate_max(n, u):
                    if inside(n, 0, B):
                        dve.wait_ge(top_ready, 4 * n + u + 1)
                        wait(dve, exped, 4 * n + u - 3)
                        nc.vector.tensor_scalar(shift[u][:, :], top[u][:, :], -SCALE, None,
                                                ALU.mult).then_inc(shift_ready, 1)

                def low_prob(n, p, u):
                    if inside(n, 0, B):
                        dve.wait_ge(prob_high, 4 * n + u + 1)
                        own = [t[:, 4 * u:4 * u + 4, :].rearrange("k g r -> k (g r)") for t in prob_t[p]]
                        nc.vector.tensor_tensor(own[1], trans_ps[u % 2][0:KC, :], own[0],
                                                ALU.subtract).then_inc(prob_low, 1)

                def low_mixed(n, p):
                    if inside(n, 0, B):
                        dve.wait_ge(mixed_high, n + 1)
                        nc.vector.tensor_tensor(mixed_t[p][1][:, :], fin_ps[:, 0:P], mixed_t[p][0][:, :],
                                                ALU.subtract).then_inc(mixed_low, 1)

                def inverse_sum(n, p):
                    if inside(n, 0, B):
                        m = mix_ps[:, 0:NH * (HD + 1)].rearrange("q (h d) -> q h d", h=NH)
                        dve.wait_ge(mix_ready, n + 1)
                        nc.vector.reciprocal(rden[p][:, :], m[:, :, HD]).then_inc(rden_ready, 1)

                def divide(n, p):
                    if inside(n, 0, B):
                        m = mix_ps[:, 0:NH * (HD + 1)].rearrange("q (h d) -> q h d", h=NH)
                        dve.wait_ge(rden_ready, n + 1)
                        wait(dve, mixed_turned, n - 1)
                        nc.vector.tensor_tensor(mixed[p][:, :, :], m[:, :, 0:HD],
                                                rden[p][:, :].unsqueeze(2).broadcast_to([P, NH, HD]),
                                                ALU.mult).then_inc(divided, 1)

                def divide_relative(n, p):
                    if inside(n, 0, B):
                        dve.wait_ge(r_in[p], (n - p) * 8 + 16)
                        nc.vector.tensor_tensor(rel[p][:, :, :], rel[p][:, :, :],
                                                rden[p][:, :].unsqueeze(2).broadcast_to([P, NH, HD]),
                                                ALU.mult).then_inc(rel_divided, 1)

                def add_relative(n, p):
                    if inside(n, 0, B):
                        dve.wait_ge(rel_divided, n + 1)
                        dve.wait_ge(divided, n + 1)
                        nc.vector.tensor_tensor(mixed[p][:, :, :], mixed[p][:, :, :], rel[p][:, :, :],
                                                ALU.add).then_inc(mixed_ready, 1)

                def residual(n):
                    if inside(n, 0, B):
                        dve.wait_ge(y_ready, n + 1)
                        dve.wait_ge(x_biased, n + 1)
                        nc.vector.tensor_tensor(x_all[:, n, :], x_all[:, n, :], fin_ps[:, 0:D],
                                                ALU.add).then_inc(x_ready, 1)

                def statistics(n):
                    if inside(n, 0, B):
                        dve.wait_ge(x_ready, n + 1)
                        nc.vector.bn_stats(stats[:, n, :], x_all[:, n, :])

                def slot(n, p):
                    o = 1 - p
                    row_max(n, 0)
                    negate_max(n, 0)
                    low_mixed(n - 4, p)
                    low_prob(n - 1, o, 2)
                    row_max(n, 1)
                    inverse_sum(n - 2, p)
                    negate_max(n, 1)
                    low_prob(n - 1, o, 3)
                    divide(n - 2, p)
                    divide_relative(n - 3, o)
                    low_parts(n, p)
                    row_max(n, 2)
                    add_relative(n - 3, o)
                    negate_max(n, 2)
                    residual(n - 4)
                    low_prob(n, p, 0)
                    low_rows_of(n + 2, p)
                    row_max(n, 3)
                    low_xn(n + 3, o)
                    negate_max(n, 3)
                    query_tail(n + 1, o)
                    low_prob(n, p, 1)
                    normalize(n + 4, p)
                    statistics(n - 4)

                slots(dve, FIRST, LO, HI, LAST, slot)


def flamingo_kernel(nc, io, out):
    B = io["x"].shape[1]
    with ExitStack() as ctx:
        def sb(n, s):
            return ctx.enter_context(nc.sbuf_tensor(n, s, F32))

        x_all = sb("x_all", [P, B, D])
        stats, mean, rstd = sb("stats", [P, B, 6]), sb("mean", [P, B, 1]), sb("rstd", [P, B, 1])
        ident, gates = sb("ident", [P, P]), sb("gates", [P, 4])

        consts_in = ctx.enter_context(nc.semaphore("consts_in"))
        gates_ready = ctx.enter_context(nc.semaphore("gates_ready"))
        with nc.Block(name="consts") as block:
            @block.scalar
            def _(act):
                act.dma_start(ident[:, :], io["ident"]).then_inc(consts_in, 16)
                act.dma_start(gates[:, :], io["gates"]).then_inc(consts_in, 16)
                act.wait_ge(consts_in, 32)
                nc.scalar.activation(gates[:, :], gates[:, :], ACT.Tanh).then_inc(gates_ready, 1)

        load_x(nc, B, io["x"], x_all, stats)
        layernorm_constants(nc, "ln0", stats, mean[:, :, 0], rstd[:, :, 0], B)
        feature_attention(nc, B, io, x_all, stats, mean, rstd, ident, gates)
        layernorm_constants(nc, "ln1", stats, mean[:, :, 0], rstd[:, :, 0], B)
        x_high = ctx.enter_context(nc.sbuf_tensor("x_high", [P, B // GB, GT], F16))
        x_low = ctx.enter_context(nc.sbuf_tensor("x_low", [P, B // GB, GT], F16))
        logits, scores = sb("logits", [P, B // GB, GB * NE]), sb("scores", [P, B, NE, 1])
        with ExitStack() as layer:
            def parts(n, s):
                return [layer.enter_context(nc.sbuf_tensor(f"{n}_{k}", s, F16)) for k in ("high", "low")]

            actor = layer.enter_context(nc.sbuf_tensor("actor", [P, B // GB, GB * MAX_K], F32))
            w_gate, w_up = parts("w_gate", [P, 1, NE * I0]), parts("w_up", [P, 1, NE * I0])
            w_down = parts("w_down", [R0, NE * C0, D])
            router(nc, "r0", B, io, x_all, mean, rstd, ident, x_high, x_low, logits,
                   [(io["gate_w"], *w_gate), (io["up_w"], *w_up), (io["down_w"], *w_down)], actor)
            expert_scores(nc, "e0", B, io, logits, actor, scores, gates[:, 1:2])
            experts(nc, "f0", B, x_high, x_low, x_all, scores, [w_gate, w_up], w_down, R0, C0, 3, 3, stats=stats)
        layernorm_constants(nc, "ln2", stats, mean[:, :, 0], rstd[:, :, 0], B)
        q_dram = [nc.dram_tensor(f"queries{p}", [QG * Q_PITCH], F16).ap() for p in range(2)]
        r_dram = [nc.dram_tensor(f"relative_values{p}", [P, D], F32).ap() for p in range(2)]
        relative_attention(nc, B, io, x_all, stats, mean, rstd, ident, gates, q_dram, r_dram)
        layernorm_constants(nc, "ln3", stats, mean[:, :, 0], rstd[:, :, 0], B)
        with ExitStack() as layer:
            def parts(n, s):
                return [layer.enter_context(nc.sbuf_tensor(f"{n}_{k}", s, F16)) for k in ("high", "low")]

            w1, w2 = parts("w1", [P, 1, NE * I1]), parts("w2", [R1, NE * C1, D])
            router(nc, "r1", B, io, x_all, mean, rstd, ident, x_high, x_low, logits,
                   [(io["w1"], *w1), (io["w2"], *w2)])
            expert_scores(nc, "e1", B, io, logits, None, scores, gates[:, 3:4])
            experts(nc, "f1", B, x_high, x_low, x_all, scores, [w1], w2, R1, C1, 4, 4, out=out)


def _layout(np, a):
    B = a["x"].shape[0]
    row = np.arange(P)
    tile = np.tile
    d = {}
    d["x"] = a["x"].transpose(1, 0, 2)
    d["ident"] = np.eye(P, dtype=np.float32)
    d["gates"] = tile(np.stack([a["g_xattn"][0], a["g_ffn"][0], a["g_xattn"][1], a["g_ffn"][1]])[None, :], (P, 1))
    d["ctx"] = a["ctx_1024"].transpose(2, 0, 1)
    d["fm_w"] = tile(a["L0_xattn_fm_w"].T, (NH, 1))
    head = row[:, None] // HD == np.arange(NH)[None, :]
    d["fm_sign"] = np.stack([head, -1.0 * head], axis=2).reshape(P, 2 * NH).astype(np.float32)
    d["fm_b"] = tile(a["L0_xattn_fm_b"], NH)[:, None]
    d["row_sign"] = np.where(row % FD < HD, 1.0, -1.0).astype(np.float32)[:, None]
    d["head_mask"] = (row[:, None] // FD == np.arange(8)[None, :]).astype(np.float32)
    d["fc_w"] = a["L0_xattn_fc_w"].T.reshape(2, P, D).transpose(1, 0, 2)
    d["fc_b"] = tile(a["L0_xattn_fc_b"][None, :], (P, 1))
    d["r0_router"] = a["L0_ffn_router_w"].T
    d["actor_w1"] = a["L0_ffn_actor_w1"].T
    d["actor_b1"] = a["L0_ffn_actor_b1"][:, None]
    d["actor_w2"] = a["L0_ffn_actor_w2"].T
    d["actor_b2"] = tile(a["L0_ffn_actor_b2"][None, :], (P, 1))
    d["experts_after"] = tile(np.arange(NE - 1, -1, -1, dtype=np.float32)[None, :], (P, 1))
    d["first_k"] = tile(np.arange(-MAX_K, 0, dtype=np.float32)[None, :], (P, 1))
    d["gate_w"] = a["L0_ffn_gate_w"].reshape(NE * I0, 1, D).transpose(2, 1, 0)
    d["up_w"] = a["L0_ffn_up_w"].reshape(NE * I0, 1, D).transpose(2, 1, 0)
    d["down_w"] = a["L0_ffn_down_w"].transpose(0, 2, 1).reshape(NE * C0, R0, D).transpose(1, 0, 2)
    d["r1_router"] = a["L1_ffn_Wg"]
    d["w1"] = a["L1_ffn_W1"].transpose(1, 0, 2).reshape(D, 1, NE * I1)
    d["w2"] = a["L1_ffn_W2"].reshape(NE * C1, R1, D).transpose(1, 0, 2)
    for n in "qkvo":
        d[f"w_{n}"] = a[f"L1_xattn_W{n}"]
    d["b_q"], d["b_k"] = a["L1_xattn_bq"][:, None], a["L1_xattn_bk"][:, None]
    by_d = np.arange(D).reshape(NH, HD).T.reshape(D)
    d["w_rows"] = a["L1_xattn_Wq"][:, by_d]
    d["b_rows"] = tile(a["L1_xattn_bq"][by_d][None, :], (P, 1))
    d["high_rows"] = (row % QB < HD).astype(np.float32)[:, None]
    d["b_v"] = tile(a["L1_xattn_bv"][:, None], (1, P))
    d["b_o"] = tile(a["L1_xattn_bo"][None, :], (P, 1))
    d["head_mask16"] = head.astype(np.float32)
    zero = a["L1_xattn_rel_key_table"].shape[0] // 2
    q, k, c, j = np.arange(P), np.arange(KC), np.arange(QC), np.arange(KT)
    keys = a["L1_xattn_rel_key_table"][zero + P - QC + c[:, None] - j[None, :]]
    d["key_table"] = tile(keys.transpose(0, 2, 1)[:, None], (1, 2, 1, 1)).reshape(QC * QB, KT)
    d["value_table"] = a["L1_xattn_rel_value_table"][zero + q[None, :] - k[:, None]]
    return {k: np.ascontiguousarray(v) for k, v in d.items()}


def kernel(**inputs):
    import numpy as np
    import concourse.bacc as bacc
    from concourse.bass_utils import run_bass_kernel_spmd as run

    arrays = _layout(np, {k: np.asarray(v) for k, v in inputs.items()})
    nc = bacc.Bacc("TRN2", target_bir_lowering=False, num_devices=1)
    io = {k: nc.dram_tensor(f"in_{k}", v.shape, mybir.dt.from_np(v.dtype), kind="ExternalInput").ap()
          for k, v in arrays.items()}
    out = nc.dram_tensor("out_x", arrays["x"].shape, F32, kind="ExternalOutput").ap()
    flamingo_kernel(nc, io, out)
    r = run(nc, [{f"in_{k}": v for k, v in arrays.items()}], core_ids=[0])
    return np.ascontiguousarray(r.results[0]["out_x"].transpose(1, 0, 2))
```
